# Optimizing a Trainium2 kernel written in Bass

```python
import numpy as np
import jax
import jax.numpy as jnp

def _softmax(x, axis=-1):
    return jax.nn.softmax(x, axis=axis)

def _gelu(x):
    return jax.nn.gelu(x, approximate=True)

def _silu(x):
    return jax.nn.silu(x)

def _sigmoid(x):
    return jax.nn.sigmoid(x)

def _layernorm(x, axis=-1, eps=1e-05):
    m = jnp.mean(x, axis=axis, keepdims=True)
    v = jnp.var(x, axis=axis, keepdims=True)
    return (x - m) / jnp.sqrt(v + eps)

def _scatter_add(tgt, idx, src, axis=0):
    return tgt.at[idx].add(src)

def _segment_sum(src, seg, n):
    return jax.ops.segment_sum(src, seg, n)
kernel_name = 'mk_seq_preln_d1_jaxref_r8_4fe468'

def setup_inputs(seed: int=0):
    np.random.seed(seed)
    _w = jnp.asarray

    def _L0_attn_setup():
        import jax, jax.numpy as jnp
        import numpy as np
        D_MODEL = 128
        D_STATE = 16
        D_CONV = 4
        EXPAND = 2
        D_INNER = EXPAND * D_MODEL
        DT_RANK = D_MODEL // 16
        BATCH = 4
        SEQLEN = 256

        def _mamba_params(key):
            ks = jax.random.split(key, 6)
            s = 0.02
            return dict(W_in=jax.random.normal(ks[0], (2 * D_INNER, D_MODEL)) * s, W_conv=jax.random.normal(ks[1], (D_INNER, D_CONV)) * s, b_conv=jnp.zeros((D_INNER,), jnp.float32), W_x=jax.random.normal(ks[2], (DT_RANK + 2 * D_STATE, D_INNER)) * s, W_dt=jax.random.normal(ks[3], (D_INNER, DT_RANK)) * s, b_dt=jax.random.normal(ks[4], (D_INNER,)) * 0.1, A_log=jnp.log(jnp.tile(jnp.arange(1, D_STATE + 1, dtype=jnp.float32), (D_INNER, 1))), D=jnp.ones((D_INNER,), jnp.float32), W_out=jax.random.normal(ks[5], (D_MODEL, D_INNER)) * s)

        def _layernorm(x, w, b, eps=1e-05):
            mu = jnp.mean(x, axis=-1, keepdims=True)
            var = jnp.mean(jnp.square(x - mu), axis=-1, keepdims=True)
            return (x - mu) * jax.lax.rsqrt(var + eps) * w + b

        def _mamba(x, W_in, W_conv, b_conv, W_x, W_dt, b_dt, A_log, Dp, W_out):
            Bb = x.shape[0]
            xz = x @ W_in.T
            xp, z = jnp.split(xz, 2, axis=-1)
            xc = jax.lax.conv_general_dilated(xp.transpose(0, 2, 1), W_conv[:, None, :], window_strides=(1,), padding=[(D_CONV - 1, 0)], dimension_numbers=('NCH', 'OIH', 'NCH'), feature_group_count=D_INNER)
            xc = jax.nn.silu(xc.transpose(0, 2, 1) + b_conv)
            x_dbl = xc @ W_x.T
            dt, Bm, Cm = jnp.split(x_dbl, [DT_RANK, DT_RANK + D_STATE], axis=-1)
            dt = jax.nn.softplus(dt @ W_dt.T + b_dt)
            A = -jnp.exp(A_log)

            def step(h, inp):
                dt_t, u_t, B_t, C_t = inp
                h = h * jnp.exp(dt_t[:, :, None] * A) + (dt_t * u_t)[:, :, None] * B_t[:, None, :]
                y = jnp.einsum('bdn,bn->bd', h, C_t)
                return (h, y)
            xs = (dt.transpose(1, 0, 2), xc.transpose(1, 0, 2), Bm.transpose(1, 0, 2), Cm.transpose(1, 0, 2))
            h0 = jnp.zeros((Bb, D_INNER, D_STATE), x.dtype)
            _, ys = jax.lax.scan(step, h0, xs)
            y = ys.transpose(1, 0, 2) + xc * Dp
            y = y * jax.nn.silu(z)
            return y @ W_out.T
        key = jax.random.key(seed)
        kx, kf, kb = jax.random.split(key, 3)
        inp = {'x': jax.random.normal(kx, (BATCH, SEQLEN, D_MODEL), jnp.float32), 'ln_w': jnp.ones((D_MODEL,), jnp.float32), 'ln_b': jnp.zeros((D_MODEL,), jnp.float32)}
        for pref, k in (('f_', kf), ('b_', kb)):
            p = _mamba_params(k)
            for name, v in p.items():
                inp[pref + name] = v
        return inp
    _L0_attn_in = _L0_attn_setup()

    def _L0_ffn_setup():
        import jax, jax.numpy as jnp
        import numpy as np
        DIM = 128
        DEPTH = 6
        HEADS = 16
        DIM_HEAD = 64
        WINDOW = 32
        INNER = HEADS * DIM_HEAD
        DIM_INNER = int(DIM * 4 * 2 / 3)
        QK_SCALE = 8.0

        def shift_tokens(t):
            a, s = jnp.split(t, 2, -1)
            s = jnp.pad(s, ((0, 0), (1, 0), (0, 0)))[:, :-1]
            return jnp.concatenate([a, s], -1)

        def l2norm(t):
            return t / jnp.maximum(jnp.linalg.norm(t, axis=-1, keepdims=True), 1e-12)

        def rotate_half(x):
            x1, x2 = jnp.split(x, 2, -1)
            return jnp.concatenate([-x2, x1], -1)

        def rotary_tables(n):
            half = jnp.arange(0, DIM_HEAD, 2, dtype=jnp.float32)
            inv_freq = 1.0 / 10000.0 ** (half / DIM_HEAD)
            t = jnp.arange(n, dtype=jnp.float32)
            freqs = t[:, None] * inv_freq[None, :]
            freqs = jnp.concatenate([freqs, freqs], -1)
            base_scale = (half + 0.4 * DIM_HEAD) / (1.4 * DIM_HEAD)
            power = (t - n // 2) / (WINDOW // 2)
            scale = base_scale[None, :] ** power[:, None]
            scale = jnp.concatenate([scale, scale], -1)
            return (freqs, scale)

        def local_attention(q, k, v):
            b, h, n, d = q.shape
            w = WINDOW
            nw = n // w
            bq = q.reshape(b, h, nw, w, d)
            bk = k.reshape(b, h, nw, w, d)
            bv = v.reshape(b, h, nw, w, d)

            def look(t):
                p = jnp.pad(t, ((0, 0), (0, 0), (1, 0), (0, 0), (0, 0)))
                return jnp.concatenate([p[:, :, :nw], p[:, :, 1:]], axis=3)
            bk2, bv2 = (look(bk), look(bv))
            seq = jnp.arange(n).reshape(nw, w)
            seq_p = jnp.pad(seq, ((1, 0), (0, 0)), constant_values=-1)
            jt = jnp.concatenate([seq_p[:nw], seq_p[1:]], axis=1)
            it = seq[:, :, None]
            jb = jt[:, None, :]
            mask = (it < jb) | (it > jb + w) | (jb == -1)
            sim = jnp.einsum('bhwie,bhwje->bhwij', bq, bk2) * QK_SCALE
            sim = jnp.where(mask, -jnp.finfo(sim.dtype).max, sim)
            attn = jax.nn.softmax(sim, -1)
            out = jnp.einsum('bhwij,bhwje->bhwie', attn, bv2)
            return out.reshape(b, h, n, d)

        def attn_layer(x, Wqkv, qs, ksc, Wo):
            b, n, _ = x.shape
            qkv = x @ Wqkv
            q, k, v = jnp.split(qkv, 3, -1)
            sh = lambda t: t.reshape(b, n, HEADS, DIM_HEAD).transpose(0, 2, 1, 3)
            q, k, v = (sh(q), sh(k), sh(v))
            q = l2norm(q) * qs
            k = l2norm(k) * ksc
            freqs, scale = rotary_tables(n)
            cos, sin = (jnp.cos(freqs), jnp.sin(freqs))
            q = q * cos * scale + rotate_half(q) * sin * scale
            inv = 1.0 / scale
            k = k * cos * inv + rotate_half(k) * sin * inv
            out = local_attention(q, k, v)
            out = out.transpose(0, 2, 1, 3).reshape(b, n, INNER)
            return out @ Wo

        def ffn_layer(x, g, bln, W1, b1, W2, b2):
            mu = x.mean(-1, keepdims=True)
            var = ((x - mu) ** 2).mean(-1, keepdims=True)
            xn = (x - mu) / jnp.sqrt(var + 1e-05) * g + bln
            hg = xn @ W1 + b1
            a, gate = jnp.split(hg, 2, -1)
            return a * jax.nn.gelu(gate, approximate=False) @ W2 + b2
        key = jax.random.key(seed)
        ks = jax.random.split(key, 8)
        B, N = (2, 256)
        init = lambda k, shape: jax.random.normal(k, shape, jnp.float32) * 0.02
        return {'x': jax.random.normal(ks[0], (B, N, DIM), jnp.float32), 'Wqkv': init(ks[1], (DEPTH, DIM, 3 * INNER)), 'q_scale': jnp.ones((DEPTH, DIM_HEAD), jnp.float32), 'k_scale': jnp.ones((DEPTH, DIM_HEAD), jnp.float32), 'Wo': init(ks[2], (DEPTH, INNER, DIM)), 'ln_g': jnp.ones((DEPTH, DIM), jnp.float32), 'ln_b': jnp.zeros((DEPTH, DIM), jnp.float32), 'W1': init(ks[3], (DEPTH, DIM, 2 * DIM_INNER)), 'b1': jnp.zeros((DEPTH, 2 * DIM_INNER), jnp.float32), 'W2': init(ks[4], (DEPTH, DIM_INNER, DIM)), 'b2': jnp.zeros((DEPTH, DIM), jnp.float32)}
    _L0_ffn_in = _L0_ffn_setup()
    _d = {'L0_attn_x': _L0_attn_in['x'], 'L0_attn_ln_w': _L0_attn_in['ln_w'], 'L0_attn_ln_b': _L0_attn_in['ln_b'], 'L0_attn_f_W_in': _L0_attn_in['f_W_in'], 'L0_attn_f_W_conv': _L0_attn_in['f_W_conv'], 'L0_attn_f_b_conv': _L0_attn_in['f_b_conv'], 'L0_attn_f_W_x': _L0_attn_in['f_W_x'], 'L0_attn_f_W_dt': _L0_attn_in['f_W_dt'], 'L0_attn_f_b_dt': _L0_attn_in['f_b_dt'], 'L0_attn_f_A_log': _L0_attn_in['f_A_log'], 'L0_attn_f_D': _L0_attn_in['f_D'], 'L0_attn_f_W_out': _L0_attn_in['f_W_out'], 'L0_attn_b_W_in': _L0_attn_in['b_W_in'], 'L0_attn_b_W_conv': _L0_attn_in['b_W_conv'], 'L0_attn_b_b_conv': _L0_attn_in['b_b_conv'], 'L0_attn_b_W_x': _L0_attn_in['b_W_x'], 'L0_attn_b_W_dt': _L0_attn_in['b_W_dt'], 'L0_attn_b_b_dt': _L0_attn_in['b_b_dt'], 'L0_attn_b_A_log': _L0_attn_in['b_A_log'], 'L0_attn_b_D': _L0_attn_in['b_D'], 'L0_attn_b_W_out': _L0_attn_in['b_W_out'], 'L0_ffn_Wqkv': _L0_ffn_in['Wqkv'], 'L0_ffn_q_scale': _L0_ffn_in['q_scale'], 'L0_ffn_k_scale': _L0_ffn_in['k_scale'], 'L0_ffn_Wo': _L0_ffn_in['Wo'], 'L0_ffn_ln_g': _L0_ffn_in['ln_g'], 'L0_ffn_ln_b': _L0_ffn_in['ln_b'], 'L0_ffn_W1': _L0_ffn_in['W1'], 'L0_ffn_b1': _L0_ffn_in['b1'], 'L0_ffn_W2': _L0_ffn_in['W2'], 'L0_ffn_b2': _L0_ffn_in['b2']}
    _x0 = _d['L0_attn_x']
    _d['L0_attn_x'] = jax.random.normal(jax.random.fold_in(jax.random.key(seed), 1), (4, 1024, 128), dtype=_x0.dtype)
    del _x0
    return _d

def reference(L0_attn_x, L0_attn_ln_w, L0_attn_ln_b, L0_attn_f_W_in, L0_attn_f_W_conv, L0_attn_f_b_conv, L0_attn_f_W_x, L0_attn_f_W_dt, L0_attn_f_b_dt, L0_attn_f_A_log, L0_attn_f_D, L0_attn_f_W_out, L0_attn_b_W_in, L0_attn_b_W_conv, L0_attn_b_b_conv, L0_attn_b_W_x, L0_attn_b_W_dt, L0_attn_b_b_dt, L0_attn_b_A_log, L0_attn_b_D, L0_attn_b_W_out, L0_ffn_Wqkv, L0_ffn_q_scale, L0_ffn_k_scale, L0_ffn_Wo, L0_ffn_ln_g, L0_ffn_ln_b, L0_ffn_W1, L0_ffn_b1, L0_ffn_W2, L0_ffn_b2):

    def _L0_attn_ref(x, ln_w, ln_b, f_W_in, f_W_conv, f_b_conv, f_W_x, f_W_dt, f_b_dt, f_A_log, f_D, f_W_out, b_W_in, b_W_conv, b_b_conv, b_W_x, b_W_dt, b_b_dt, b_A_log, b_D, b_W_out):
        import jax, jax.numpy as jnp
        import numpy as np
        D_MODEL = 128
        D_STATE = 16
        D_CONV = 4
        EXPAND = 2
        D_INNER = EXPAND * D_MODEL
        DT_RANK = D_MODEL // 16
        BATCH = 4
        SEQLEN = 256

        def _mamba_params(key):
            ks = jax.random.split(key, 6)
            s = 0.02
            return dict(W_in=jax.random.normal(ks[0], (2 * D_INNER, D_MODEL)) * s, W_conv=jax.random.normal(ks[1], (D_INNER, D_CONV)) * s, b_conv=jnp.zeros((D_INNER,), jnp.float32), W_x=jax.random.normal(ks[2], (DT_RANK + 2 * D_STATE, D_INNER)) * s, W_dt=jax.random.normal(ks[3], (D_INNER, DT_RANK)) * s, b_dt=jax.random.normal(ks[4], (D_INNER,)) * 0.1, A_log=jnp.log(jnp.tile(jnp.arange(1, D_STATE + 1, dtype=jnp.float32), (D_INNER, 1))), D=jnp.ones((D_INNER,), jnp.float32), W_out=jax.random.normal(ks[5], (D_MODEL, D_INNER)) * s)

        def _layernorm(x, w, b, eps=1e-05):
            mu = jnp.mean(x, axis=-1, keepdims=True)
            var = jnp.mean(jnp.square(x - mu), axis=-1, keepdims=True)
            return (x - mu) * jax.lax.rsqrt(var + eps) * w + b

        def _mamba(x, W_in, W_conv, b_conv, W_x, W_dt, b_dt, A_log, Dp, W_out):
            Bb = x.shape[0]
            xz = x @ W_in.T
            xp, z = jnp.split(xz, 2, axis=-1)
            xc = jax.lax.conv_general_dilated(xp.transpose(0, 2, 1), W_conv[:, None, :], window_strides=(1,), padding=[(D_CONV - 1, 0)], dimension_numbers=('NCH', 'OIH', 'NCH'), feature_group_count=D_INNER)
            xc = jax.nn.silu(xc.transpose(0, 2, 1) + b_conv)
            x_dbl = xc @ W_x.T
            dt, Bm, Cm = jnp.split(x_dbl, [DT_RANK, DT_RANK + D_STATE], axis=-1)
            dt = jax.nn.softplus(dt @ W_dt.T + b_dt)
            A = -jnp.exp(A_log)

            def step(h, inp):
                dt_t, u_t, B_t, C_t = inp
                h = h * jnp.exp(dt_t[:, :, None] * A) + (dt_t * u_t)[:, :, None] * B_t[:, None, :]
                y = jnp.einsum('bdn,bn->bd', h, C_t)
                return (h, y)
            xs = (dt.transpose(1, 0, 2), xc.transpose(1, 0, 2), Bm.transpose(1, 0, 2), Cm.transpose(1, 0, 2))
            h0 = jnp.zeros((Bb, D_INNER, D_STATE), x.dtype)
            _, ys = jax.lax.scan(step, h0, xs)
            y = ys.transpose(1, 0, 2) + xc * Dp
            y = y * jax.nn.silu(z)
            return y @ W_out.T
        xn = _layernorm(x, ln_w, ln_b)
        y_fwd = _mamba(xn, f_W_in, f_W_conv, f_b_conv, f_W_x, f_W_dt, f_b_dt, f_A_log, f_D, f_W_out)
        xr = jnp.flip(xn, axis=1)
        y_bwd = jnp.flip(_mamba(xr, b_W_in, b_W_conv, b_b_conv, b_W_x, b_W_dt, b_b_dt, b_A_log, b_D, b_W_out), axis=1)
        return x + 0.5 * (y_fwd + y_bwd)

    def _L0_ffn_ref(x, Wqkv, q_scale, k_scale, Wo, ln_g, ln_b, W1, b1, W2, b2):
        import jax, jax.numpy as jnp
        import numpy as np
        DIM = 128
        DEPTH = 6
        HEADS = 16
        DIM_HEAD = 64
        WINDOW = 32
        INNER = HEADS * DIM_HEAD
        DIM_INNER = int(DIM * 4 * 2 / 3)
        QK_SCALE = 8.0

        def shift_tokens(t):
            a, s = jnp.split(t, 2, -1)
            s = jnp.pad(s, ((0, 0), (1, 0), (0, 0)))[:, :-1]
            return jnp.concatenate([a, s], -1)

        def l2norm(t):
            return t / jnp.maximum(jnp.linalg.norm(t, axis=-1, keepdims=True), 1e-12)

        def rotate_half(x):
            x1, x2 = jnp.split(x, 2, -1)
            return jnp.concatenate([-x2, x1], -1)

        def rotary_tables(n):
            half = jnp.arange(0, DIM_HEAD, 2, dtype=jnp.float32)
            inv_freq = 1.0 / 10000.0 ** (half / DIM_HEAD)
            t = jnp.arange(n, dtype=jnp.float32)
            freqs = t[:, None] * inv_freq[None, :]
            freqs = jnp.concatenate([freqs, freqs], -1)
            base_scale = (half + 0.4 * DIM_HEAD) / (1.4 * DIM_HEAD)
            power = (t - n // 2) / (WINDOW // 2)
            scale = base_scale[None, :] ** power[:, None]
            scale = jnp.concatenate([scale, scale], -1)
            return (freqs, scale)

        def local_attention(q, k, v):
            b, h, n, d = q.shape
            w = WINDOW
            nw = n // w
            bq = q.reshape(b, h, nw, w, d)
            bk = k.reshape(b, h, nw, w, d)
            bv = v.reshape(b, h, nw, w, d)

            def look(t):
                p = jnp.pad(t, ((0, 0), (0, 0), (1, 0), (0, 0), (0, 0)))
                return jnp.concatenate([p[:, :, :nw], p[:, :, 1:]], axis=3)
            bk2, bv2 = (look(bk), look(bv))
            seq = jnp.arange(n).reshape(nw, w)
            seq_p = jnp.pad(seq, ((1, 0), (0, 0)), constant_values=-1)
            jt = jnp.concatenate([seq_p[:nw], seq_p[1:]], axis=1)
            it = seq[:, :, None]
            jb = jt[:, None, :]
            mask = (it < jb) | (it > jb + w) | (jb == -1)
            sim = jnp.einsum('bhwie,bhwje->bhwij', bq, bk2) * QK_SCALE
            sim = jnp.where(mask, -jnp.finfo(sim.dtype).max, sim)
            attn = jax.nn.softmax(sim, -1)
            out = jnp.einsum('bhwij,bhwje->bhwie', attn, bv2)
            return out.reshape(b, h, n, d)

        def attn_layer(x, Wqkv, qs, ksc, Wo):
            b, n, _ = x.shape
            qkv = x @ Wqkv
            q, k, v = jnp.split(qkv, 3, -1)
            sh = lambda t: t.reshape(b, n, HEADS, DIM_HEAD).transpose(0, 2, 1, 3)
            q, k, v = (sh(q), sh(k), sh(v))
            q = l2norm(q) * qs
            k = l2norm(k) * ksc
            freqs, scale = rotary_tables(n)
            cos, sin = (jnp.cos(freqs), jnp.sin(freqs))
            q = q * cos * scale + rotate_half(q) * sin * scale
            inv = 1.0 / scale
            k = k * cos * inv + rotate_half(k) * sin * inv
            out = local_attention(q, k, v)
            out = out.transpose(0, 2, 1, 3).reshape(b, n, INNER)
            return out @ Wo

        def ffn_layer(x, g, bln, W1, b1, W2, b2):
            mu = x.mean(-1, keepdims=True)
            var = ((x - mu) ** 2).mean(-1, keepdims=True)
            xn = (x - mu) / jnp.sqrt(var + 1e-05) * g + bln
            hg = xn @ W1 + b1
            a, gate = jnp.split(hg, 2, -1)
            return a * jax.nn.gelu(gate, approximate=False) @ W2 + b2
        for i in range(DEPTH):
            x = attn_layer(shift_tokens(x), Wqkv[i], q_scale[i], k_scale[i], Wo[i]) + x
            x = ffn_layer(shift_tokens(x), ln_g[i], ln_b[i], W1[i], b1[i], W2[i], b2[i]) + x
        return x
    x = L0_attn_x
    x = x + _L0_attn_ref(_layernorm(x, axis=-1), L0_attn_ln_w, L0_attn_ln_b, L0_attn_f_W_in, L0_attn_f_W_conv, L0_attn_f_b_conv, L0_attn_f_W_x, L0_attn_f_W_dt, L0_attn_f_b_dt, L0_attn_f_A_log, L0_attn_f_D, L0_attn_f_W_out, L0_attn_b_W_in, L0_attn_b_W_conv, L0_attn_b_b_conv, L0_attn_b_W_x, L0_attn_b_W_dt, L0_attn_b_b_dt, L0_attn_b_A_log, L0_attn_b_D, L0_attn_b_W_out)
    x = x + _L0_ffn_ref(_layernorm(x, axis=-1), L0_ffn_Wqkv, L0_ffn_q_scale, L0_ffn_k_scale, L0_ffn_Wo, L0_ffn_ln_g, L0_ffn_ln_b, L0_ffn_W1, L0_ffn_b1, L0_ffn_W2, L0_ffn_b2)
    return x

_drawn_inputs = setup_inputs


def setup_inputs(seed=0):
    import zlib

    import numpy as np

    out = dict(_drawn_inputs(seed))
    spreads = {'L0_attn_ln_w': (1.0, 0.6),
     'L0_attn_ln_b': (0.0, 0.8),
     'L0_attn_f_b_conv': (0.0, 0.8),
     'L0_attn_f_D': (1.0, 0.6),
     'L0_attn_b_b_conv': (0.0, 0.8),
     'L0_attn_b_D': (1.0, 0.6),
     'L0_ffn_q_scale': (1.0, 0.6),
     'L0_ffn_k_scale': (1.0, 0.6),
     'L0_ffn_ln_g': (1.0, 0.6),
     'L0_ffn_ln_b': (0.0, 0.8),
     'L0_ffn_b1': (0.0, 0.8),
     'L0_ffn_b2': (0.0, 0.8)}
    factors = {'L0_attn_f_W_in': 8.0,
     'L0_attn_f_W_conv': 8.0,
     'L0_attn_f_W_x': 8.0,
     'L0_attn_f_W_dt': 8.0,
     'L0_attn_f_b_dt': 8.0,
     'L0_attn_f_A_log': 8.0,
     'L0_attn_f_W_out': 8.0,
     'L0_attn_b_W_in': 8.0,
     'L0_attn_b_W_conv': 8.0,
     'L0_attn_b_W_x': 8.0,
     'L0_attn_b_W_dt': 8.0,
     'L0_attn_b_b_dt': 8.0,
     'L0_attn_b_A_log': 8.0,
     'L0_attn_b_W_out': 8.0,
     'L0_ffn_W1': 5.433,
     'L0_ffn_W2': 5.335}
    for name, (base, spread) in spreads.items():
        noise = np.random.default_rng([zlib.crc32(name.encode()), seed]).standard_normal(out[name].shape)
        drawn = base * np.exp(spread * noise) if base else spread * noise
        out[name] = jnp.asarray(drawn.astype(out[name].dtype))
    for name, factor in factors.items():
        out[name] = (out[name] * factor).astype(out[name].dtype)
    return out
```

```python
from contextlib import ExitStack

import numpy as np

import concourse.bass as bass
from concourse import mybir

F32 = mybir.dt.float32
BF16 = mybir.dt.bfloat16
ALU = mybir.AluOpType
ACT = mybir.ActivationFunctionType
AX_X = mybir.AxisListType.X

P = 128
BANK = 512
BATCH, SEQ, DIM = 4, 1024, 128
TOKENS = BATCH * SEQ
HALF_BANKS = SEQ // BANK
D_INNER, D_STATE, D_CONV, DT_RANK = 256, 16, 4, 8
HALVES = D_INNER // P
EPS = 1e-5

CONV_W, CONV_B, DT_B, A_LOG, D_SKIP = 0, 8, 10, 12, 44
PACKED = 46


class Steps:

    def __init__(self, sem, base=0):
        self.sem, self.base, self.count = sem, base, 0

    def mark(self, instruction):
        instruction.then_inc(self.sem, 1)
        self.count += 1

    def wait(self, eng):
        eng.wait_ge(self.sem, self.base + self.count)


def layer_norm_block(nc, ctx, sem, ones_mean, eps_col, src, out, work, finish, name):
    chunks = TOKENS // BANK
    mean_ready = sem(name + "_mean_ready")
    centred = sem(name + "_centred")
    squared = sem(name + "_squared")
    var_ready = sem(name + "_var_ready")
    log_done = sem(name + "_log_done")
    rstd_ready = sem(name + "_rstd_ready")
    dve_done = sem(name + "_dve_done")
    stats = ctx.enter_context(nc.psum_tensor(name + "_stats", [P, chunks, BANK], F32))
    with nc.Block() as block:
        @block.tensor
        def _(pe):
            for c in range(chunks):
                pe.matmul(stats[:, c, :], ones_mean[:, :], src[:, c * BANK:(c + 1) * BANK],
                          start=True, stop=True).then_inc(mean_ready, 1)
            for c in range(chunks):
                pe.wait_ge(squared, c + 1)
                pe.matmul(stats[:, c, :], ones_mean[:, :], work[:, c * BANK:(c + 1) * BANK],
                          start=True, stop=True).then_inc(var_ready, 1)

        @block.vector
        def _(dve):
            for c in range(chunks):
                cols = slice(c * BANK, (c + 1) * BANK)
                dve.wait_ge(mean_ready, c + 1)
                dve.tensor_tensor(out[:, cols], src[:, cols], stats[:, c, :],
                                  ALU.subtract).then_inc(centred, 1)
            for c in range(chunks):
                cols = slice(c * BANK, (c + 1) * BANK)
                steps = Steps(dve_done, c * finish[0])
                dve.wait_ge(rstd_ready, c + 1)
                steps.mark(dve.tensor_tensor(out[:, cols], out[:, cols], work[:, cols], ALU.mult))
                finish[1](dve, cols, steps)

        @block.scalar
        def _(act):
            for c in range(chunks):
                cols = slice(c * BANK, (c + 1) * BANK)
                act.wait_ge(centred, c + 1)
                act.activation(work[:, cols], out[:, cols], ACT.Square).then_inc(squared, 1)
            for c in range(chunks):
                cols = slice(c * BANK, (c + 1) * BANK)
                act.wait_ge(var_ready, c + 1)
                act.activation(work[:, cols], stats[:, c, :], ACT.Ln, bias=eps_col[:, 0:1]).then_inc(log_done, 1)
                act.wait_ge(log_done, c + 1)
                act.activation(work[:, cols], work[:, cols], ACT.Exp, scale=-0.5).then_inc(rstd_ready, 1)


def mamba(nc, xn, resid, weights):
    win, wx, wdt, wout, packed, ident, sel_b, sel_c = weights
    with ExitStack() as ctx:
        def sb(name, shape, dt=F32):
            return ctx.enter_context(nc.sbuf_tensor(name, shape, dt))

        def sem(name):
            return ctx.enter_context(nc.semaphore(name))

        UNITS = D_STATE * HALVES
        PAD = D_CONV - 1
        neg_a = sb("neg_a", [P, 2, HALVES * D_STATE])
        xp = sb("xp", [P, HALVES, PAD + SEQ])
        xc = sb("xc", [P, HALVES, SEQ])
        zs = sb("zs", [P, HALVES, SEQ])
        dt = sb("dt", [P, HALVES, SEQ])
        dtx = sb("dtx", [P, HALVES, SEQ])
        expd = sb("expd", [P, SEQ])
        relu = sb("relu", [P, SEQ])
        dt_raw = sb("dt_raw", [DT_RANK, SEQ])
        bc = sb("bc", [96, SEQ], BF16)
        bc_rest = sb("bc_rest", [96, SEQ])
        bc_mid = sb("bc_mid", [96, SEQ], BF16)
        decay = sb("decay", [P, HALVES, 2, SEQ])
        drive = sb("drive", [P, 2, SEQ])
        state = sb("state", [P, 3, SEQ])
        c_row = sb("c_row", [P, 2, SEQ])
        read = sb("read", [P, 2, SEQ])
        gated = sb("gated", [P, HALVES, SEQ])
        ps = ctx.enter_context(nc.psum_tensor("mamba_ps", [P, 8, BANK], F32))
        b_ps, c_ps = ps[:, 0:2, :], ps[:, 2:4, :]

        a_exp = sem("a_exp"); a_ready = sem("a_ready"); pad_ready = sem("pad_ready")
        xz_ready = sem("xz_ready"); xp_ready = sem("xp_ready"); zs_ready = sem("zs_ready")
        conv_ready = sem("conv_ready"); conv_step = sem("conv_step"); xc_ready = sem("xc_ready")
        xdbl_ready = sem("xdbl_ready"); dt_raw_ready = sem("dt_raw_ready"); bc_high = sem("bc_high")
        split_step = sem("split_step"); bc_ready = sem("bc_ready"); v_ready = sem("v_ready")
        soft_step = sem("soft_step"); soft_ready = sem("soft_ready"); relu_ready = sem("relu_ready")
        dt_done = sem("dt_done"); dt_ready = sem("dt_ready")
        b_ready = sem("b_ready"); c_ready = sem("c_ready"); c_copied = sem("c_copied")
        decay_ready = sem("decay_ready"); drive_ready = sem("drive_ready"); state_ready = sem("state_ready")
        read_ready = sem("read_ready"); summed = sem("summed"); skip_added = sem("skip_added")
        gated_ready = sem("gated_ready"); out_ready = sem("out_ready"); resid_done = sem("resid_done")

        def passes(eng):
            for direction in range(2):
                with eng.Fori(0, BATCH) as b:
                    yield direction, b, b + direction * BATCH

        with nc.Block() as block:
            @block.tensor
            def _(pe):
                for direction, b, s in passes(pe):
                    for m in range(2 * HALVES):
                        for c in range(HALF_BANKS):
                            last = pe.matmul(ps[:, 2 * m + c, :], win[:, direction, m * P:(m + 1) * P],
                                             xn[:, direction, bass.ds(b * SEQ + c * BANK, BANK)],
                                             start=True, stop=True)
                        last.then_inc(xz_ready, 1)
                    pe.wait_ge(xp_ready, HALVES * s + HALVES)
                    pe.wait_ge(xc_ready, HALVES * s + HALVES)
                    for c in range(HALF_BANKS):
                        for h in range(HALVES):
                            pe.matmul(ps[0:96, c, :], wx[:, direction, h, 0:96], xc[:, h, c * BANK:(c + 1) * BANK],
                                      start=h == 0, stop=h == HALVES - 1)
                        for h in range(HALVES):
                            last = pe.matmul(ps[0:DT_RANK, 2 + c, :], wx[:, direction, h, 96:96 + DT_RANK],
                                             xc[:, h, c * BANK:(c + 1) * BANK], start=h == 0, stop=h == HALVES - 1)
                    last.then_inc(xdbl_ready, 1)
                    pe.wait_ge(zs_ready, HALVES * s + HALVES)
                    pe.wait_ge(dt_raw_ready, s + 1)
                    for h in range(HALVES):
                        for c in range(HALF_BANKS):
                            last = pe.matmul(ps[:, 4 + 2 * h + c, :], wdt[:, direction, h * P:(h + 1) * P],
                                             dt_raw[:, c * BANK:(c + 1) * BANK], start=True, stop=True)
                        last.then_inc(v_ready, 1)
                    pe.wait_ge(bc_ready, s + 1)
                    pe.wait_ge(dt_ready, HALVES * s + HALVES)

                    def add_reads(n):
                        for h in range(HALVES):
                            pe.wait_ge(read_ready, UNITS * s + 2 * n + h + 1)
                            for c in range(HALF_BANKS):
                                last = pe.matmul(ps[:, 4 + 2 * h + c, :], ident[:, :],
                                                 read[:, h, c * BANK:(c + 1) * BANK],
                                                 start=n == 0, stop=n == D_STATE - 1)
                            last.then_inc(summed, 1)

                    for n in range(D_STATE):
                        if n:
                            pe.wait_ge(drive_ready, UNITS * s + 2 * n)
                        for c in range(HALF_BANKS):
                            last = pe.matmul(b_ps[:, c, :], sel_b[:, n, :], bc[:, c * BANK:(c + 1) * BANK],
                                             start=True, stop=True)
                        last.then_inc(b_ready, 1)
                        if n:
                            pe.wait_ge(c_copied, D_STATE * s + n)
                        for c in range(HALF_BANKS):
                            last = pe.matmul(c_ps[:, c, :], sel_c[:, n, :], bc[:, c * BANK:(c + 1) * BANK],
                                             start=True, stop=True)
                        last.then_inc(c_ready, 1)
                        if n:
                            add_reads(n - 1)
                    add_reads(D_STATE - 1)
                    pe.wait_ge(drive_ready, UNITS * s + UNITS)
                    for h in range(HALVES):
                        pe.wait_ge(gated_ready, HALVES * s + h + 1)
                        for c in range(HALF_BANKS):
                            last = pe.matmul(ps[:, c, :], wout[:, direction, h, :], gated[:, h, c * BANK:(c + 1) * BANK],
                                             start=h == 0, stop=h == HALVES - 1)
                    last.then_inc(out_ready, 1)
                    pe.wait_ge(resid_done, s + 1)

            @block.scalar
            def _(act):
                for direction in range(2):
                    act.activation(neg_a[:, direction, :], packed[:, direction, A_LOG:A_LOG + 32], ACT.Exp).then_inc(a_exp, 1)
                act.wait_ge(a_ready, 1)
                for direction, b, s in passes(act):
                    for h in range(HALVES):
                        act.wait_ge(xz_ready, 4 * s + h + 1)
                        act.copy(xp[:, h, PAD:], ps[:, 2 * h:2 * h + 2, :]).then_inc(xp_ready, 1)
                    for h in range(HALVES):
                        act.wait_ge(xz_ready, 4 * s + HALVES + h + 1)
                        act.activation(zs[:, h, :], ps[:, 4 + 2 * h:6 + 2 * h, :], ACT.Silu).then_inc(zs_ready, 1)
                    for h in range(HALVES):
                        act.wait_ge(conv_ready, HALVES * s + h + 1)
                        act.activation(xc[:, h, :], dtx[:, h, :], ACT.Silu,
                                       bias=packed[:, direction, CONV_B + h:CONV_B + h + 1]).then_inc(xc_ready, 1)
                    act.wait_ge(xdbl_ready, s + 1)
                    act.copy(dt_raw[:, :], ps[0:DT_RANK, 2:4, :]).then_inc(dt_raw_ready, 1)
                    act.copy(bc[:, :], ps[0:96, 0:2, :]).then_inc(bc_high, 1)
                    soft = Steps(soft_step, 4 * s)
                    for h in range(HALVES):
                        act.wait_ge(v_ready, HALVES * s + h + 1)
                        soft.mark(act.activation(expd[:, :], ps[:, 4 + 2 * h:6 + 2 * h, :], ACT.Abs,
                                                 bias=packed[:, direction, DT_B + h:DT_B + h + 1]))
                        soft.wait(act)
                        soft.mark(act.activation(expd[:, :], expd[:, :], ACT.Exp, scale=-1.0))
                        soft.wait(act)
                        act.activation(dt[:, h, :], expd[:, :], ACT.Ln, bias=1.0).then_inc(soft_ready, 1)
                        act.wait_ge(soft_ready, HALVES * s + h + 1)
                    act.wait_ge(dt_ready, HALVES * s + HALVES)
                    for n in range(D_STATE):
                        act.wait_ge(c_ready, D_STATE * s + n + 1)
                        if n > 1:
                            act.wait_ge(read_ready, UNITS * s + 2 * (n - 1))
                        act.copy(c_row[:, n % 2, :], c_ps).then_inc(c_copied, 1)
                        for h in range(HALVES):
                            if n > 1:
                                act.wait_ge(state_ready, UNITS * s + 2 * (n - 2) + h + 1)
                            act.activation(decay[:, h, n % 2, :], dt[:, h, :], ACT.Exp,
                                           scale=neg_a[:, direction, h * D_STATE + n:h * D_STATE + n + 1]
                                           ).then_inc(decay_ready, 1)

            @block.vector
            def _(dve):
                dve.memset(xp[:, :, 0:PAD], 0.0).then_inc(pad_ready, 1)
                dve.wait_ge(a_exp, 2)
                dve.tensor_scalar(neg_a[:, :, :], neg_a[:, :, :], -1.0, None, ALU.mult).then_inc(a_ready, 1)
                dve.wait_ge(pad_ready, 1)
                for direction, b, s in passes(dve):
                    conv = Steps(conv_step, HALVES * (D_CONV - 1) * s)
                    for h in range(HALVES):
                        dve.wait_ge(xp_ready, HALVES * s + h + 1)
                        for k in range(D_CONV):
                            w = packed[:, direction, CONV_W + h * D_CONV + k:CONV_W + h * D_CONV + k + 1]
                            tap = xp[:, h, k:k + SEQ]
                            if k == 0:
                                conv.mark(dve.tensor_scalar(dtx[:, h, :], tap, w, None, ALU.mult))
                                conv.wait(dve)
                                continue
                            ins = dve.scalar_tensor_tensor(out=dtx[:, h, :], in0=tap, scalar=w, in1=dtx[:, h, :],
                                                           op0=ALU.mult, op1=ALU.add)
                            if k < D_CONV - 1:
                                conv.mark(ins)
                                conv.wait(dve)
                            else:
                                ins.then_inc(conv_ready, 1)
                    split = Steps(split_step, 4 * s)
                    dve.wait_ge(bc_high, s + 1)
                    split.mark(dve.tensor_tensor(bc_rest[:, :], ps[0:96, 0:2, :], bc[:, :], ALU.subtract))
                    split.wait(dve)
                    split.mark(dve.tensor_copy(bc[32:64, :], bc_rest[32:64, :]))
                    split.mark(dve.tensor_copy(bc_mid[64:96, :], bc_rest[64:96, :]))
                    split.wait(dve)
                    split.mark(dve.tensor_tensor(bc_rest[64:96, :], bc_rest[64:96, :], bc_mid[64:96, :], ALU.subtract))
                    split.wait(dve)
                    dve.tensor_copy(bc[64:96, :], bc_rest[64:96, :]).then_inc(bc_ready, 1)
                    for h in range(HALVES):
                        dve.wait_ge(v_ready, HALVES * s + h + 1)
                        if h:
                            dve.wait_ge(dt_done, HALVES * s + h)
                        dve.wait_ge(soft_step, 4 * s + 2 * h + 1)
                        dve.tensor_scalar(relu[:, :], ps[:, 4 + 2 * h:6 + 2 * h, :],
                                          packed[:, direction, DT_B + h:DT_B + h + 1], 0.0,
                                          ALU.add, ALU.max).then_inc(relu_ready, 1)
                        dve.wait_ge(relu_ready, HALVES * s + h + 1)
                        dve.wait_ge(soft_ready, HALVES * s + h + 1)
                        dve.tensor_tensor(dt[:, h, :], dt[:, h, :], relu[:, :], ALU.add).then_inc(dt_done, 1)
                        dve.wait_ge(dt_done, HALVES * s + h + 1)
                        dve.wait_ge(xc_ready, HALVES * s + h + 1)
                        dve.tensor_tensor(dtx[:, h, :], dt[:, h, :], xc[:, h, :], ALU.mult).then_inc(dt_ready, 1)
                    dve.wait_ge(dt_ready, HALVES * s + HALVES)

                    def make_drive(u):
                        dve.wait_ge(b_ready, D_STATE * s + u // 2 + 1)
                        if u > 1:
                            dve.wait_ge(state_ready, UNITS * s + u - 1)
                        dve.tensor_tensor(drive[:, u % 2, :], dtx[:, u % 2, :], b_ps, ALU.mult).then_inc(drive_ready, 1)

                    make_drive(0)
                    for u in range(UNITS):
                        if u + 1 < UNITS:
                            make_drive(u + 1)
                        dve.wait_ge(decay_ready, UNITS * s + u + 1)
                        dve.wait_ge(drive_ready, UNITS * s + u + 1)
                        if u > 2:
                            dve.wait_ge(read_ready, UNITS * s + u - 2)
                        dve.tensor_tensor_scan(state[:, u % 3, :], decay[:, u % 2, (u // 2) % 2, :], drive[:, u % 2, :],
                                               0.0, ALU.mult, ALU.add).then_inc(state_ready, 1)
                    for h in range(HALVES):
                        dve.wait_ge(summed, UNITS * s + UNITS - 1 + h)
                        dve.scalar_tensor_tensor(out=gated[:, h, :], in0=xc[:, h, :],
                                                 scalar=packed[:, direction, D_SKIP + h:D_SKIP + h + 1],
                                                 in1=ps[:, 4 + 2 * h:6 + 2 * h, :], op0=ALU.mult,
                                                 op1=ALU.add).then_inc(skip_added, 1)
                        dve.wait_ge(skip_added, HALVES * s + h + 1)
                        dve.wait_ge(zs_ready, HALVES * s + h + 1)
                        dve.tensor_tensor(gated[:, h, :], gated[:, h, :], zs[:, h, :], ALU.mult).then_inc(gated_ready, 1)
                    dve.wait_ge(out_ready, s + 1)
                    r = resid[:, bass.ds(b * SEQ, SEQ)]
                    y = ps[:, 0:2, :].rearrange("p a b -> p (a b)")
                    if direction:
                        y = y[:, ::-1]
                    dve.scalar_tensor_tensor(out=r, in0=y, scalar=0.5, in1=r,
                                             op0=ALU.mult, op1=ALU.add).then_inc(resid_done, 1)
                    dve.wait_ge(resid_done, s + 1)

            @block.gpsimd
            def _(pool):
                for direction, b, s in passes(pool):
                    for u in range(UNITS):
                        pool.wait_ge(state_ready, UNITS * s + u + 1)
                        pool.wait_ge(c_copied, D_STATE * s + u // 2 + 1)
                        if u > 1:
                            pool.wait_ge(summed, UNITS * s + u - 1)
                        pool.tensor_tensor(read[:, u % 2, :], state[:, u % 3, :], c_row[:, (u // 2) % 2, :],
                                           ALU.mult).then_inc(read_ready, 1)


DEPTH, HEADS, HEAD_DIM, WINDOW = 6, 16, 64, 32
PAIRS = HEADS // 2
INNER = HEADS * HEAD_DIM
HIDDEN = int(DIM * 4 * 2 / 3)
HIDDEN_PARTS = [(0, P), (P, P), (2 * P, HIDDEN - 2 * P)]
QK_SCALE = 8.0
TILES = TOKENS // P
SEQ_TILES = SEQ // P
CHUNKS = TOKENS // BANK
SEQ_CHUNKS = SEQ // BANK
WINDOWS = P // WINDOW
LEAD = 64
KEYS = P + WINDOW
HIDDEN_ROW = -1e30
NORM_SHIFT = 20
LN_G, LN_B, OUT_B, A_B, GATE_B = 0, 1, 2, 3, 6
LAYER_PACKED = 9


def pipeline(eng, stages, warm):
    last = max(lag for lag, _ in stages)

    def step(i, odd):
        for lag, stage in stages:
            if not isinstance(i, int) or 0 <= i - lag < TILES:
                stage(i - lag, (odd - lag) % 2)

    for i in range(warm):
        step(i, i % 2)
    with eng.Fori(warm // 2, TILES // 2) as two:
        step(2 * two, 0)
        step(2 * two + 1, 1)
    for i in range(TILES, TILES + last):
        step(i, i % 2)


def later(tile, n):
    return not isinstance(tile, int) or tile >= n


def transformer(nc, ctx, ident, xa, xb, hbm):
    def sb(name, shape, dt=F32):
        return ctx.enter_context(nc.sbuf_tensor(name, shape, dt))

    def sem(name):
        return ctx.enter_context(nc.semaphore(name))

    w_qk = sb("w_qk", [P, 2 * INNER])
    w_v = sb("w_v", [P, PAIRS, P])
    w_o = sb("w_o", [P, PAIRS, P])
    w_vo = sb("w_vo", [P, HEADS, P])
    w1 = sb("w1", [P, 2 * HIDDEN])
    w2 = sb("w2", [P, 3, P])
    lp = sb("lp", [P, LAYER_PACKED])
    head_scale = sb("head_scale", [P, 2, HEAD_DIM])
    rope = sb("rope", [P, 4, SEQ_TILES, HEAD_DIM])
    rope_l = sb("rope_l", [P, 4, SEQ_TILES, HEAD_DIM])
    sight = sb("sight", [P, SEQ_TILES, 2 * WINDOW])
    keep = sb("keep", [P, SEQ_TILES])
    exp_shift = sb("exp_shift", [P, 1])
    ones_mean = sb("ones_mean2", [P, P])
    eps_col = sb("eps_col2", [P, 1])

    xs = sb("xs", [P, 2, P])
    xw = sb("xw", [P, 2, WINDOWS, 2 * 2 * WINDOW])
    x_rows = sb("x_rows", [P, 2, WINDOWS, P])
    qk = sb("qk", [P, 2, 2 * INNER])
    sq = sb("sq", [P, 2, 2 * INNER])
    ssq = sb("ssq", [P, 2, 2 * HEADS])
    rnorm = sb("rnorm", [P, 2, 2 * HEADS])
    q_t = sb("q_t", [P, PAIRS, P])
    k_t = sb("k_t", [P, 2, PAIRS, 2, KEYS])
    prob = sb("prob", [P, 2, HEADS, 2 * WINDOW])
    stat = sb("stat", [P, 2, 2, HEADS])
    prob_t = sb("prob_t", [P, PAIRS, P])
    mixed = sb("mixed", [P, 2, PAIRS, 2, P])
    ps = ctx.enter_context(nc.psum_tensor("ps", [P, 8, BANK], F32))
    A, T, S, G = 0, 2, 4, 6

    names = """wqk_loaded wvo_loaded wff_loaded const_loaded const_set vo_ready vo_copied rope_ready
        xs_low xs_high xs_ready xw_low xw_high xw_ready proj_ready qk_kept sq_ready ssq_raw ssq_ready rot_s rot_c
        rs_log rs_ready rot_sum rot_done heads_ready heads_copied rows_ready rows_copied halo_done s_ready masked
        max_ready shifted exp_ready sum_raw sum_ready prob_ready pt_ready pt_copied px_ready px_copied o_ready o_added
        fx_low fx_high fx_ready mean_ready centred squared var_ready log_ready rstd_ready scaled fn_ready
        gate_ready gelu_ready a_ready hidden_ready fo_ready x_written""".split()
    z = {n: sem(n) for n in names}
    (wqk_loaded, wvo_loaded, wff_loaded, const_loaded, const_set, vo_ready, vo_copied, rope_ready,
     xs_low, xs_high, xs_ready, xw_low, xw_high, xw_ready, proj_ready, qk_kept, sq_ready, ssq_raw, ssq_ready, rot_s,
     rot_c, rs_log, rs_ready, rot_sum, rot_done, heads_ready, heads_copied, rows_ready, rows_copied, halo_done, s_ready,
     masked, max_ready, shifted, exp_ready, sum_raw, sum_ready, prob_ready, pt_ready, pt_copied, px_ready, px_copied,
     o_ready, o_added, fx_low, fx_high, fx_ready, mean_ready, centred, squared, var_ready, log_ready, rstd_ready,
     scaled, fn_ready, gate_ready, gelu_ready, a_ready, hidden_ready, fo_ready, x_written) = [z[n] for n in names]

    def ff(odd):
        return (qk[:, odd, 0:BANK], qk[:, odd, BANK:2 * BANK], qk[:, odd, 2 * BANK:3 * BANK],
                [sq[0:m, odd, k * BANK:(k + 1) * BANK] for k, (_, m) in enumerate(HIDDEN_PARTS)])
    MEAN, VAR, GATE, VALUE = 0, 1, 2, 5

    def ff_pipeline(eng, stages):
        def step(c, odd):
            for ahead, stage in stages:
                if not isinstance(c, int) or 0 <= c + ahead < CHUNKS:
                    stage(c + ahead, (odd + ahead) % 2)
        step(-1, 1)
        step(0, 0)
        step(1, 1)
        with eng.Fori(1, CHUNKS // 2 - 1) as two:
            step(2 * two, 0)
            step(2 * two + 1, 1)
        step(CHUNKS - 2, 0)
        step(CHUNKS - 1, 1)

    def shift_in(eng, dst, src, first, tokens_before, tile, low, high, ready, n, start):
        width = dst.shape[1]
        eng.tensor_copy(dst[0:64, :], src[0:64, bass.ds(first, width)]).then_inc(low, 1)
        ins = eng.tensor_copy(dst[64:128, :], src[64:128, bass.ds(first - 1, width)])
        if not start:
            ins.then_inc(ready, 1)
            return
        ins.then_inc(high, 1)
        eng.wait_ge(high, n)
        col = dst[64:128, tokens_before:tokens_before + 1]
        eng.tensor_tensor(col, col, keep[64:128, bass.ds(tile % SEQ_TILES, 1)], ALU.mult).then_inc(ready, 1)

    with nc.Block() as block:
        @block.sync
        def _(sp):
            consts = [(rope, hbm["rope"]), (sight, hbm["sight"]), (keep, hbm["keep"])]
            for dst, src in consts:
                sp.dma_start(dst[:], src).then_inc(const_loaded, 16)
            for l in range(DEPTH):
                if l:
                    sp.wait_ge(proj_ready, 4 * TILES * l)
                    sp.wait_ge(rope_ready, 4 * l)
                sp.dma_start(w_qk[:, :], hbm["w_qk"][l]).then_inc(wqk_loaded, 16)
                sp.dma_start(head_scale[:, :, :], hbm["head_scale"][l].partition_broadcast(P)
                             ).then_inc(wqk_loaded, 16)
                if l:
                    sp.wait_ge(vo_ready, l)
                sp.dma_start(w_v[:, :, :], hbm["w_v"][l]).then_inc(wvo_loaded, 16)
                sp.dma_start(w_o[:, :, :], hbm["w_o"][l]).then_inc(wvo_loaded, 16)
                if l:
                    sp.wait_ge(x_written, CHUNKS * l)
                sp.dma_start(w1[:, :], hbm["w1"][l]).then_inc(wff_loaded, 16)
                sp.dma_start(w2[:, :, :], hbm["w2"][l]).then_inc(wff_loaded, 16)
                sp.dma_start(lp[:, :], hbm["lp"][l]).then_inc(wff_loaded, 16)

        @block.tensor
        def _(pe):
            pe.wait_ge(const_set, 6)
            with pe.Fori(0, DEPTH) as l:
                base = l * TILES
                pe.wait_ge(wvo_loaded, 32 * l + 32)
                for h in range(HEADS):
                    rows = slice(64 * (h % 2), 64 * (h % 2) + 64)
                    last = pe.matmul(ps[:, 2 * (h % 2) + h // 8, (h // 2 % 4) * P:(h // 2 % 4 + 1) * P],
                                     w_v[rows, h // 2, :], w_o[rows, h // 2, :], start=True, stop=True)
                last.then_inc(vo_ready, 1)
                pe.wait_ge(vo_copied, 4 * l + 4)

                def project(c):
                    def stage(t, odd):
                        g = base + t
                        if c == 0:
                            pe.wait_ge(xs_ready, g + 1)
                            if isinstance(t, int) and t == 0:
                                pe.wait_ge(wqk_loaded, 32 * l + 32)
                        if later(t, 1) or c > 1:
                            pe.wait_ge(sq_ready, 4 * g + c - 1)
                        pe.matmul(ps[:, A + c % 2, :], xs[:, odd, :], w_qk[:, c * BANK:(c + 1) * BANK],
                                  start=True, stop=True).then_inc(proj_ready, 1)
                    return stage

                def head_transposes(c):
                    def stage(t, odd):
                        g = base + t
                        pe.wait_ge(rot_done, 2 * g + c // 2 + 1)
                        if c == 0:
                            if later(t, 2):
                                pe.wait_ge(pt_copied, 2 * g - 2)
                            elif t == 1:
                                pe.wait_ge(rows_copied, g)
                        elif c == 1:
                            if later(t, 3):
                                pe.wait_ge(o_added, g - 2)
                            elif t == 2:
                                pe.wait_ge(pt_copied, 2 * g - 3)
                            elif t == 1:
                                pe.wait_ge(heads_copied, 4 * g)
                        elif c > 1:
                            pe.wait_ge(heads_copied, 4 * g + c - 1)
                        for j in range(4):
                            col = c * BANK + j * P
                            last = pe.transpose(ps[:, T + c % 2, j * P:(j + 1) * P], qk[:, odd, col:col + P], ident[:, :])
                        last.then_inc(heads_ready, 1)
                    return stage

                def row_transposes(t, odd):
                    g = base + t
                    pe.wait_ge(xw_ready, g + 1)
                    pe.wait_ge(heads_copied, 4 * g + 3)
                    for w in range(WINDOWS):
                        last = pe.transpose(ps[:, T, w * P:(w + 1) * P], xw[:, odd, w, :], ident[:, :])
                    last.then_inc(rows_ready, 1)

                def scores(t, odd):
                    g = base + t
                    pe.wait_ge(heads_copied, 4 * g + 4)
                    pe.wait_ge(halo_done, g + 1)
                    if later(t, 1):
                        pe.wait_ge(masked, g)
                    for a in range(PAIRS):
                        for w in range(WINDOWS):
                            last = pe.matmul(ps[w * WINDOW:(w + 1) * WINDOW, S + a // 4, (a % 4) * P:(a % 4 + 1) * P],
                                             q_t[:, a, w * WINDOW:(w + 1) * WINDOW],
                                             k_t[:, odd, a, :, w * WINDOW:(w + 2) * WINDOW], start=True, stop=True,
                                             skip_group_check=True)
                    last.then_inc(s_ready, 1)

                def prob_transposes(c):
                    def stage(t, odd):
                        g = base + t
                        pe.wait_ge(prob_ready, g + 1)
                        if c == 0:
                            if not isinstance(t, int) or t + 1 < TILES:
                                pe.wait_ge(heads_copied, 4 * g + 8)
                            elif t + 1 == TILES:
                                pe.wait_ge(o_added, g - 1)
                            bank = T + 1
                        else:
                            if not isinstance(t, int) or t + 1 < TILES:
                                pe.wait_ge(rows_copied, g + 2)
                            elif t + 1 == TILES:
                                pe.wait_ge(pt_copied, 2 * g)
                            bank = T
                        for j in range(4):
                            a = 4 * c + j
                            last = pe.transpose(ps[:, bank, j * P:(j + 1) * P],
                                                prob[:, odd, 2 * a:2 * a + 2, :].rearrange("p h k -> p (h k)"), ident[:, :])
                        last.then_inc(pt_ready, 1)
                    return stage

                def mix(r):
                    def stage(t, odd):
                        g = base + t
                        if r == 0:
                            pe.wait_ge(rows_copied, g + 1)
                            pe.wait_ge(pt_copied, 2 * g + 2)
                        if later(t, 1) or r:
                            pe.wait_ge(px_copied, 2 * (2 * g + r))
                        for w in (2 * r, 2 * r + 1):
                            for h in range(2):
                                rows = slice(64 * h, 64 * h + 64)
                                last = pe.matmul(ps[:, G + h, (w % 2) * 256:(w % 2 + 1) * 256],
                                                 x_rows[rows, odd, w, :], prob_t[rows, :, w * WINDOW:(w + 1) * WINDOW],
                                                 start=True, stop=True, skip_group_check=True)
                        last.then_inc(px_ready, 1)
                    return stage

                def output(t, odd):
                    g = base + t
                    pe.wait_ge(px_copied, 4 * g + 4)
                    if not isinstance(t, int) or t + 1 < TILES:
                        pe.wait_ge(pt_copied, 2 * g + 3)
                    else:
                        pe.wait_ge(o_added, g)
                    for a in range(PAIRS):
                        for h in range(2):
                            last = pe.matmul(ps[:, T + 1, 0:P], w_vo[:, 2 * a + h, :], mixed[:, odd, a, h, :],
                                             start=a + h == 0, stop=a == PAIRS - 1 and h == 1)
                    last.then_inc(o_ready, 1)

                pipeline(pe, [(3, head_transposes(0)), (3, head_transposes(1)), (1, project(0)),
                              (3, head_transposes(2)), (3, head_transposes(3)), (3, row_transposes), (1, project(1)),
                              (4, prob_transposes(0)), (4, prob_transposes(1)), (3, scores), (1, project(2)),
                              (4, mix(0)), (1, project(3)), (4, mix(1)), (5, output)], 6)

                def means(c, odd):
                    xf, xc, work, hid = ff(odd)
                    pe.wait_ge(fx_ready, CHUNKS * l + c + 1)
                    if isinstance(c, int) and c == 0:
                        pe.wait_ge(o_added, base + TILES)
                    if later(c, 2):
                        pe.wait_ge(x_written, CHUNKS * l + c - 1)
                    elif c == 1:
                        pe.wait_ge(centred, CHUNKS * l + 1)
                    pe.matmul(ps[:, MEAN, :], ones_mean[:, :], xf, start=True, stop=True).then_inc(mean_ready, 1)

                def variances(c, odd):
                    xf, xc, work, hid = ff(odd)
                    pe.wait_ge(squared, CHUNKS * l + c + 1)
                    if later(c, 1):
                        pe.wait_ge(log_ready, CHUNKS * l + c)
                    pe.matmul(ps[:, VAR, :], ones_mean[:, :], work, start=True, stop=True).then_inc(var_ready, 1)

                def hidden(kind):
                    def stage(c, odd):
                        xf, xc, work, hid = ff(odd)
                        if isinstance(c, int) and c == 0:
                            pe.wait_ge(wff_loaded, 48 * l + 48)
                        pe.wait_ge(fn_ready, CHUNKS * l + c + 1)
                        bank, ready, taken, first = ((GATE, gate_ready, gelu_ready, HIDDEN) if kind else
                                                     (VALUE, a_ready, hidden_ready, 0))
                        for k, (lo, m) in enumerate(HIDDEN_PARTS):
                            if later(c, 1):
                                pe.wait_ge(taken, 3 * (CHUNKS * l + c) - 2 + k)
                            pe.matmul(ps[0:m, bank + k, :], w1[:, first + lo:first + lo + m], xc,
                                      start=True, stop=True).then_inc(ready, 1)
                    return stage

                def ff_out(c, odd):
                    xf, xc, work, hid = ff(odd)
                    if not isinstance(c, int) or c + 1 < CHUNKS:
                        pe.wait_ge(centred, CHUNKS * l + c + 2)
                    else:
                        pe.wait_ge(x_written, CHUNKS * l + c)
                    for k, (lo, m) in enumerate(HIDDEN_PARTS):
                        pe.wait_ge(hidden_ready, 3 * (CHUNKS * l + c) + k + 1)
                        last = pe.matmul(ps[:, MEAN, :], w2[0:m, k, :], hid[k], start=k == 0, stop=k == 2)
                    last.then_inc(fo_ready, 1)

                ff_pipeline(pe, [(1, means), (0, hidden(1)), (0, hidden(0)), (1, variances), (0, ff_out)])
                pe.wait_ge(x_written, CHUNKS * l + CHUNKS)

        @block.scalar
        def _(act):
            act.preload_act_table_set("natural_log_exp_and_others")
            act.wait_ge(const_set, 6)
            with act.Fori(0, DEPTH) as l:
                base = l * TILES
                for k in range(4):
                    act.wait_ge(vo_ready, l + 1)
                    act.copy(w_vo[:, (k % 2) * 8 + k // 2:(k % 2) * 8 + k // 2 + 7:2, :],
                             ps[:, k, :].rearrange("p (j n) -> p j n", j=4)).then_inc(vo_copied, 1)

                def keep_projection(c):
                    def stage(t, odd):
                        g = base + t
                        act.wait_ge(proj_ready, 4 * g + c + 1)
                        if later(t, 2):
                            act.wait_ge(heads_ready, 4 * (g - 2) + c + 1)
                        cols = slice(c * BANK, (c + 1) * BANK)
                        act.copy(qk[:, odd, cols], ps[:, A + c % 2, :]).then_inc(qk_kept, 1)
                        act.activation(sq[:, odd, cols], ps[:, A + c % 2, :], ACT.Square).then_inc(sq_ready, 1)
                    return stage

                def rsqrt_norms(t, odd):
                    g = base + t
                    act.wait_ge(ssq_ready, g + 1)
                    if later(t, 2):
                        act.wait_ge(rot_done, 2 * (g - 2) + 2)
                    act.activation(rnorm[:, odd, :], ssq[:, odd, :], ACT.Ln, scale=float(2 ** NORM_SHIFT)).then_inc(rs_log, 1)
                    act.wait_ge(rs_log, g + 1)
                    act.activation(rnorm[:, odd, :], rnorm[:, odd, :], ACT.Exp, scale=-0.5,
                                   bias=exp_shift[:, 0:1]).then_inc(rs_ready, 1)

                def copy_heads(c):
                    def stage(t, odd):
                        g = base + t
                        act.wait_ge(heads_ready, 4 * g + c + 1)
                        if later(t, 1) and c == 0:
                            act.wait_ge(s_ready, g)
                        bank = ps[:, T + c % 2, :].rearrange("p (j n) -> p j n", j=4)
                        if c < 2:
                            act.copy(q_t[:, 4 * c:4 * c + 4, :], bank).then_inc(heads_copied, 1)
                            return
                        if later(t, 1):
                            act.wait_ge(halo_done, g)
                        pairs = slice(4 * (c - 2), 4 * (c - 2) + 4)
                        act.copy(k_t[0:64, odd, pairs, 0, WINDOW:], bank[0:64])
                        act.copy(k_t[64:128, odd, pairs, 1, WINDOW:], bank[64:128]).then_inc(heads_copied, 1)
                    return stage

                def copy_rows(t, odd):
                    g = base + t
                    act.wait_ge(rows_ready, g + 1)
                    if later(t, 2):
                        act.wait_ge(px_ready, 2 * (g - 2) + 2)
                    act.copy(x_rows[:, odd, :, :], ps[:, T, :].rearrange("p (w n) -> p w n", w=4)).then_inc(rows_copied, 1)

                def exponent(t, odd):
                    g = base + t
                    act.wait_ge(shifted, g + 1)
                    act.activation(prob[:, odd, :, :], prob[:, odd, :, :], ACT.Exp, scale=QK_SCALE).then_inc(exp_ready, 1)

                def copy_probs(c):
                    def stage(t, odd):
                        g = base + t
                        act.wait_ge(pt_ready, 2 * g + c + 1)
                        if later(t, 1):
                            act.wait_ge(px_ready, 2 * g)
                        act.copy(prob_t[:, 4 * c:4 * c + 4, :],
                                 ps[:, T + 1 - c, :].rearrange("p (j n) -> p j n", j=4)).then_inc(pt_copied, 1)
                    return stage

                def copy_mixed(r):
                    def stage(t, odd):
                        g = base + t
                        act.wait_ge(px_ready, 2 * g + r + 1)
                        if later(t, 2):
                            act.wait_ge(o_ready, g - 1)
                        for h in range(2):
                            dst = mixed[:, odd, :, h, :].rearrange("p a (w n) -> p w a n", w=4)[:, 2 * r:2 * r + 2]
                            act.copy(dst, ps[:, G + h, :].rearrange("p (w a n) -> p w a n", w=2, a=PAIRS)
                                     ).then_inc(px_copied, 1)
                    return stage

                pipeline(act, [(3, copy_heads(0)), (3, copy_heads(1)), (1, keep_projection(0)),
                               (3, copy_heads(2)), (3, copy_heads(3)), (3, copy_rows), (2, rsqrt_norms),
                               (1, keep_projection(1)), (4, copy_probs(0)), (4, copy_probs(1)),
                               (1, keep_projection(2)), (4, copy_mixed(0)), (3, exponent),
                               (1, keep_projection(3)), (4, copy_mixed(1))], 6)

                def square(c, odd):
                    xf, xc, work, hid = ff(odd)
                    act.wait_ge(centred, CHUNKS * l + c + 1)
                    act.activation(work, xc, ACT.Square).then_inc(squared, 1)

                def rstd(c, odd):
                    xf, xc, work, hid = ff(odd)
                    act.wait_ge(var_ready, CHUNKS * l + c + 1)
                    act.activation(work, ps[:, VAR, :], ACT.Ln, bias=eps_col[:, 0:1]).then_inc(log_ready, 1)
                    act.wait_ge(log_ready, CHUNKS * l + c + 1)
                    act.activation(work, work, ACT.Exp, scale=-0.5).then_inc(rstd_ready, 1)

                def gelu(c, odd):
                    xf, xc, work, hid = ff(odd)
                    for k, (lo, m) in enumerate(HIDDEN_PARTS):
                        act.wait_ge(gate_ready, 3 * (CHUNKS * l + c) + k + 1)
                        if later(c, 2):
                            act.wait_ge(fo_ready, CHUNKS * l + c - 1)
                        act.activation(hid[k], ps[0:m, GATE + k, :], ACT.Gelu,
                                       bias=lp[0:m, GATE_B + k:GATE_B + k + 1]).then_inc(gelu_ready, 1)

                ff_pipeline(act, [(1, square), (0, gelu), (1, rstd)])

        @block.vector
        def _(dve):
            dve.memset(exp_shift[:, :], float(np.log(2.0) * NORM_SHIFT / 2)).then_inc(const_set, 1)
            dve.memset(ones_mean[:, :], 1.0 / DIM).then_inc(const_set, 1)
            dve.memset(eps_col[:, :], EPS).then_inc(const_set, 1)
            dve.memset(xb[:, 0:LEAD], 0.0).then_inc(const_set, 1)
            dve.wait_ge(const_loaded, 48)
            dve.wait_ge(const_set, 6)
            with dve.Fori(0, DEPTH) as l:
                base = l * TILES

                def rotate(part):
                    def stage(t, odd):
                        g = base + t
                        cols = slice(part * INNER, (part + 1) * INNER)
                        heads = qk[:, odd, cols].rearrange("p (h d) -> p h d", d=HEAD_DIM)
                        swapped = qk[:, odd, cols].rearrange("p (h s d) -> p h s d", s=2, d=HEAD_DIM // 2)[:, :, ::-1, :]
                        sines = sq[:, odd, cols].rearrange("p (h d) -> p h d", d=HEAD_DIM)
                        dve.wait_ge(sq_ready, 4 * g + 2 * part + 2)
                        if later(t, 2) and part == 0:
                            dve.wait_ge(rs_log, g - 1)
                        dve.tensor_reduce(ssq[:, odd, part * HEADS:(part + 1) * HEADS], sines, AX_X, ALU.add).then_inc(ssq_raw, 1)
                        dve.wait_ge(ssq_raw, 2 * g + part + 1)
                        if isinstance(t, int) and t == 0:
                            dve.wait_ge(rope_ready, 4 * l + 4)

                        def table(i):
                            return rope_l[:, 2 * part + i, bass.ds(t % SEQ_TILES, 1), :].to_broadcast([P, HEADS, HEAD_DIM])
                        dve.tensor_tensor(sq[:, odd, cols].rearrange("p (h s d) -> p h s d", s=2, d=HEAD_DIM // 2), swapped,
                                          table(1).rearrange("p h (s d) -> p h s d", s=2), ALU.mult).then_inc(rot_s, 1)
                        dve.wait_ge(rot_s, 2 * g + part + 1)
                        dve.tensor_tensor(heads, heads, table(0), ALU.mult).then_inc(rot_c, 1)
                        if part == 1:
                            dve.tensor_scalar(ssq[:, odd, :], ssq[:, odd, :], 1e-24, None, ALU.max).then_inc(ssq_ready, 1)
                    return stage

                def masked_softmax(t, odd):
                    g = base + t
                    dve.wait_ge(s_ready, g + 1)
                    if later(t, 2):
                        dve.wait_ge(pt_ready, 2 * g - 2)
                    p = prob[:, odd, :, :]
                    mx, sm = stat[:, odd, 0, :], stat[:, odd, 1, :]
                    dve.tensor_tensor(p, ps[:, S:S + 2, :].rearrange("p b (h k) -> p (b h) k", k=2 * WINDOW),
                                      sight[:, bass.ds(t % SEQ_TILES, 1), :].to_broadcast([P, HEADS, 2 * WINDOW]),
                                      ALU.add).then_inc(masked, 1)
                    dve.wait_ge(masked, g + 1)
                    dve.tensor_reduce(mx, p, AX_X, ALU.max).then_inc(max_ready, 1)
                    dve.wait_ge(max_ready, g + 1)
                    dve.tensor_tensor(p, p, mx.unsqueeze(2).to_broadcast([P, HEADS, 2 * WINDOW]),
                                      ALU.subtract).then_inc(shifted, 1)

                def sums(t, odd):
                    g = base + t
                    sm = stat[:, odd, 1, :]
                    dve.wait_ge(exp_ready, g + 1)
                    if later(t, 2):
                        dve.wait_ge(prob_ready, g - 1)
                    dve.tensor_reduce(sm, prob[:, odd, :, :], AX_X, ALU.add).then_inc(sum_raw, 1)
                    dve.wait_ge(sum_raw, g + 1)
                    dve.reciprocal(sm, sm).then_inc(sum_ready, 1)

                def add_output(t, odd):
                    g = base + t
                    dve.wait_ge(o_ready, g + 1)
                    cols = bass.ds(LEAD + t * P, P)
                    dve.tensor_tensor(xb[:, cols], ps[:, T + 1, 0:P], xa[:, cols], ALU.add).then_inc(o_added, 1)

                def shift_tile(t, odd):
                    if later(t, 2):
                        dve.wait_ge(proj_ready, 4 * (base + t - 1))
                    shift_in(dve, xs[:, odd, :], xa, LEAD + t * P, 0, t, xs_low, xs_high, xs_ready, base + t + 1, True)

                def shift_windows(t, odd):
                    g = base + t
                    if later(t, 2):
                        dve.wait_ge(rows_ready, g - 1)

                    def seen(rows, before):
                        first = xa[rows, bass.ds(LEAD + t * P - WINDOW - before, KEYS)]
                        return bass.AP(first.tensor, first.offset, [first.ap[0], (WINDOW, WINDOWS), (0, 2), (1, 2 * WINDOW)])
                    low, high = (xw[r, odd].rearrange("p w (c k) -> p w c k", c=2) for r in (slice(0, 64), slice(64, 128)))
                    dve.tensor_copy(low, seen(slice(0, 64), 0)).then_inc(xw_low, 1)
                    dve.tensor_copy(high, seen(slice(64, 128), 1)).then_inc(xw_high, 1)
                    dve.wait_ge(xw_high, g + 1)
                    for w, key in ((0, WINDOW), (1, 0)):
                        col = high[:, w, :, key]
                        last = dve.tensor_tensor(col, col, keep[64:128, bass.ds(t % SEQ_TILES, 1)].to_broadcast([64, 2]), ALU.mult)
                    last.then_inc(xw_ready, 1)

                pipeline(dve, [(0, shift_tile), (2, shift_windows), (2, rotate(0)), (2, rotate(1)), (5, add_output), (3, masked_softmax), (3, sums)], 6)

                def centre(c, odd):
                    xf, xc, work, hid = ff(odd)
                    dve.wait_ge(mean_ready, CHUNKS * l + c + 1)
                    if later(c, 2):
                        dve.wait_ge(a_ready, 3 * (CHUNKS * l + c - 1))
                    dve.tensor_tensor(xc, xf, ps[:, MEAN, :], ALU.subtract).then_inc(centred, 1)

                def normalise(c, odd):
                    xf, xc, work, hid = ff(odd)
                    dve.wait_ge(rstd_ready, CHUNKS * l + c + 1)
                    dve.tensor_tensor(xc, xc, work, ALU.mult).then_inc(scaled, 1)
                    if isinstance(c, int) and c == 0:
                        dve.wait_ge(wff_loaded, 48 * l + 48)
                    dve.wait_ge(scaled, CHUNKS * l + c + 1)
                    dve.tensor_scalar(xc, xc, lp[:, LN_G:LN_G + 1], lp[:, LN_B:LN_B + 1], ALU.mult,
                                      ALU.add).then_inc(fn_ready, 1)

                def gate(c, odd):
                    xf, xc, work, hid = ff(odd)
                    for k, (lo, m) in enumerate(HIDDEN_PARTS):
                        dve.wait_ge(a_ready, 3 * (CHUNKS * l + c) + k + 1)
                        dve.wait_ge(gelu_ready, 3 * (CHUNKS * l + c) + k + 1)
                        dve.scalar_tensor_tensor(out=hid[k], in0=ps[0:m, VALUE + k, :], scalar=lp[0:m, A_B + k:A_B + k + 1],
                                                 in1=hid[k], op0=ALU.add, op1=ALU.mult).then_inc(hidden_ready, 1)

                def add_ff(c, odd):
                    dve.wait_ge(fo_ready, CHUNKS * l + c + 1)
                    cols = bass.ds(LEAD + c * BANK, BANK)
                    dve.scalar_tensor_tensor(out=xa[:, cols], in0=ps[:, MEAN, :], scalar=lp[:, OUT_B:OUT_B + 1],
                                             in1=xb[:, cols], op0=ALU.add, op1=ALU.add).then_inc(x_written, 1)

                def shift_chunk(c, odd):
                    xf, xc, work, hid = ff(odd)
                    if isinstance(c, int) and c == 0:
                        dve.wait_ge(o_added, base + TILES)
                    shift_in(dve, xf, xb, LEAD + c * BANK, 0, (SEQ_TILES // SEQ_CHUNKS) * c, fx_low, fx_high, fx_ready,
                             (CHUNKS // SEQ_CHUNKS) * l + c // 2 + 1 if odd == 0 else 0, odd == 0)

                ff_pipeline(dve, [(1, shift_chunk), (1, centre), (0, gate), (1, normalise), (0, add_ff)])
                dve.wait_ge(x_written, CHUNKS * l + CHUNKS)

        @block.gpsimd
        def _(pool):
            pool.memset(k_t[:, 0], 0.0).then_inc(const_set, 1)
            pool.memset(k_t[:, 1], 0.0).then_inc(const_set, 1)
            pool.wait_ge(const_loaded, 48)
            pool.wait_ge(const_set, 6)

            with pool.Fori(0, DEPTH) as l:
                base = l * TILES
                pool.wait_ge(wqk_loaded, 32 * l + 32)
                for part in range(2):
                    scale = head_scale[:, part, :]
                    partner = scale.rearrange("p (s d) -> p s d", s=2)[:, ::-1, :]
                    pool.tensor_tensor(rope_l[:, 2 * part], rope[:, 2 * part],
                                       scale.unsqueeze(1).to_broadcast([P, SEQ_TILES, HEAD_DIM]), ALU.mult).then_inc(rope_ready, 1)
                    pool.tensor_tensor(rope_l[:, 2 * part + 1].rearrange("p t (s d) -> p t s d", s=2),
                                       rope[:, 2 * part + 1].rearrange("p t (s d) -> p t s d", s=2),
                                       partner.unsqueeze(1).to_broadcast([P, SEQ_TILES, 2, HEAD_DIM // 2]),
                                       ALU.mult).then_inc(rope_ready, 1)

                def halo(t, odd):
                    g = base + t
                    if later(t, 1):
                        pool.wait_ge(heads_copied, 4 * g)
                    if later(t, 2):
                        pool.wait_ge(s_ready, g - 1)
                    first = keep[:, bass.ds(t % SEQ_TILES, 1)].unsqueeze(2).to_broadcast([P, 2 * PAIRS, WINDOW])
                    pool.tensor_tensor(k_t[:, odd, :, :, 0:WINDOW].rearrange("p a h k -> p (a h) k"),
                                       k_t[:, 1 - odd, :, :, P:P + WINDOW].rearrange("p a h k -> p (a h) k"), first,
                                       ALU.mult).then_inc(halo_done, 1)

                def combine(part):
                    def stage(t, odd):
                        g = base + t
                        cols = slice(part * INNER, (part + 1) * INNER)
                        heads = qk[:, odd, cols].rearrange("p (h d) -> p h d", d=HEAD_DIM)
                        pool.wait_ge(rot_c, 2 * g + part + 1)
                        pool.tensor_tensor(qk[:, odd, cols], qk[:, odd, cols], sq[:, odd, cols], ALU.add).then_inc(rot_sum, 1)
                        pool.wait_ge(rot_sum, 2 * g + part + 1)
                        pool.wait_ge(rs_ready, g + 1)
                        norms = rnorm[:, odd, part * HEADS:(part + 1) * HEADS].unsqueeze(2).to_broadcast([P, HEADS, HEAD_DIM])
                        pool.tensor_tensor(heads, heads, norms, ALU.mult).then_inc(rot_done, 1)
                    return stage

                def probabilities(t, odd):
                    g = base + t
                    pool.wait_ge(sum_ready, g + 1)
                    inverse = stat[:, odd, 1, :].unsqueeze(2).to_broadcast([P, HEADS, 2 * WINDOW])
                    pool.tensor_tensor(prob[:, odd], prob[:, odd], inverse, ALU.mult).then_inc(prob_ready, 1)

                pipeline(pool, [(3, halo), (2, combine(0)), (2, combine(1)),
                                (3, probabilities)], 6)


def program(nc, hbm, out):
    with ExitStack() as ctx:
        def sb(name, shape, dt=F32):
            return ctx.enter_context(nc.sbuf_tensor(name, shape, dt))

        def sem(name):
            return ctx.enter_context(nc.semaphore(name))

        resid = sb("resid", [P, TOKENS])
        ident = sb("ident", [P, P])
        ones_mean = sb("ones_mean", [P, P])
        eps_col = sb("eps_col", [P, 1])
        loaded = sem("loaded"); consts = sem("consts"); resid_started = sem("resid_started")
        sum_ready = sem("final_sum_ready"); stored = sem("stored")

        with ExitStack() as front:
            def fsb(name, shape, dt=F32):
                return front.enter_context(nc.sbuf_tensor(name, shape, dt))
            xn = fsb("xn", [P, 2, TOKENS])
            win = fsb("win", [P, 2, 2 * D_INNER]); wx = fsb("wx", [P, 2, HALVES, 96 + DT_RANK])
            wdt = fsb("wdt", [DT_RANK, 2, D_INNER]); wout = fsb("wout", [P, 2, HALVES, DIM])
            packed = fsb("packed", [P, 2, PACKED]); ln = fsb("ln", [P, 2])
            sel = fsb("sel", [96, 2 * D_STATE, P], BF16)
            loads = [(xn[:, 0, :], "x"), (win, "win"), (wx, "wx"), (wdt, "wdt"), (wout, "wout"), (packed, "packed"),
                     (ln, "ln"), (ident, "ident"), (sel, "sel")]
            with nc.Block() as block:
                @block.sync
                def _(sp):
                    for dst, name in loads:
                        sp.dma_start(dst[:], hbm[name]).then_inc(loaded, 16)
                    sp.wait_ge(loaded, 16 * len(loads))

                @block.vector
                def _(dve):
                    dve.memset(ones_mean[:, :], 1.0 / DIM).then_inc(consts, 1)
                    dve.memset(eps_col[:, :], EPS).then_inc(consts, 1)
                    dve.wait_ge(consts, 2)
            with ExitStack() as norms:
                u = norms.enter_context(nc.sbuf_tensor("u", [P, TOKENS], F32))
                work = norms.enter_context(nc.sbuf_tensor("work", [P, TOKENS], F32))

                def add_input(dve, cols, steps):
                    steps.wait(dve)
                    dve.tensor_tensor(resid[:, cols], xn[:, 0, cols], u[:, cols], ALU.add).then_inc(resid_started, 1)

                def affine_both_ways(dve, cols, steps):
                    steps.wait(dve)
                    steps.mark(dve.tensor_scalar(xn[:, 0, cols], xn[:, 0, cols], ln[:, 0:1], ln[:, 1:2], ALU.mult, ALU.add))
                    steps.wait(dve)
                    b, off = divmod(cols.start, SEQ)
                    lo = b * SEQ + SEQ - off - BANK
                    dve.tensor_copy(xn[:, 1, lo:lo + BANK][:, ::-1], xn[:, 0, cols]).then_inc(resid_started, 1)

                with ExitStack() as a:
                    layer_norm_block(nc, a, sem, ones_mean, eps_col, xn[:, 0, :], u, work, (1, add_input), "outer")
                with ExitStack() as a:
                    layer_norm_block(nc, a, sem, ones_mean, eps_col, u, xn[:, 0, :], work, (2, affine_both_ways), "inner")
            mamba(nc, xn, resid, (win, wx, wdt, wout, packed, ident, sel[:, 0:D_STATE, :], sel[:, D_STATE:, :]))
        with ExitStack() as back:
            xa = back.enter_context(nc.sbuf_tensor("xa", [P, LEAD + TOKENS], F32))
            xb = back.enter_context(nc.sbuf_tensor("xb", [P, LEAD + TOKENS], F32))

            def clear_lead(dve, cols, steps):
                if cols.start == 0:
                    dve.memset(xa[:, 0:LEAD], 0.0).then_inc(resid_started, 1)

            with ExitStack() as a:
                layer_norm_block(nc, a, sem, ones_mean, eps_col, resid, xa[:, LEAD:], xb[:, LEAD:], (1, clear_lead), "middle")
            with ExitStack() as a:
                transformer(nc, a, ident, xa, xb, hbm)
            with nc.Block() as block:
                @block.vector
                def _(dve):
                    for c in range(CHUNKS):
                        cols = slice(c * BANK, (c + 1) * BANK)
                        dve.tensor_tensor(resid[:, cols], resid[:, cols], xa[:, LEAD + c * BANK:LEAD + (c + 1) * BANK],
                                          ALU.add).then_inc(sum_ready, 1)

                @block.sync
                def _(sp):
                    for c in range(CHUNKS):
                        sp.wait_ge(sum_ready, c + 1)
                        sp.dma_start(out[:, c * BANK:(c + 1) * BANK], resid[:, c * BANK:(c + 1) * BANK]).then_inc(stored, 16)
                    sp.wait_ge(stored, 16 * CHUNKS)


def rope_tables():
    half = np.arange(0, HEAD_DIM, 2, dtype=np.float64)
    angle = np.arange(SEQ)[:, None] * (10000.0 ** (-half / HEAD_DIM))[None]
    power = (np.arange(SEQ) - SEQ // 2) / (WINDOW // 2)
    scale = ((half + 0.4 * HEAD_DIM) / (1.4 * HEAD_DIM))[None] ** power[:, None]
    cos, sin = np.cos(angle), np.sin(angle)
    tables = [np.concatenate(v, axis=1) for v in ((cos * scale,) * 2, (-sin * scale, sin * scale),
                                                  (cos / scale,) * 2, (-sin / scale, sin / scale))]
    t = np.stack(tables).astype(np.float32).reshape(4, SEQ_TILES, P, HEAD_DIM)
    return np.ascontiguousarray(t.transpose(2, 0, 1, 3))


def sight_table():
    i, j = np.arange(P)[:, None] % WINDOW, np.arange(2 * WINDOW)[None]
    seen = np.where(j < WINDOW, j >= i, j - WINDOW <= i)
    table = np.repeat(np.where(seen, 0.0, HIDDEN_ROW)[:, None, :], SEQ_TILES, axis=1)
    table[:WINDOW, 0, :WINDOW] = HIDDEN_ROW
    return table.astype(np.float32)


def host_layout(inputs):
    a = {k: np.asarray(v) for k, v in inputs.items()}
    both = lambda name, f: np.stack([f(a[f"L0_attn_{d}_{name}"]) for d in "fb"], axis=1)
    halves = lambda v: np.moveaxis(v.reshape(HALVES, P, *v.shape[1:]), 0, 1).reshape(P, -1)
    wx = [a[f"L0_attn_{d}_W_x"].T.reshape(HALVES, P, -1).transpose(1, 0, 2) for d in "fb"]
    bcs = [np.concatenate([w[:, :, DT_RANK:]] * 3 + [w[:, :, :DT_RANK]], axis=2) for w in wx]
    packed = [np.concatenate([halves(a[f"L0_attn_{d}_{n}"]) for n in ("W_conv", "b_conv", "b_dt", "A_log", "D")], axis=1)
              for d in "fb"]
    row, state = np.arange(96)[:, None] % 32, np.arange(32)[None]
    wqkv = a["L0_ffn_Wqkv"]
    w2 = np.zeros((DEPTH, P, 3, DIM), np.float32)
    lp = np.zeros((DEPTH, P, LAYER_PACKED), np.float32)
    lp[:, :, LN_G], lp[:, :, LN_B], lp[:, :, OUT_B] = a["L0_ffn_ln_g"], a["L0_ffn_ln_b"], a["L0_ffn_b2"]
    for k, (lo, m) in enumerate(HIDDEN_PARTS):
        w2[:, :m, k] = a["L0_ffn_W2"][:, lo:lo + m]
        lp[:, :m, A_B + k] = a["L0_ffn_b1"][:, lo:lo + m]
        lp[:, :m, GATE_B + k] = a["L0_ffn_b1"][:, HIDDEN + lo:HIDDEN + lo + m]
    return {
        "x": np.ascontiguousarray(a["L0_attn_x"].reshape(TOKENS, DIM).T),
        "win": np.ascontiguousarray(both("W_in", lambda w: w.T)),
        "wx": np.ascontiguousarray(np.stack(bcs, axis=1)),
        "wdt": np.ascontiguousarray(both("W_dt", lambda w: w.T)),
        "wout": np.ascontiguousarray(both("W_out", lambda w: w.T.reshape(HALVES, P, DIM).transpose(1, 0, 2))),
        "packed": np.ascontiguousarray(np.stack(packed, axis=1)),
        "ln": np.ascontiguousarray(np.stack([a["L0_attn_ln_w"], a["L0_attn_ln_b"]], axis=1)),
        "ident": np.eye(P, dtype=np.float32),
        "sel": np.ascontiguousarray(np.broadcast_to((row == state)[:, :, None], (96, 32, P))).astype(mybir.dt.np(BF16)),
        "rope": rope_tables(),
        "sight": sight_table(),
        "keep": np.ascontiguousarray(np.broadcast_to((np.arange(SEQ_TILES) > 0).astype(np.float32), (P, SEQ_TILES))),
        "w_qk": np.ascontiguousarray(wqkv[:, :, :2 * INNER]),
        "w_v": np.ascontiguousarray(wqkv[:, :, 2 * INNER:].transpose(0, 2, 1).reshape(DEPTH, PAIRS, P, DIM).transpose(0, 2, 1, 3)),
        "w_o": np.ascontiguousarray(a["L0_ffn_Wo"].reshape(DEPTH, PAIRS, P, DIM).transpose(0, 2, 1, 3)),
        "w1": a["L0_ffn_W1"],
        "w2": w2,
        "lp": lp,
        "head_scale": np.stack([a["L0_ffn_q_scale"], a["L0_ffn_k_scale"]], axis=1),
    }


def kernel(**inputs):
    import concourse.bacc as bacc
    from concourse.bass_utils import run_bass_kernel_spmd

    nc = bacc.Bacc("TRN2", target_bir_lowering=False, num_devices=1)
    arrays = {f"{name}_hbm": array for name, array in host_layout(inputs).items()}
    hbm = {name[:-4]: nc.dram_tensor(name, array.shape, mybir.dt.from_np(array.dtype), kind="ExternalInput").ap()
           for name, array in arrays.items()}
    out = nc.dram_tensor("out_hbm", (P, TOKENS), F32, kind="ExternalOutput").ap()
    program(nc, hbm, out)
    result = run_bass_kernel_spmd(nc, [arrays], core_ids=[0]).results[0]["out_hbm"]
    return np.ascontiguousarray(np.asarray(result).T).reshape(BATCH, SEQ, DIM)
```

```python
from contextlib import ExitStack

import numpy as np

import concourse.bass as bass
from concourse import mybir

F32 = mybir.dt.float32
F32R = mybir.dt.float32r
BF16 = mybir.dt.bfloat16
ALU = mybir.AluOpType
ACT = mybir.ActivationFunctionType
AX_X = mybir.AxisListType.X

P = 128
BANK = 512
BATCH, SEQ, DIM = 4, 1024, 128
TOKENS = BATCH * SEQ
HALF_BANKS = SEQ // BANK
D_INNER, D_STATE, D_CONV, DT_RANK = 256, 16, 4, 8
HALVES = D_INNER // P
EPS = 1e-5

CONV_W, CONV_B, DT_B, A_LOG, D_SKIP = 0, 8, 10, 12, 44
PACKED = 46


class Steps:

    def __init__(self, sem, base=0):
        self.sem, self.base, self.count = sem, base, 0

    def mark(self, instruction):
        instruction.then_inc(self.sem, 1)
        self.count += 1

    def wait(self, eng):
        eng.wait_ge(self.sem, self.base + self.count)


def layer_norm_block(nc, ctx, sem, ones_mean, eps_col, src, out, work, finish, name):
    chunks = TOKENS // BANK
    mean_ready = sem(name + "_mean_ready")
    centred = sem(name + "_centred")
    squared = sem(name + "_squared")
    var_ready = sem(name + "_var_ready")
    log_done = sem(name + "_log_done")
    rstd_ready = sem(name + "_rstd_ready")
    dve_done = sem(name + "_dve_done")
    stats = ctx.enter_context(nc.psum_tensor(name + "_stats", [P, chunks, BANK], F32))
    with nc.Block() as block:
        @block.tensor
        def _(pe):
            for c in range(chunks):
                pe.matmul(stats[:, c, :], ones_mean[:, :], src[:, c * BANK:(c + 1) * BANK],
                          start=True, stop=True).then_inc(mean_ready, 1)
            for c in range(chunks):
                pe.wait_ge(squared, c + 1)
                pe.matmul(stats[:, c, :], ones_mean[:, :], work[:, c * BANK:(c + 1) * BANK],
                          start=True, stop=True).then_inc(var_ready, 1)

        @block.vector
        def _(dve):
            for c in range(chunks):
                cols = slice(c * BANK, (c + 1) * BANK)
                dve.wait_ge(mean_ready, c + 1)
                dve.tensor_tensor(out[:, cols], src[:, cols], stats[:, c, :],
                                  ALU.subtract).then_inc(centred, 1)
            for c in range(chunks):
                cols = slice(c * BANK, (c + 1) * BANK)
                steps = Steps(dve_done, c * finish[0])
                dve.wait_ge(rstd_ready, c + 1)
                steps.mark(dve.tensor_tensor(out[:, cols], out[:, cols], work[:, cols], ALU.mult))
                finish[1](dve, cols, steps)

        @block.scalar
        def _(act):
            for c in range(chunks):
                cols = slice(c * BANK, (c + 1) * BANK)
                act.wait_ge(centred, c + 1)
                act.activation(work[:, cols], out[:, cols], ACT.Square).then_inc(squared, 1)
            for c in range(chunks):
                cols = slice(c * BANK, (c + 1) * BANK)
                act.wait_ge(var_ready, c + 1)
                act.activation(work[:, cols], stats[:, c, :], ACT.Ln, bias=eps_col[:, 0:1]).then_inc(log_done, 1)
                act.wait_ge(log_done, c + 1)
                act.activation(work[:, cols], work[:, cols], ACT.Exp, scale=-0.5).then_inc(rstd_ready, 1)


def mamba(nc, xn, resid, weights):
    win, wx, wdt, wout, packed, ident, sel_b, sel_c = weights
    with ExitStack() as ctx:
        def sb(name, shape, dt=F32):
            return ctx.enter_context(nc.sbuf_tensor(name, shape, dt))

        def sem(name):
            return ctx.enter_context(nc.semaphore(name))

        UNITS = D_STATE * HALVES
        PAD = D_CONV - 1
        neg_a = sb("neg_a", [P, 2, HALVES * D_STATE])
        xp = sb("xp", [P, HALVES, PAD + SEQ])
        xc = sb("xc", [P, HALVES, SEQ])
        zs = sb("zs", [P, HALVES, SEQ])
        dt = sb("dt", [P, HALVES, SEQ])
        dtx = sb("dtx", [P, HALVES, SEQ])
        expd = sb("expd", [P, SEQ])
        relu = sb("relu", [P, SEQ])
        dt_raw = sb("dt_raw", [DT_RANK, SEQ])
        bc = sb("bc", [96, SEQ], BF16)
        bc_rest = sb("bc_rest", [96, SEQ])
        bc_mid = sb("bc_mid", [96, SEQ], BF16)
        decay = sb("decay", [P, HALVES, 2, SEQ])
        drive = sb("drive", [P, 2, SEQ])
        state = sb("state", [P, 3, SEQ])
        c_row = sb("c_row", [P, 2, SEQ])
        read = sb("read", [P, 2, SEQ])
        gated = sb("gated", [P, HALVES, SEQ])
        ps = ctx.enter_context(nc.psum_tensor("mamba_ps", [P, 8, BANK], F32))
        b_ps, c_ps = ps[:, 0:2, :], ps[:, 2:4, :]

        a_exp = sem("a_exp"); a_ready = sem("a_ready"); pad_ready = sem("pad_ready")
        xz_ready = sem("xz_ready"); xp_ready = sem("xp_ready"); zs_ready = sem("zs_ready")
        conv_ready = sem("conv_ready"); conv_step = sem("conv_step"); xc_ready = sem("xc_ready")
        xdbl_ready = sem("xdbl_ready"); dt_raw_ready = sem("dt_raw_ready"); bc_high = sem("bc_high")
        split_step = sem("split_step"); bc_ready = sem("bc_ready"); v_ready = sem("v_ready")
        soft_step = sem("soft_step"); soft_ready = sem("soft_ready"); relu_ready = sem("relu_ready")
        dt_done = sem("dt_done"); dt_ready = sem("dt_ready")
        b_ready = sem("b_ready"); c_ready = sem("c_ready"); c_copied = sem("c_copied")
        decay_ready = sem("decay_ready"); drive_ready = sem("drive_ready"); state_ready = sem("state_ready")
        read_ready = sem("read_ready"); summed = sem("summed"); skip_added = sem("skip_added")
        gated_ready = sem("gated_ready"); out_ready = sem("out_ready"); resid_done = sem("resid_done")

        def passes(eng):
            for direction in range(2):
                with eng.Fori(0, BATCH) as b:
                    yield direction, b, b + direction * BATCH

        with nc.Block() as block:
            @block.tensor
            def _(pe):
                for direction, b, s in passes(pe):
                    for m in range(2 * HALVES):
                        for c in range(HALF_BANKS):
                            last = pe.matmul(ps[:, 2 * m + c, :], win[:, direction, m * P:(m + 1) * P],
                                             xn[:, direction, bass.ds(b * SEQ + c * BANK, BANK)],
                                             start=True, stop=True)
                        last.then_inc(xz_ready, 1)
                    pe.wait_ge(xp_ready, HALVES * s + HALVES)
                    pe.wait_ge(xc_ready, HALVES * s + HALVES)
                    for c in range(HALF_BANKS):
                        for h in range(HALVES):
                            pe.matmul(ps[0:96, c, :], wx[:, direction, h, 0:96], xc[:, h, c * BANK:(c + 1) * BANK],
                                      start=h == 0, stop=h == HALVES - 1)
                        for h in range(HALVES):
                            last = pe.matmul(ps[0:DT_RANK, 2 + c, :], wx[:, direction, h, 96:96 + DT_RANK],
                                             xc[:, h, c * BANK:(c + 1) * BANK], start=h == 0, stop=h == HALVES - 1)
                    last.then_inc(xdbl_ready, 1)
                    pe.wait_ge(zs_ready, HALVES * s + HALVES)
                    pe.wait_ge(dt_raw_ready, s + 1)
                    for h in range(HALVES):
                        for c in range(HALF_BANKS):
                            last = pe.matmul(ps[:, 4 + 2 * h + c, :], wdt[:, direction, h * P:(h + 1) * P],
                                             dt_raw[:, c * BANK:(c + 1) * BANK], start=True, stop=True)
                        last.then_inc(v_ready, 1)
                    pe.wait_ge(bc_ready, s + 1)
                    pe.wait_ge(dt_ready, HALVES * s + HALVES)

                    def add_reads(n):
                        for h in range(HALVES):
                            pe.wait_ge(read_ready, UNITS * s + 2 * n + h + 1)
                            for c in range(HALF_BANKS):
                                last = pe.matmul(ps[:, 4 + 2 * h + c, :], ident[:, :],
                                                 read[:, h, c * BANK:(c + 1) * BANK],
                                                 start=n == 0, stop=n == D_STATE - 1)
                            last.then_inc(summed, 1)

                    for n in range(D_STATE):
                        if n:
                            pe.wait_ge(drive_ready, UNITS * s + 2 * n)
                        for c in range(HALF_BANKS):
                            last = pe.matmul(b_ps[:, c, :], sel_b[:, n, :], bc[:, c * BANK:(c + 1) * BANK],
                                             start=True, stop=True)
                        last.then_inc(b_ready, 1)
                        if n:
                            pe.wait_ge(c_copied, D_STATE * s + n)
                        for c in range(HALF_BANKS):
                            last = pe.matmul(c_ps[:, c, :], sel_c[:, n, :], bc[:, c * BANK:(c + 1) * BANK],
                                             start=True, stop=True)
                        last.then_inc(c_ready, 1)
                        if n:
                            add_reads(n - 1)
                    add_reads(D_STATE - 1)
                    pe.wait_ge(drive_ready, UNITS * s + UNITS)
                    for h in range(HALVES):
                        pe.wait_ge(gated_ready, HALVES * s + h + 1)
                        for c in range(HALF_BANKS):
                            last = pe.matmul(ps[:, c, :], wout[:, direction, h, :], gated[:, h, c * BANK:(c + 1) * BANK],
                                             start=h == 0, stop=h == HALVES - 1)
                    last.then_inc(out_ready, 1)
                    pe.wait_ge(resid_done, s + 1)

            @block.scalar
            def _(act):
                for direction in range(2):
                    act.activation(neg_a[:, direction, :], packed[:, direction, A_LOG:A_LOG + 32], ACT.Exp).then_inc(a_exp, 1)
                act.wait_ge(a_ready, 1)
                for direction, b, s in passes(act):
                    for h in range(HALVES):
                        act.wait_ge(xz_ready, 4 * s + h + 1)
                        act.copy(xp[:, h, PAD:], ps[:, 2 * h:2 * h + 2, :]).then_inc(xp_ready, 1)
                    for h in range(HALVES):
                        act.wait_ge(xz_ready, 4 * s + HALVES + h + 1)
                        act.activation(zs[:, h, :], ps[:, 4 + 2 * h:6 + 2 * h, :], ACT.Silu).then_inc(zs_ready, 1)
                    for h in range(HALVES):
                        act.wait_ge(conv_ready, HALVES * s + h + 1)
                        act.activation(xc[:, h, :], dtx[:, h, :], ACT.Silu,
                                       bias=packed[:, direction, CONV_B + h:CONV_B + h + 1]).then_inc(xc_ready, 1)
                    act.wait_ge(xdbl_ready, s + 1)
                    act.copy(dt_raw[:, :], ps[0:DT_RANK, 2:4, :]).then_inc(dt_raw_ready, 1)
                    act.copy(bc[:, :], ps[0:96, 0:2, :]).then_inc(bc_high, 1)
                    soft = Steps(soft_step, 4 * s)
                    for h in range(HALVES):
                        act.wait_ge(v_ready, HALVES * s + h + 1)
                        soft.mark(act.activation(expd[:, :], ps[:, 4 + 2 * h:6 + 2 * h, :], ACT.Abs,
                                                 bias=packed[:, direction, DT_B + h:DT_B + h + 1]))
                        soft.wait(act)
                        soft.mark(act.activation(expd[:, :], expd[:, :], ACT.Exp, scale=-1.0))
                        soft.wait(act)
                        act.activation(dt[:, h, :], expd[:, :], ACT.Ln, bias=1.0).then_inc(soft_ready, 1)
                        act.wait_ge(soft_ready, HALVES * s + h + 1)
                    act.wait_ge(dt_ready, HALVES * s + HALVES)
                    for n in range(D_STATE):
                        act.wait_ge(c_ready, D_STATE * s + n + 1)
                        if n > 1:
                            act.wait_ge(read_ready, UNITS * s + 2 * (n - 1))
                        act.copy(c_row[:, n % 2, :], c_ps).then_inc(c_copied, 1)
                        for h in range(HALVES):
                            if n > 1:
                                act.wait_ge(state_ready, UNITS * s + 2 * (n - 2) + h + 1)
                            act.activation(decay[:, h, n % 2, :], dt[:, h, :], ACT.Exp,
                                           scale=neg_a[:, direction, h * D_STATE + n:h * D_STATE + n + 1]
                                           ).then_inc(decay_ready, 1)

            @block.vector
            def _(dve):
                dve.memset(xp[:, :, 0:PAD], 0.0).then_inc(pad_ready, 1)
                dve.wait_ge(a_exp, 2)
                dve.tensor_scalar(neg_a[:, :, :], neg_a[:, :, :], -1.0, None, ALU.mult).then_inc(a_ready, 1)
                dve.wait_ge(pad_ready, 1)
                for direction, b, s in passes(dve):
                    conv = Steps(conv_step, HALVES * (D_CONV - 1) * s)
                    for h in range(HALVES):
                        dve.wait_ge(xp_ready, HALVES * s + h + 1)
                        for k in range(D_CONV):
                            w = packed[:, direction, CONV_W + h * D_CONV + k:CONV_W + h * D_CONV + k + 1]
                            tap = xp[:, h, k:k + SEQ]
                            if k == 0:
                                conv.mark(dve.tensor_scalar(dtx[:, h, :], tap, w, None, ALU.mult))
                                conv.wait(dve)
                                continue
                            ins = dve.scalar_tensor_tensor(out=dtx[:, h, :], in0=tap, scalar=w, in1=dtx[:, h, :],
                                                           op0=ALU.mult, op1=ALU.add)
                            if k < D_CONV - 1:
                                conv.mark(ins)
                                conv.wait(dve)
                            else:
                                ins.then_inc(conv_ready, 1)
                    split = Steps(split_step, 4 * s)
                    dve.wait_ge(bc_high, s + 1)
                    split.mark(dve.tensor_tensor(bc_rest[:, :], ps[0:96, 0:2, :], bc[:, :], ALU.subtract))
                    split.wait(dve)
                    split.mark(dve.tensor_copy(bc[32:64, :], bc_rest[32:64, :]))
                    split.mark(dve.tensor_copy(bc_mid[64:96, :], bc_rest[64:96, :]))
                    split.wait(dve)
                    split.mark(dve.tensor_tensor(bc_rest[64:96, :], bc_rest[64:96, :], bc_mid[64:96, :], ALU.subtract))
                    split.wait(dve)
                    dve.tensor_copy(bc[64:96, :], bc_rest[64:96, :]).then_inc(bc_ready, 1)
                    for h in range(HALVES):
                        dve.wait_ge(v_ready, HALVES * s + h + 1)
                        if h:
                            dve.wait_ge(dt_done, HALVES * s + h)
                        dve.wait_ge(soft_step, 4 * s + 2 * h + 1)
                        dve.tensor_scalar(relu[:, :], ps[:, 4 + 2 * h:6 + 2 * h, :],
                                          packed[:, direction, DT_B + h:DT_B + h + 1], 0.0,
                                          ALU.add, ALU.max).then_inc(relu_ready, 1)
                        dve.wait_ge(relu_ready, HALVES * s + h + 1)
                        dve.wait_ge(soft_ready, HALVES * s + h + 1)
                        dve.tensor_tensor(dt[:, h, :], dt[:, h, :], relu[:, :], ALU.add).then_inc(dt_done, 1)
                        dve.wait_ge(dt_done, HALVES * s + h + 1)
                        dve.wait_ge(xc_ready, HALVES * s + h + 1)
                        dve.tensor_tensor(dtx[:, h, :], dt[:, h, :], xc[:, h, :], ALU.mult).then_inc(dt_ready, 1)
                    dve.wait_ge(dt_ready, HALVES * s + HALVES)

                    def make_drive(u):
                        dve.wait_ge(b_ready, D_STATE * s + u // 2 + 1)
                        if u > 1:
                            dve.wait_ge(state_ready, UNITS * s + u - 1)
                        dve.tensor_tensor(drive[:, u % 2, :], dtx[:, u % 2, :], b_ps, ALU.mult).then_inc(drive_ready, 1)

                    make_drive(0)
                    for u in range(UNITS):
                        if u + 1 < UNITS:
                            make_drive(u + 1)
                        dve.wait_ge(decay_ready, UNITS * s + u + 1)
                        dve.wait_ge(drive_ready, UNITS * s + u + 1)
                        if u > 2:
                            dve.wait_ge(read_ready, UNITS * s + u - 2)
                        dve.tensor_tensor_scan(state[:, u % 3, :], decay[:, u % 2, (u // 2) % 2, :], drive[:, u % 2, :],
                                               0.0, ALU.mult, ALU.add).then_inc(state_ready, 1)
                    for h in range(HALVES):
                        dve.wait_ge(summed, UNITS * s + UNITS - 1 + h)
                        dve.scalar_tensor_tensor(out=gated[:, h, :], in0=xc[:, h, :],
                                                 scalar=packed[:, direction, D_SKIP + h:D_SKIP + h + 1],
                                                 in1=ps[:, 4 + 2 * h:6 + 2 * h, :], op0=ALU.mult,
                                                 op1=ALU.add).then_inc(skip_added, 1)
                        dve.wait_ge(skip_added, HALVES * s + h + 1)
                        dve.wait_ge(zs_ready, HALVES * s + h + 1)
                        dve.tensor_tensor(gated[:, h, :], gated[:, h, :], zs[:, h, :], ALU.mult).then_inc(gated_ready, 1)
                    dve.wait_ge(out_ready, s + 1)
                    r = resid[:, bass.ds(b * SEQ, SEQ)]
                    y = ps[:, 0:2, :].rearrange("p a b -> p (a b)")
                    if direction:
                        y = y[:, ::-1]
                    dve.scalar_tensor_tensor(out=r, in0=y, scalar=0.5, in1=r,
                                             op0=ALU.mult, op1=ALU.add).then_inc(resid_done, 1)
                    dve.wait_ge(resid_done, s + 1)

            @block.gpsimd
            def _(pool):
                for direction, b, s in passes(pool):
                    for u in range(UNITS):
                        pool.wait_ge(state_ready, UNITS * s + u + 1)
                        pool.wait_ge(c_copied, D_STATE * s + u // 2 + 1)
                        if u > 1:
                            pool.wait_ge(summed, UNITS * s + u - 1)
                        pool.tensor_tensor(read[:, u % 2, :], state[:, u % 3, :], c_row[:, (u // 2) % 2, :],
                                           ALU.mult).then_inc(read_ready, 1)


DEPTH, HEADS, HEAD_DIM, WINDOW = 6, 16, 64, 32
PAIRS = HEADS // 2
INNER = HEADS * HEAD_DIM
HIDDEN = int(DIM * 4 * 2 / 3)
HIDDEN_PARTS = [(0, P), (P, P), (2 * P, HIDDEN - 2 * P)]
QK_SCALE = 8.0
TILES = TOKENS // P
SEQ_TILES = SEQ // P
CHUNKS = TOKENS // BANK
SEQ_CHUNKS = SEQ // BANK
WINDOWS = P // WINDOW
LEAD = 64
KEYS = P + WINDOW
HIDDEN_ROW = -1e30
NORM_SHIFT = 20
LN_G, LN_B, OUT_B, A_B, GATE_B = 0, 1, 2, 3, 6
LAYER_PACKED = 9


PE_ORDER = [(0, "project1"), (2, "head_turn1"), (0, "project0"), (2, "head_turn0"), (5, "mix1"), (0, "project3"),
            (4, "prob_turn1"), (4, "prob_turn0"), (0, "project2"), (3, "row_turn"), (2, "head_turn3"), (4, "mix0"),
            (2, "head_turn2"), (5, "output"), (2, "score")]
ACT_ORDER = [(1, "keep1"), (3, "copy_heads0"), (1, "keep0"), (3, "copy_heads1"), (6, "copy_mixed1"), (5, "copy_probs1"),
             (5, "copy_probs0"), (4, "copy_rows"), (3, "copy_heads3"), (3, "copy_heads2"), (2, "inverse_norm"),
             (4, "exponent"), (1, "keep3"), (1, "keep2"), (5, "copy_mixed0")]
DVE_ORDER = [(2, "cosines0"), (2, "guard"), (4, "subtract_max"), (2, "sines1"), (0, "shift_tile"), (2, "cosines1"),
             (4, "sum_probs"), (1, "squares0"), (4, "invert_sum"), (6, "add_output"), (3, "shift_windows"), (1, "sines0"),
             (3, "mask_scores"), (1, "squares1"), (3, "find_max")]
POOL_ORDER = [(1, "rotated0"), (1, "normed0"), (1, "rotated1"), (3, "normalise_probs"), (1, "normed1"), (1, "halo")]
MAX_LAG = 6
TURN_READERS = {"head_turn0": "copy_heads0", "head_turn1": "copy_heads1", "head_turn2": "copy_heads2",
                "head_turn3": "copy_heads3", "row_turn": "copy_rows", "prob_turn0": "copy_probs0",
                "prob_turn1": "copy_probs1", "output": "add_output"}
TURNS = [(lag, name) for lag, name in PE_ORDER if name in TURN_READERS]
TURN_BANK = {name: k % 2 for k, (_, name) in enumerate(TURNS)}


def pipeline(eng, order, stages):
    def step(i, odd):
        for lag, name in order:
            if not isinstance(i, int) or 0 <= i - lag < TILES:
                stages[name](i - lag, (odd - lag) % 2)

    warm = (MAX_LAG + 3) // 2 * 2
    for i in range(warm):
        step(i, i % 2)
    with eng.Fori(warm // 2, TILES // 2) as two:
        step(2 * two, 0)
        step(2 * two + 1, 1)
    for i in range(TILES, TILES + MAX_LAG):
        step(i, i % 2)


def later(tile, n):
    return not isinstance(tile, int) or tile >= n


def last_turn(name, tile):
    k = [n for _, n in TURNS].index(name)
    lag = TURNS[k][0]
    step = 0
    while True:
        k -= 2
        if k < 0:
            k, step = k + len(TURNS), step - 1
        used = tile + (lag + step - TURNS[k][0])
        if not isinstance(tile, int) or 0 <= used < TILES:
            return TURNS[k][1], used
        if tile + lag + step < 0:
            return None, None


def transformer(nc, ctx, ident, xa, xb, hbm):
    def sb(name, shape, dt=F32):
        return ctx.enter_context(nc.sbuf_tensor(name, shape, dt))

    def sem(name):
        return ctx.enter_context(nc.semaphore(name))

    w_qk = sb("w_qk", [P, 2, 2 * INNER], F32R)
    w_vo = sb("w_vo", [P, HEADS, P])
    w1 = sb("w1", [P, 2 * HIDDEN])
    w2 = sb("w2", [P, 3, P])
    lp = sb("lp", [P, LAYER_PACKED])
    head_scale = sb("head_scale", [P, 2, HEAD_DIM])
    rope = sb("rope", [P, 4, SEQ_TILES, HEAD_DIM])
    rope_l = sb("rope_l", [P, 4, SEQ_TILES, HEAD_DIM])
    sight = sb("sight", [P, SEQ_TILES, 2 * WINDOW])
    keep = sb("keep", [P, SEQ_TILES])
    exp_shift = sb("exp_shift", [P, 1])
    ones_mean = sb("ones_mean2", [P, P])
    eps_col = sb("eps_col2", [P, 1])

    xs = sb("xs", [P, 2, P])
    xs_parts = sb("xs_parts", [P, 2, 2, P], F32R)
    xw = sb("xw", [P, 2, WINDOWS, 2 * 2 * WINDOW])
    x_rows = sb("x_rows", [P, 2, WINDOWS, P])
    qk = sb("qk", [P, 2, 2 * INNER])
    sq = sb("sq", [P, 2, 2 * INNER])
    ssq = sb("ssq", [P, 2, 2 * HEADS])
    rnorm = sb("rnorm", [P, 2, 2 * HEADS])
    q_t = sb("q_t", [P, PAIRS, P])
    k_t = sb("k_t", [P, 2, PAIRS, 2, KEYS])
    prob = sb("prob", [P, 2, HEADS, 2 * WINDOW])
    stat = sb("stat", [P, 2, 2, HEADS])
    prob_t = sb("prob_t", [P, PAIRS, P])
    mixed = sb("mixed", [P, 2, PAIRS, 2, P])
    ps = ctx.enter_context(nc.psum_tensor("ps", [P, 8, BANK], F32))
    A, T, S, G = 0, 2, 4, 6

    w_in = mixed[:, 0].rearrange("p a h n -> p (a h n)")
    w_v = mixed[:, 1, 0:4].rearrange("p a h n -> p (a h) n")
    w_o = mixed[:, 1, 4:8].rearrange("p a h n -> p (a h) n")

    done = {name: sem(name) for order in (PE_ORDER, ACT_ORDER, DVE_ORDER, POOL_ORDER) for _, name in order}
    names = """wqk_loaded wvo_loaded wff_loaded scale_loaded const_loaded const_set vo_ready vo_copied rope_ready
        wqk_high wqk_low xs_low xs_high xs_whole xs_rounded xw_low xw_high rs_log
        fx_low fx_high fx_ready mean_ready centred squared var_ready log_ready rstd_ready scaled fn_ready
        gate_ready gelu_ready a_ready hidden_ready fo_ready x_written""".split()
    z = {n: sem(n) for n in names}
    (wqk_loaded, wvo_loaded, wff_loaded, scale_loaded, const_loaded, const_set, vo_ready, vo_copied, rope_ready,
     wqk_high, wqk_low, xs_low, xs_high, xs_whole, xs_rounded, xw_low, xw_high, rs_log,
     fx_low, fx_high, fx_ready, mean_ready, centred, squared, var_ready, log_ready, rstd_ready, scaled, fn_ready,
     gate_ready, gelu_ready, a_ready, hidden_ready, fo_ready, x_written) = [z[n] for n in names]

    def ff(odd):
        return (qk[:, odd, 0:BANK], qk[:, odd, BANK:2 * BANK], qk[:, odd, 2 * BANK:3 * BANK],
                [sq[0:m, odd, k * BANK:(k + 1) * BANK] for k, (_, m) in enumerate(HIDDEN_PARTS)])
    MEAN, VAR, GATE, VALUE = 0, 1, 2, 5

    def ff_pipeline(eng, stages):
        def step(c, odd):
            for ahead, stage in stages:
                if not isinstance(c, int) or 0 <= c + ahead < CHUNKS:
                    stage(c + ahead, (odd + ahead) % 2)
        step(-1, 1)
        step(0, 0)
        step(1, 1)
        with eng.Fori(1, CHUNKS // 2 - 1) as two:
            step(2 * two, 0)
            step(2 * two + 1, 1)
        step(CHUNKS - 2, 0)
        step(CHUNKS - 1, 1)

    def shift_in(eng, dst, src, first, tokens_before, tile, low, high, ready, n, start):
        width = dst.shape[1]
        eng.tensor_copy(dst[0:64, :], src[0:64, bass.ds(first, width)]).then_inc(low, 1)
        ins = eng.tensor_copy(dst[64:128, :], src[64:128, bass.ds(first - 1, width)])
        if not start:
            ins.then_inc(ready, 1)
            return
        ins.then_inc(high, 1)
        eng.wait_ge(high, n)
        col = dst[64:128, tokens_before:tokens_before + 1]
        eng.tensor_tensor(col, col, keep[64:128, bass.ds(tile % SEQ_TILES, 1)], ALU.mult).then_inc(ready, 1)

    def after(eng, base, *producers):
        for name, tile in producers:
            eng.wait_ge(done[name], base + tile + 1)

    def indexed(name, f, n):
        return {f"{name}{i}": f(i) for i in range(n)}

    with nc.Block() as block:
        @block.sync
        def _(sp):
            consts = [(rope, hbm["rope"]), (sight, hbm["sight"]), (keep, hbm["keep"])]
            for dst, src in consts:
                sp.dma_start(dst[:], src).then_inc(const_loaded, 16)
            for l in range(DEPTH):
                if l:
                    sp.wait_ge(rope_ready, 4 * l)
                sp.dma_start(head_scale[:, :, :], hbm["head_scale"][l].partition_broadcast(P)
                             ).then_inc(scale_loaded, 16)
                if l:
                    sp.wait_ge(done["output"], TILES * l)
                sp.dma_start(w_in, hbm["w_qk"][l]).then_inc(wqk_loaded, 16)
                sp.dma_start(w_v, hbm["w_v"][l]).then_inc(wvo_loaded, 16)
                sp.dma_start(w_o, hbm["w_o"][l]).then_inc(wvo_loaded, 16)
                if l:
                    sp.wait_ge(x_written, CHUNKS * l)
                sp.dma_start(w1[:, :], hbm["w1"][l]).then_inc(wff_loaded, 16)
                sp.dma_start(w2[:, :, :], hbm["w2"][l]).then_inc(wff_loaded, 16)
                sp.dma_start(lp[:, :], hbm["lp"][l]).then_inc(wff_loaded, 16)

        @block.tensor
        def _(pe):
            pe.wait_ge(const_set, 6)
            with pe.Fori(0, DEPTH) as l:
                base = l * TILES
                pe.wait_ge(wvo_loaded, 32 * l + 32)
                for h in range(HEADS):
                    rows = slice(64 * (h % 2), 64 * (h % 2) + 64)
                    last = pe.matmul(ps[:, 2 * (h % 2) + h // 8, (h // 2 % 4) * P:(h // 2 % 4 + 1) * P],
                                     w_v[rows, h // 2, :], w_o[rows, h // 2, :], start=True, stop=True)
                last.then_inc(vo_ready, 1)
                pe.wait_ge(vo_copied, 4 * l + 4)

                def turn_bank_free(name, t):
                    user, tile = last_turn(name, t)
                    if user:
                        after(pe, base, (TURN_READERS[user], tile))
                    return T + TURN_BANK[name]

                def project(c):
                    def stage(t, odd):
                        after(pe, base, ("shift_tile", t))
                        if isinstance(t, int) and t == 0:
                            pe.wait_ge(wqk_low, l + 1)
                        if c < 2:
                            if later(t, 1):
                                after(pe, base, (f"keep{c + 2}", t - 1))
                        else:
                            after(pe, base, (f"keep{c - 2}", t))
                        for k, (xpart, wpart) in enumerate([(0, 0), (1, 0), (0, 1)]):
                            last = pe.matmul(ps[:, A + c % 2, :], xs_parts[:, odd, xpart, :],
                                             w_qk[:, wpart, c * BANK:(c + 1) * BANK], start=k == 0, stop=k == 2)
                        last.then_inc(done[f"project{c}"], 1)
                    return stage

                def head_turn(c):
                    def stage(t, odd):
                        after(pe, base, (f"normed{c // 2}", t))
                        bank = turn_bank_free(f"head_turn{c}", t)
                        for j in range(4):
                            col = c * BANK + j * P
                            last = pe.transpose(ps[:, bank, j * P:(j + 1) * P], qk[:, odd, col:col + P], ident[:, :])
                        last.then_inc(done[f"head_turn{c}"], 1)
                    return stage

                def row_turn(t, odd):
                    after(pe, base, ("shift_windows", t))
                    bank = turn_bank_free("row_turn", t)
                    for w in range(WINDOWS):
                        last = pe.transpose(ps[:, bank, w * P:(w + 1) * P], xw[:, odd, w, :], ident[:, :])
                    last.then_inc(done["row_turn"], 1)

                def score(t, odd):
                    after(pe, base, ("copy_heads0", t), ("copy_heads1", t), ("copy_heads2", t), ("copy_heads3", t), ("halo", t))
                    if later(t, 1):
                        after(pe, base, ("mask_scores", t - 1))
                    for a in range(PAIRS):
                        for w in range(WINDOWS):
                            last = pe.matmul(ps[w * WINDOW:(w + 1) * WINDOW, S + a // 4, (a % 4) * P:(a % 4 + 1) * P],
                                             q_t[:, a, w * WINDOW:(w + 1) * WINDOW],
                                             k_t[:, odd, a, :, w * WINDOW:(w + 2) * WINDOW], start=True, stop=True,
                                             skip_group_check=True)
                    last.then_inc(done["score"], 1)

                def prob_turn(c):
                    def stage(t, odd):
                        after(pe, base, ("normalise_probs", t))
                        bank = turn_bank_free(f"prob_turn{c}", t)
                        for j in range(4):
                            a = 4 * c + j
                            last = pe.transpose(ps[:, bank, j * P:(j + 1) * P],
                                                prob[:, odd, 2 * a:2 * a + 2, :].rearrange("p h k -> p (h k)"), ident[:, :])
                        last.then_inc(done[f"prob_turn{c}"], 1)
                    return stage

                def mix(r):
                    def stage(t, odd):
                        after(pe, base, ("copy_rows", t), ("copy_probs0", t), ("copy_probs1", t))
                        if r:
                            after(pe, base, ("copy_mixed0", t))
                        elif later(t, 1):
                            after(pe, base, ("copy_mixed1", t - 1))
                        for w in (2 * r, 2 * r + 1):
                            for h in range(2):
                                rows = slice(64 * h, 64 * h + 64)
                                last = pe.matmul(ps[:, G + h, (w % 2) * 256:(w % 2 + 1) * 256],
                                                 x_rows[rows, odd, w, :], prob_t[rows, :, w * WINDOW:(w + 1) * WINDOW],
                                                 start=True, stop=True, skip_group_check=True)
                        last.then_inc(done[f"mix{r}"], 1)
                    return stage

                def output(t, odd):
                    after(pe, base, ("copy_mixed0", t), ("copy_mixed1", t))
                    bank = turn_bank_free("output", t)
                    for a in range(PAIRS):
                        for h in range(2):
                            last = pe.matmul(ps[:, bank, 0:P], w_vo[:, 2 * a + h, :], mixed[:, odd, a, h, :],
                                             start=a + h == 0, stop=a == PAIRS - 1 and h == 1)
                    last.then_inc(done["output"], 1)

                pipeline(pe, PE_ORDER, {**indexed("project", project, 4), **indexed("head_turn", head_turn, 4),
                                        "row_turn": row_turn, "score": score, **indexed("prob_turn", prob_turn, 2),
                                        **indexed("mix", mix, 2), "output": output})

                def means(c, odd):
                    xf, xc, work, hid = ff(odd)
                    pe.wait_ge(fx_ready, CHUNKS * l + c + 1)
                    if isinstance(c, int) and c == 0:
                        after(pe, base, ("add_output", TILES - 1))
                    if later(c, 2):
                        pe.wait_ge(x_written, CHUNKS * l + c - 1)
                    elif c == 1:
                        pe.wait_ge(centred, CHUNKS * l + 1)
                    pe.matmul(ps[:, MEAN, :], ones_mean[:, :], xf, start=True, stop=True).then_inc(mean_ready, 1)

                def variances(c, odd):
                    xf, xc, work, hid = ff(odd)
                    pe.wait_ge(squared, CHUNKS * l + c + 1)
                    if later(c, 1):
                        pe.wait_ge(log_ready, CHUNKS * l + c)
                    pe.matmul(ps[:, VAR, :], ones_mean[:, :], work, start=True, stop=True).then_inc(var_ready, 1)

                def hidden(kind):
                    def stage(c, odd):
                        xf, xc, work, hid = ff(odd)
                        if isinstance(c, int) and c == 0:
                            pe.wait_ge(wff_loaded, 48 * l + 48)
                        pe.wait_ge(fn_ready, CHUNKS * l + c + 1)
                        bank, ready, taken, first = ((GATE, gate_ready, gelu_ready, HIDDEN) if kind else
                                                     (VALUE, a_ready, hidden_ready, 0))
                        for k, (lo, m) in enumerate(HIDDEN_PARTS):
                            if later(c, 1):
                                pe.wait_ge(taken, 3 * (CHUNKS * l + c) - 2 + k)
                            pe.matmul(ps[0:m, bank + k, :], w1[:, first + lo:first + lo + m], xc,
                                      start=True, stop=True).then_inc(ready, 1)
                    return stage

                def ff_out(c, odd):
                    xf, xc, work, hid = ff(odd)
                    if not isinstance(c, int) or c + 1 < CHUNKS:
                        pe.wait_ge(centred, CHUNKS * l + c + 2)
                    else:
                        pe.wait_ge(x_written, CHUNKS * l + c)
                    for k, (lo, m) in enumerate(HIDDEN_PARTS):
                        pe.wait_ge(hidden_ready, 3 * (CHUNKS * l + c) + k + 1)
                        last = pe.matmul(ps[:, MEAN, :], w2[0:m, k, :], hid[k], start=k == 0, stop=k == 2)
                    last.then_inc(fo_ready, 1)

                ff_pipeline(pe, [(1, means), (0, hidden(1)), (0, hidden(0)), (1, variances), (0, ff_out)])
                pe.wait_ge(x_written, CHUNKS * l + CHUNKS)

        @block.scalar
        def _(act):
            act.wait_ge(const_set, 6)
            with act.Fori(0, DEPTH) as l:
                base = l * TILES
                act.preload_act_table_set("natural_log_exp_and_others")
                act.wait_ge(wqk_loaded, 16 * l + 16)
                act.copy(w_qk[:, 0, :], w_in).then_inc(wqk_high, 1)
                for k in range(4):
                    act.wait_ge(vo_ready, l + 1)
                    act.copy(w_vo[:, (k % 2) * 8 + k // 2:(k % 2) * 8 + k // 2 + 7:2, :],
                             ps[:, k, :].rearrange("p (j n) -> p j n", j=4)).then_inc(vo_copied, 1)

                def keep_part(c):
                    def stage(t, odd):
                        after(act, base, (f"project{c}", t))
                        if later(t, 2):
                            after(act, base, (f"head_turn{c}", t - 2))
                        cols = slice(c * BANK, (c + 1) * BANK)
                        act.copy(qk[:, odd, cols], ps[:, A + c % 2, :])
                        act.activation(sq[:, odd, cols], ps[:, A + c % 2, :], ACT.Square).then_inc(done[f"keep{c}"], 1)
                    return stage

                def inverse_norm(t, odd):
                    after(act, base, ("guard", t))
                    if later(t, 2):
                        after(act, base, ("normed0", t - 2), ("normed1", t - 2))
                    act.activation(rnorm[:, odd, :], ssq[:, odd, :], ACT.Ln, scale=float(2 ** NORM_SHIFT)).then_inc(rs_log, 1)
                    act.wait_ge(rs_log, base + t + 1)
                    act.activation(rnorm[:, odd, :], rnorm[:, odd, :], ACT.Exp, scale=-0.5,
                                   bias=exp_shift[:, 0:1]).then_inc(done["inverse_norm"], 1)

                def copy_heads(c):
                    def stage(t, odd):
                        name = f"copy_heads{c}"
                        after(act, base, (f"head_turn{c}", t))
                        bank = ps[:, T + TURN_BANK[f"head_turn{c}"], :].rearrange("p (j n) -> p j n", j=4)
                        if c < 2:
                            if later(t, 1):
                                after(act, base, ("score", t - 1))
                            act.copy(q_t[:, 4 * c:4 * c + 4, :], bank).then_inc(done[name], 1)
                            return
                        if later(t, 1):
                            after(act, base, ("halo", t - 1))
                        if later(t, 2):
                            after(act, base, ("score", t - 2))
                        pairs = slice(4 * (c - 2), 4 * (c - 2) + 4)
                        act.copy(k_t[0:64, odd, pairs, 0, WINDOW:], bank[0:64])
                        act.copy(k_t[64:128, odd, pairs, 1, WINDOW:], bank[64:128]).then_inc(done[name], 1)
                    return stage

                def copy_rows(t, odd):
                    after(act, base, ("row_turn", t))
                    if later(t, 2):
                        after(act, base, ("mix0", t - 2), ("mix1", t - 2))
                    act.copy(x_rows[:, odd, :, :], ps[:, T + TURN_BANK["row_turn"], :].rearrange("p (w n) -> p w n", w=4)
                             ).then_inc(done["copy_rows"], 1)

                def exponent(t, odd):
                    after(act, base, ("subtract_max", t))
                    act.activation(prob[:, odd, :, :], prob[:, odd, :, :], ACT.Exp, scale=QK_SCALE).then_inc(done["exponent"], 1)

                def copy_probs(c):
                    def stage(t, odd):
                        after(act, base, (f"prob_turn{c}", t))
                        if later(t, 1):
                            after(act, base, ("mix0", t - 1), ("mix1", t - 1))
                        act.copy(prob_t[:, 4 * c:4 * c + 4, :], ps[:, T + TURN_BANK[f"prob_turn{c}"], :].rearrange(
                            "p (j n) -> p j n", j=4)).then_inc(done[f"copy_probs{c}"], 1)
                    return stage

                def copy_mixed(r):
                    def stage(t, odd):
                        after(act, base, (f"mix{r}", t))
                        if later(t, 2):
                            after(act, base, ("output", t - 2))
                        elif t == 0:
                            act.wait_ge(wqk_low, l + 1)
                        for h in range(2):
                            dst = mixed[:, odd, :, h, :].rearrange("p a (w n) -> p w a n", w=4)[:, 2 * r:2 * r + 2]
                            last = act.copy(dst, ps[:, G + h, :].rearrange("p (w a n) -> p w a n", w=2, a=PAIRS))
                        last.then_inc(done[f"copy_mixed{r}"], 1)
                    return stage

                pipeline(act, ACT_ORDER, {**indexed("keep", keep_part, 4), **indexed("copy_heads", copy_heads, 4),
                                          "copy_rows": copy_rows, "inverse_norm": inverse_norm, "exponent": exponent,
                                          **indexed("copy_probs", copy_probs, 2), **indexed("copy_mixed", copy_mixed, 2)})

                def square(c, odd):
                    xf, xc, work, hid = ff(odd)
                    act.wait_ge(centred, CHUNKS * l + c + 1)
                    act.activation(work, xc, ACT.Square).then_inc(squared, 1)

                def rstd(c, odd):
                    xf, xc, work, hid = ff(odd)
                    act.preload_act_table_set("natural_log_exp_and_others")
                    act.wait_ge(var_ready, CHUNKS * l + c + 1)
                    act.activation(work, ps[:, VAR, :], ACT.Ln, bias=eps_col[:, 0:1]).then_inc(log_ready, 1)
                    act.wait_ge(log_ready, CHUNKS * l + c + 1)
                    act.activation(work, work, ACT.Exp, scale=-0.5).then_inc(rstd_ready, 1)

                def gelu(c, odd):
                    xf, xc, work, hid = ff(odd)
                    for k, (lo, m) in enumerate(HIDDEN_PARTS):
                        act.wait_ge(gate_ready, 3 * (CHUNKS * l + c) + k + 1)
                        if later(c, 2):
                            act.wait_ge(fo_ready, CHUNKS * l + c - 1)
                        act.activation(hid[k], ps[0:m, GATE + k, :], ACT.Gelu,
                                       bias=lp[0:m, GATE_B + k:GATE_B + k + 1]).then_inc(gelu_ready, 1)

                ff_pipeline(act, [(1, square), (0, gelu), (1, rstd)])

        @block.vector
        def _(dve):
            dve.memset(exp_shift[:, :], float(np.log(2.0) * NORM_SHIFT / 2)).then_inc(const_set, 1)
            dve.memset(ones_mean[:, :], 1.0 / DIM).then_inc(const_set, 1)
            dve.memset(eps_col[:, :], EPS).then_inc(const_set, 1)
            dve.memset(xb[:, 0:LEAD], 0.0).then_inc(const_set, 1)
            dve.wait_ge(const_loaded, 48)
            dve.wait_ge(const_set, 6)
            with dve.Fori(0, DEPTH) as l:
                base = l * TILES
                dve.wait_ge(wqk_loaded, 16 * l + 16)
                dve.wait_ge(wqk_high, l + 1)
                dve.tensor_tensor(w_qk[:, 1, :], w_in, w_qk[:, 0, :].bitcast(F32), ALU.subtract).then_inc(wqk_low, 1)

                def views(part, odd):
                    cols = slice(part * INNER, (part + 1) * INNER)
                    return qk[:, odd, cols], sq[:, odd, cols]

                def table(part, i, t):
                    return rope_l[:, 2 * part + i, bass.ds(t % SEQ_TILES, 1), :].to_broadcast([P, HEADS, HEAD_DIM])

                def squares(part):
                    def stage(t, odd):
                        kept, squared_heads = views(part, odd)
                        after(dve, base, (f"keep{2 * part}", t), (f"keep{2 * part + 1}", t))
                        if later(t, 2):
                            after(dve, base, ("inverse_norm", t - 2))
                        dve.tensor_reduce(ssq[:, odd, part * HEADS:(part + 1) * HEADS],
                                          squared_heads.rearrange("p (h d) -> p h d", d=HEAD_DIM),
                                          AX_X, ALU.add).then_inc(done[f"squares{part}"], 1)
                    return stage

                def guard(t, odd):
                    after(dve, base, ("squares0", t), ("squares1", t))
                    dve.tensor_scalar(ssq[:, odd, :], ssq[:, odd, :], 1e-24, None, ALU.max).then_inc(done["guard"], 1)

                def sines(part):
                    def stage(t, odd):
                        kept, turned = views(part, odd)
                        after(dve, base, (f"squares{part}", t))
                        if isinstance(t, int) and t == 0:
                            dve.wait_ge(rope_ready, 4 * l + 4)
                        swapped = kept.rearrange("p (h s d) -> p h s d", s=2, d=HEAD_DIM // 2)[:, :, ::-1, :]
                        dve.tensor_tensor(turned.rearrange("p (h s d) -> p h s d", s=2, d=HEAD_DIM // 2), swapped,
                                          table(part, 1, t).rearrange("p h (s d) -> p h s d", s=2),
                                          ALU.mult).then_inc(done[f"sines{part}"], 1)
                    return stage

                def cosines(part):
                    def stage(t, odd):
                        heads = views(part, odd)[0].rearrange("p (h d) -> p h d", d=HEAD_DIM)
                        after(dve, base, (f"sines{part}", t))
                        dve.tensor_tensor(heads, heads, table(part, 0, t), ALU.mult).then_inc(done[f"cosines{part}"], 1)
                    return stage

                def mask_scores(t, odd):
                    after(dve, base, ("score", t))
                    if later(t, 2):
                        after(dve, base, ("prob_turn0", t - 2), ("prob_turn1", t - 2))
                    dve.tensor_tensor(prob[:, odd], ps[:, S:S + 2, :].rearrange("p b (h k) -> p (b h) k", k=2 * WINDOW),
                                      sight[:, bass.ds(t % SEQ_TILES, 1), :].to_broadcast([P, HEADS, 2 * WINDOW]),
                                      ALU.add).then_inc(done["mask_scores"], 1)

                def find_max(t, odd):
                    after(dve, base, ("mask_scores", t))
                    dve.tensor_reduce(stat[:, odd, 0, :], prob[:, odd], AX_X, ALU.max).then_inc(done["find_max"], 1)

                def subtract_max(t, odd):
                    after(dve, base, ("find_max", t))
                    dve.tensor_tensor(prob[:, odd], prob[:, odd], stat[:, odd, 0, :].unsqueeze(2).to_broadcast(
                        [P, HEADS, 2 * WINDOW]), ALU.subtract).then_inc(done["subtract_max"], 1)

                def sum_probs(t, odd):
                    after(dve, base, ("exponent", t))
                    if later(t, 2):
                        after(dve, base, ("normalise_probs", t - 2))
                    dve.tensor_reduce(stat[:, odd, 1, :], prob[:, odd], AX_X, ALU.add).then_inc(done["sum_probs"], 1)

                def invert_sum(t, odd):
                    after(dve, base, ("sum_probs", t))
                    dve.reciprocal(stat[:, odd, 1, :], stat[:, odd, 1, :]).then_inc(done["invert_sum"], 1)

                def add_output(t, odd):
                    after(dve, base, ("output", t))
                    cols = bass.ds(LEAD + t * P, P)
                    dve.tensor_tensor(xb[:, cols], ps[:, T + TURN_BANK["output"], 0:P], xa[:, cols],
                                      ALU.add).then_inc(done["add_output"], 1)

                def shift_tile(t, odd):
                    if later(t, 2):
                        after(dve, base, *[(f"project{c}", t - 2) for c in range(4)])
                    shift_in(dve, xs[:, odd, :], xa, LEAD + t * P, 0, t, xs_low, xs_high, xs_whole, base + t + 1, True)
                    dve.wait_ge(xs_low, base + t + 1)
                    dve.wait_ge(xs_whole, base + t + 1)
                    dve.tensor_copy(xs_parts[:, odd, 0, :], xs[:, odd, :]).then_inc(xs_rounded, 1)
                    dve.wait_ge(xs_rounded, base + t + 1)
                    dve.tensor_tensor(xs_parts[:, odd, 1, :], xs[:, odd, :], xs_parts[:, odd, 0, :].bitcast(F32),
                                      ALU.subtract).then_inc(done["shift_tile"], 1)

                def shift_windows(t, odd):
                    if later(t, 2):
                        after(dve, base, ("row_turn", t - 2))

                    def seen(rows, before):
                        first = xa[rows, bass.ds(LEAD + t * P - WINDOW - before, KEYS)]
                        return bass.AP(first.tensor, first.offset, [first.ap[0], (WINDOW, WINDOWS), (0, 2), (1, 2 * WINDOW)])
                    low, high = (xw[r, odd].rearrange("p w (c k) -> p w c k", c=2) for r in (slice(0, 64), slice(64, 128)))
                    dve.tensor_copy(low, seen(slice(0, 64), 0)).then_inc(xw_low, 1)
                    dve.tensor_copy(high, seen(slice(64, 128), 1)).then_inc(xw_high, 1)
                    dve.wait_ge(xw_high, base + t + 1)
                    for w, key in ((0, WINDOW), (1, 0)):
                        col = high[:, w, :, key]
                        last = dve.tensor_tensor(col, col, keep[64:128, bass.ds(t % SEQ_TILES, 1)].to_broadcast([64, 2]), ALU.mult)
                    last.then_inc(done["shift_windows"], 1)

                pipeline(dve, DVE_ORDER, {
                    "shift_tile": shift_tile, "shift_windows": shift_windows, **indexed("squares", squares, 2), "guard": guard,
                    **indexed("sines", sines, 2), **indexed("cosines", cosines, 2), "mask_scores": mask_scores,
                    "find_max": find_max, "subtract_max": subtract_max, "sum_probs": sum_probs, "invert_sum": invert_sum,
                    "add_output": add_output})

                def centre(c, odd):
                    xf, xc, work, hid = ff(odd)
                    dve.wait_ge(mean_ready, CHUNKS * l + c + 1)
                    if later(c, 2):
                        dve.wait_ge(a_ready, 3 * (CHUNKS * l + c - 1))
                    dve.tensor_tensor(xc, xf, ps[:, MEAN, :], ALU.subtract).then_inc(centred, 1)

                def normalise(c, odd):
                    xf, xc, work, hid = ff(odd)
                    dve.wait_ge(rstd_ready, CHUNKS * l + c + 1)
                    dve.tensor_tensor(xc, xc, work, ALU.mult).then_inc(scaled, 1)
                    if isinstance(c, int) and c == 0:
                        dve.wait_ge(wff_loaded, 48 * l + 48)
                    dve.wait_ge(scaled, CHUNKS * l + c + 1)
                    dve.tensor_scalar(xc, xc, lp[:, LN_G:LN_G + 1], lp[:, LN_B:LN_B + 1], ALU.mult,
                                      ALU.add).then_inc(fn_ready, 1)

                def gate(c, odd):
                    xf, xc, work, hid = ff(odd)
                    for k, (lo, m) in enumerate(HIDDEN_PARTS):
                        dve.wait_ge(a_ready, 3 * (CHUNKS * l + c) + k + 1)
                        dve.wait_ge(gelu_ready, 3 * (CHUNKS * l + c) + k + 1)
                        dve.scalar_tensor_tensor(out=hid[k], in0=ps[0:m, VALUE + k, :], scalar=lp[0:m, A_B + k:A_B + k + 1],
                                                 in1=hid[k], op0=ALU.add, op1=ALU.mult).then_inc(hidden_ready, 1)

                def add_ff(c, odd):
                    dve.wait_ge(fo_ready, CHUNKS * l + c + 1)
                    cols = bass.ds(LEAD + c * BANK, BANK)
                    dve.scalar_tensor_tensor(out=xa[:, cols], in0=ps[:, MEAN, :], scalar=lp[:, OUT_B:OUT_B + 1],
                                             in1=xb[:, cols], op0=ALU.add, op1=ALU.add).then_inc(x_written, 1)

                def shift_chunk(c, odd):
                    xf, xc, work, hid = ff(odd)
                    if isinstance(c, int) and c == 0:
                        after(dve, base, ("add_output", TILES - 1))
                    shift_in(dve, xf, xb, LEAD + c * BANK, 0, (SEQ_TILES // SEQ_CHUNKS) * c, fx_low, fx_high, fx_ready,
                             (CHUNKS // SEQ_CHUNKS) * l + c // 2 + 1 if odd == 0 else 0, odd == 0)

                ff_pipeline(dve, [(1, shift_chunk), (1, centre), (0, gate), (1, normalise), (0, add_ff)])
                dve.wait_ge(x_written, CHUNKS * l + CHUNKS)

        @block.gpsimd
        def _(pool):
            pool.memset(k_t[:, 0], 0.0).then_inc(const_set, 1)
            pool.memset(k_t[:, 1], 0.0).then_inc(const_set, 1)
            pool.wait_ge(const_loaded, 48)
            pool.wait_ge(const_set, 6)

            with pool.Fori(0, DEPTH) as l:
                base = l * TILES
                pool.wait_ge(scale_loaded, 16 * l + 16)
                for part in range(2):
                    scale = head_scale[:, part, :]
                    partner = scale.rearrange("p (s d) -> p s d", s=2)[:, ::-1, :]
                    pool.tensor_tensor(rope_l[:, 2 * part], rope[:, 2 * part],
                                       scale.unsqueeze(1).to_broadcast([P, SEQ_TILES, HEAD_DIM]), ALU.mult).then_inc(rope_ready, 1)
                    pool.tensor_tensor(rope_l[:, 2 * part + 1].rearrange("p t (s d) -> p t s d", s=2),
                                       rope[:, 2 * part + 1].rearrange("p t (s d) -> p t s d", s=2),
                                       partner.unsqueeze(1).to_broadcast([P, SEQ_TILES, 2, HEAD_DIM // 2]),
                                       ALU.mult).then_inc(rope_ready, 1)

                def halo(t, odd):
                    if later(t, 1):
                        after(pool, base, ("copy_heads2", t - 1), ("copy_heads3", t - 1))
                    if later(t, 2):
                        after(pool, base, ("score", t - 2))
                    first = keep[:, bass.ds(t % SEQ_TILES, 1)].unsqueeze(2).to_broadcast([P, 2 * PAIRS, WINDOW])
                    pool.tensor_tensor(k_t[:, odd, :, :, 0:WINDOW].rearrange("p a h k -> p (a h) k"),
                                       k_t[:, 1 - odd, :, :, P:P + WINDOW].rearrange("p a h k -> p (a h) k"), first,
                                       ALU.mult).then_inc(done["halo"], 1)

                def rotated(part):
                    def stage(t, odd):
                        cols = slice(part * INNER, (part + 1) * INNER)
                        after(pool, base, (f"cosines{part}", t))
                        pool.tensor_tensor(qk[:, odd, cols], qk[:, odd, cols], sq[:, odd, cols],
                                           ALU.add).then_inc(done[f"rotated{part}"], 1)
                    return stage

                def normed(part):
                    def stage(t, odd):
                        heads = qk[:, odd, part * INNER:(part + 1) * INNER].rearrange("p (h d) -> p h d", d=HEAD_DIM)
                        after(pool, base, (f"rotated{part}", t), ("inverse_norm", t))
                        norms = rnorm[:, odd, part * HEADS:(part + 1) * HEADS].unsqueeze(2).to_broadcast([P, HEADS, HEAD_DIM])
                        pool.tensor_tensor(heads, heads, norms, ALU.mult).then_inc(done[f"normed{part}"], 1)
                    return stage

                def normalise_probs(t, odd):
                    after(pool, base, ("invert_sum", t))
                    inverse = stat[:, odd, 1, :].unsqueeze(2).to_broadcast([P, HEADS, 2 * WINDOW])
                    pool.tensor_tensor(prob[:, odd], prob[:, odd], inverse, ALU.mult).then_inc(done["normalise_probs"], 1)

                pipeline(pool, POOL_ORDER, {**indexed("rotated", rotated, 2), **indexed("normed", normed, 2),
                                            "halo": halo, "normalise_probs": normalise_probs})


def program(nc, hbm, out):
    with ExitStack() as ctx:
        def sb(name, shape, dt=F32):
            return ctx.enter_context(nc.sbuf_tensor(name, shape, dt))

        def sem(name):
            return ctx.enter_context(nc.semaphore(name))

        resid = sb("resid", [P, TOKENS])
        ident = sb("ident", [P, P])
        ones_mean = sb("ones_mean", [P, P])
        eps_col = sb("eps_col", [P, 1])
        loaded = sem("loaded"); consts = sem("consts"); resid_started = sem("resid_started")
        sum_ready = sem("final_sum_ready"); stored = sem("stored")

        with ExitStack() as front:
            def fsb(name, shape, dt=F32):
                return front.enter_context(nc.sbuf_tensor(name, shape, dt))
            xn = fsb("xn", [P, 2, TOKENS])
            win = fsb("win", [P, 2, 2 * D_INNER]); wx = fsb("wx", [P, 2, HALVES, 96 + DT_RANK])
            wdt = fsb("wdt", [DT_RANK, 2, D_INNER]); wout = fsb("wout", [P, 2, HALVES, DIM])
            packed = fsb("packed", [P, 2, PACKED]); ln = fsb("ln", [P, 2])
            sel = fsb("sel", [96, 2 * D_STATE, P], BF16)
            loads = [(xn[:, 0, :], "x"), (win, "win"), (wx, "wx"), (wdt, "wdt"), (wout, "wout"), (packed, "packed"),
                     (ln, "ln"), (ident, "ident"), (sel, "sel")]
            with nc.Block() as block:
                @block.sync
                def _(sp):
                    for dst, name in loads:
                        sp.dma_start(dst[:], hbm[name]).then_inc(loaded, 16)
                    sp.wait_ge(loaded, 16 * len(loads))

                @block.vector
                def _(dve):
                    dve.memset(ones_mean[:, :], 1.0 / DIM).then_inc(consts, 1)
                    dve.memset(eps_col[:, :], EPS).then_inc(consts, 1)
                    dve.wait_ge(consts, 2)
            with ExitStack() as norms:
                u = norms.enter_context(nc.sbuf_tensor("u", [P, TOKENS], F32))
                work = norms.enter_context(nc.sbuf_tensor("work", [P, TOKENS], F32))

                def add_input(dve, cols, steps):
                    steps.wait(dve)
                    dve.tensor_tensor(resid[:, cols], xn[:, 0, cols], u[:, cols], ALU.add).then_inc(resid_started, 1)

                def affine_both_ways(dve, cols, steps):
                    steps.wait(dve)
                    steps.mark(dve.tensor_scalar(xn[:, 0, cols], xn[:, 0, cols], ln[:, 0:1], ln[:, 1:2], ALU.mult, ALU.add))
                    steps.wait(dve)
                    b, off = divmod(cols.start, SEQ)
                    lo = b * SEQ + SEQ - off - BANK
                    dve.tensor_copy(xn[:, 1, lo:lo + BANK][:, ::-1], xn[:, 0, cols]).then_inc(resid_started, 1)

                with ExitStack() as a:
                    layer_norm_block(nc, a, sem, ones_mean, eps_col, xn[:, 0, :], u, work, (1, add_input), "outer")
                with ExitStack() as a:
                    layer_norm_block(nc, a, sem, ones_mean, eps_col, u, xn[:, 0, :], work, (2, affine_both_ways), "inner")
            mamba(nc, xn, resid, (win, wx, wdt, wout, packed, ident, sel[:, 0:D_STATE, :], sel[:, D_STATE:, :]))
        with ExitStack() as back:
            xa = back.enter_context(nc.sbuf_tensor("xa", [P, LEAD + TOKENS], F32))
            xb = back.enter_context(nc.sbuf_tensor("xb", [P, LEAD + TOKENS], F32))

            def clear_lead(dve, cols, steps):
                if cols.start == 0:
                    dve.memset(xa[:, 0:LEAD], 0.0).then_inc(resid_started, 1)

            with ExitStack() as a:
                layer_norm_block(nc, a, sem, ones_mean, eps_col, resid, xa[:, LEAD:], xb[:, LEAD:], (1, clear_lead), "middle")
            with ExitStack() as a:
                transformer(nc, a, ident, xa, xb, hbm)
            with nc.Block() as block:
                @block.vector
                def _(dve):
                    for c in range(CHUNKS):
                        cols = slice(c * BANK, (c + 1) * BANK)
                        dve.tensor_tensor(resid[:, cols], resid[:, cols], xa[:, LEAD + c * BANK:LEAD + (c + 1) * BANK],
                                          ALU.add).then_inc(sum_ready, 1)

                @block.sync
                def _(sp):
                    for c in range(CHUNKS):
                        sp.wait_ge(sum_ready, c + 1)
                        sp.dma_start(out[:, c * BANK:(c + 1) * BANK], resid[:, c * BANK:(c + 1) * BANK]).then_inc(stored, 16)
                    sp.wait_ge(stored, 16 * CHUNKS)


def rope_tables():
    half = np.arange(0, HEAD_DIM, 2, dtype=np.float64)
    angle = np.arange(SEQ)[:, None] * (10000.0 ** (-half / HEAD_DIM))[None]
    power = (np.arange(SEQ) - SEQ // 2) / (WINDOW // 2)
    scale = ((half + 0.4 * HEAD_DIM) / (1.4 * HEAD_DIM))[None] ** power[:, None]
    cos, sin = np.cos(angle), np.sin(angle)
    tables = [np.concatenate(v, axis=1) for v in ((cos * scale,) * 2, (-sin * scale, sin * scale),
                                                  (cos / scale,) * 2, (-sin / scale, sin / scale))]
    t = np.stack(tables).astype(np.float32).reshape(4, SEQ_TILES, P, HEAD_DIM)
    return np.ascontiguousarray(t.transpose(2, 0, 1, 3))


def sight_table():
    i, j = np.arange(P)[:, None] % WINDOW, np.arange(2 * WINDOW)[None]
    seen = np.where(j < WINDOW, j >= i, j - WINDOW <= i)
    table = np.repeat(np.where(seen, 0.0, HIDDEN_ROW)[:, None, :], SEQ_TILES, axis=1)
    table[:WINDOW, 0, :WINDOW] = HIDDEN_ROW
    return table.astype(np.float32)


def host_layout(inputs):
    a = {k: np.asarray(v) for k, v in inputs.items()}
    both = lambda name, f: np.stack([f(a[f"L0_attn_{d}_{name}"]) for d in "fb"], axis=1)
    halves = lambda v: np.moveaxis(v.reshape(HALVES, P, *v.shape[1:]), 0, 1).reshape(P, -1)
    wx = [a[f"L0_attn_{d}_W_x"].T.reshape(HALVES, P, -1).transpose(1, 0, 2) for d in "fb"]
    bcs = [np.concatenate([w[:, :, DT_RANK:]] * 3 + [w[:, :, :DT_RANK]], axis=2) for w in wx]
    packed = [np.concatenate([halves(a[f"L0_attn_{d}_{n}"]) for n in ("W_conv", "b_conv", "b_dt", "A_log", "D")], axis=1)
              for d in "fb"]
    row, state = np.arange(96)[:, None] % 32, np.arange(32)[None]
    wqkv = a["L0_ffn_Wqkv"]
    w2 = np.zeros((DEPTH, P, 3, DIM), np.float32)
    lp = np.zeros((DEPTH, P, LAYER_PACKED), np.float32)
    lp[:, :, LN_G], lp[:, :, LN_B], lp[:, :, OUT_B] = a["L0_ffn_ln_g"], a["L0_ffn_ln_b"], a["L0_ffn_b2"]
    for k, (lo, m) in enumerate(HIDDEN_PARTS):
        w2[:, :m, k] = a["L0_ffn_W2"][:, lo:lo + m]
        lp[:, :m, A_B + k] = a["L0_ffn_b1"][:, lo:lo + m]
        lp[:, :m, GATE_B + k] = a["L0_ffn_b1"][:, HIDDEN + lo:HIDDEN + lo + m]
    return {
        "x": np.ascontiguousarray(a["L0_attn_x"].reshape(TOKENS, DIM).T),
        "win": np.ascontiguousarray(both("W_in", lambda w: w.T)),
        "wx": np.ascontiguousarray(np.stack(bcs, axis=1)),
        "wdt": np.ascontiguousarray(both("W_dt", lambda w: w.T)),
        "wout": np.ascontiguousarray(both("W_out", lambda w: w.T.reshape(HALVES, P, DIM).transpose(1, 0, 2))),
        "packed": np.ascontiguousarray(np.stack(packed, axis=1)),
        "ln": np.ascontiguousarray(np.stack([a["L0_attn_ln_w"], a["L0_attn_ln_b"]], axis=1)),
        "ident": np.eye(P, dtype=np.float32),
        "sel": np.ascontiguousarray(np.broadcast_to((row == state)[:, :, None], (96, 32, P))).astype(mybir.dt.np(BF16)),
        "rope": rope_tables(),
        "sight": sight_table(),
        "keep": np.ascontiguousarray(np.broadcast_to((np.arange(SEQ_TILES) > 0).astype(np.float32), (P, SEQ_TILES))),
        "w_qk": np.ascontiguousarray(wqkv[:, :, :2 * INNER]),
        "w_v": np.ascontiguousarray(wqkv[:, :, 2 * INNER:].transpose(0, 2, 1).reshape(DEPTH, PAIRS, P, DIM).transpose(0, 2, 1, 3)),
        "w_o": np.ascontiguousarray(a["L0_ffn_Wo"].reshape(DEPTH, PAIRS, P, DIM).transpose(0, 2, 1, 3)),
        "w1": a["L0_ffn_W1"],
        "w2": w2,
        "lp": lp,
        "head_scale": np.stack([a["L0_ffn_q_scale"], a["L0_ffn_k_scale"]], axis=1),
    }


def kernel(**inputs):
    import concourse.bacc as bacc
    from concourse.bass_utils import run_bass_kernel_spmd

    nc = bacc.Bacc("TRN2", target_bir_lowering=False, num_devices=1)
    arrays = {f"{name}_hbm": array for name, array in host_layout(inputs).items()}
    hbm = {name[:-4]: nc.dram_tensor(name, array.shape, mybir.dt.from_np(array.dtype), kind="ExternalInput").ap()
           for name, array in arrays.items()}
    out = nc.dram_tensor("out_hbm", (P, TOKENS), F32, kind="ExternalOutput").ap()
    program(nc, hbm, out)
    result = run_bass_kernel_spmd(nc, [arrays], core_ids=[0]).results[0]["out_hbm"]
    return np.ascontiguousarray(np.asarray(result).T).reshape(BATCH, SEQ, DIM)
```

```python
from contextlib import ExitStack

import numpy as np

import concourse.bass as bass
from concourse import mybir

F32 = mybir.dt.float32
F32R = mybir.dt.float32r
BF16 = mybir.dt.bfloat16
ALU = mybir.AluOpType
ACT = mybir.ActivationFunctionType
AX_X = mybir.AxisListType.X

P = 128
BANK = 512
BATCH, SEQ, DIM = 4, 1024, 128
TOKENS = BATCH * SEQ
HALF_BANKS = SEQ // BANK
D_INNER, D_STATE, D_CONV, DT_RANK = 256, 16, 4, 8
HALVES = D_INNER // P
EPS = 1e-5

CONV_W, CONV_B, DT_B, A_LOG, D_SKIP = 0, 8, 10, 12, 44
PACKED = 46
BC_ROWS = 3 * 2 * D_STATE


class Steps:

    def __init__(self, sem, base=0):
        self.sem, self.base, self.count = sem, base, 0

    def mark(self, instruction):
        instruction.then_inc(self.sem, 1)
        self.count += 1

    def wait(self, eng):
        eng.wait_ge(self.sem, self.base + self.count)


def layer_norm_block(nc, ctx, sems, number, ones_mean, eps_col, src, out, work, finish):
    chunks = TOKENS // BANK
    base = number * chunks
    mean_ready, centred, squared, var_ready, log_done, rstd_ready, dve_done = sems
    stats = ctx.enter_context(nc.psum_tensor(f"stats{number}", [P, chunks, BANK], F32))
    with nc.Block() as block:
        @block.tensor
        def _(pe):
            for c in range(chunks):
                pe.matmul(stats[:, c, :], ones_mean[:, :], src[:, c * BANK:(c + 1) * BANK],
                          start=True, stop=True).then_inc(mean_ready, 1)
            for c in range(chunks):
                pe.wait_ge(squared, base + c + 1)
                pe.matmul(stats[:, c, :], ones_mean[:, :], work[:, c * BANK:(c + 1) * BANK],
                          start=True, stop=True).then_inc(var_ready, 1)

        @block.vector
        def _(dve):
            for c in range(chunks):
                cols = slice(c * BANK, (c + 1) * BANK)
                dve.wait_ge(mean_ready, base + c + 1)
                dve.tensor_tensor(out[:, cols], src[:, cols], stats[:, c, :],
                                  ALU.subtract).then_inc(centred, 1)
            for c in range(chunks):
                cols = slice(c * BANK, (c + 1) * BANK)
                steps = Steps(dve_done, base + c)
                dve.wait_ge(rstd_ready, base + c + 1)
                steps.mark(dve.tensor_tensor(out[:, cols], out[:, cols], work[:, cols], ALU.mult))
                finish(dve, cols, steps)

        @block.scalar
        def _(act):
            for c in range(chunks):
                cols = slice(c * BANK, (c + 1) * BANK)
                act.wait_ge(centred, base + c + 1)
                act.activation(work[:, cols], out[:, cols], ACT.Square).then_inc(squared, 1)
            for c in range(chunks):
                cols = slice(c * BANK, (c + 1) * BANK)
                act.wait_ge(var_ready, base + c + 1)
                act.activation(work[:, cols], stats[:, c, :], ACT.Ln, bias=eps_col[:, 0:1]).then_inc(log_done, 1)
            for c in range(chunks):
                cols = slice(c * BANK, (c + 1) * BANK)
                act.wait_ge(log_done, base + c + 1)
                act.activation(work[:, cols], work[:, cols], ACT.Exp, scale=-0.5).then_inc(rstd_ready, 1)


def mamba(nc, xn, resid, weights):
    win, wx, wdt, wout, packed, ident, sel_b, sel_c = weights
    with ExitStack() as ctx:
        def sb(name, shape, dt=F32):
            return ctx.enter_context(nc.sbuf_tensor(name, shape, dt))

        def sem(name):
            return ctx.enter_context(nc.semaphore(name))

        UNITS = D_STATE * HALVES
        AHEAD = 4
        PAD = D_CONV
        neg_a = sb("neg_a", [P, 2, HALVES * D_STATE])
        dt_pad = sb("dt_pad", [P, 2, HALVES, PAD + SEQ])
        xc = sb("xc", [P, 2, HALVES, SEQ])
        zs = sb("zs", [P, 2, HALVES, SEQ])
        dtx = sb("dtx", [P, 2, HALVES, SEQ])
        bc = sb("bc", [BC_ROWS, 2, SEQ], BF16)
        x_dbl = sb("x_dbl", [BC_ROWS + DT_RANK, SEQ])
        x_back = sb("x_back", [P, SEQ])
        bc_mid = x_back[64:96, 0:SEQ // 2].bitcast(BF16)
        decay = sb("decay", [P, HALVES, AHEAD, SEQ])
        drive = sb("drive", [P, 2, SEQ])
        state = sb("state", [P, 4, SEQ])
        c_row = sb("c_row", [P, 2, SEQ])
        read = sb("read", [P, 4, SEQ])
        ps = ctx.enter_context(nc.psum_tensor("mamba_ps", [P, 8, BANK], F32))
        b_ps, turn, y_ps = ps[:, 0:2, :], ps[:, 2:4, :], [ps[:, 4 + 2 * h:6 + 2 * h, :] for h in range(HALVES)]

        a_exp = sem("a_exp"); a_ready = sem("a_ready"); pad_ready = sem("pad_ready"); turned = sem("turned")
        xz_ready = sem("xz_ready"); xp_ready = sem("xp_ready"); zs_ready = sem("zs_ready")
        first_tap = sem("first_tap"); conv_step = sem("conv_step"); conv_ready = sem("conv_ready"); xc_ready = sem("xc_ready")
        xdbl_ready = sem("xdbl_ready"); xdbl_copied = sem("xdbl_copied"); bc_high = sem("bc_high")
        split_step = sem("split_step"); bc_ready = sem("bc_ready"); v_ready = sem("v_ready")
        abs_ready = sem("abs_ready"); relu_ready = sem("relu_ready"); exp_done = sem("exp_done"); log_done = sem("log_done")
        dt_ready = sem("dt_ready"); dtx_ready = sem("dtx_ready")
        b_ready = sem("b_ready"); c_ready = sem("c_ready"); c_copied = sem("c_copied")
        decay_ready = sem("decay_ready"); drive_ready = sem("drive_ready"); state_ready = sem("state_ready")
        read_ready = sem("read_ready"); summed = sem("summed"); skip_added = sem("skip_added")
        gated_ready = sem("gated_ready"); out_ready = sem("out_ready"); resid_done = sem("resid_done")

        def passes(body):
            def run(eng):
                body(0, 0, 0, True, False)
                with eng.Fori(0, BATCH - 1) as b:
                    body(2 * b + 1, b, 1, False, False)
                    body(2 * b + 2, b + 1, 0, False, False)
                body(2 * BATCH - 1, BATCH - 1, 1, False, True)
            return run

        def earlier(s, i, k):
            return not (isinstance(s, int) and s == 0 and i < k)

        PROJECT_AT = {3: 0, 4: 1, 5: 2, 6: 3, 7: 4, 8: 5, 9: 6}
        SOFTPLUS_AT, CONV_AT, SPLIT_AT, DT_AT, DTX_AT = 10, {5: 0, 6: 1}, 10, 12, 15
        LEAD_DECAYS = 3
        GATE_AT, OUTPUT_AT = 1, 2

        with nc.Block() as block:
            @block.tensor
            def _(pe):
                reader = [None]

                def take_turn(now):
                    if reader[0]:
                        pe.wait_ge(*reader[0])
                    reader[0] = now

                def project(k, s, b, d):
                    if k < 2 * HALVES:
                        take_turn((xp_ready, HALVES * s + k + 1) if k < HALVES else (zs_ready, HALVES * s + k - 1))
                        if d:
                            pe.wait_ge(turned, b + 1)
                        for c in range(HALF_BANKS):
                            tokens = x_back[:, c * BANK:(c + 1) * BANK] if d else xn[:, bass.ds(b * SEQ + c * BANK, BANK)]
                            last = pe.matmul(turn[:, c, :], win[:, d, k * P:(k + 1) * P], tokens, start=True, stop=True)
                        last.then_inc(xz_ready, 1)
                    elif k == 4:
                        take_turn((bc_high, s + 1))
                        pe.wait_ge(xc_ready, HALVES * s + HALVES)
                        for c in range(HALF_BANKS):
                            for h in range(HALVES):
                                last = pe.matmul(turn[0:BC_ROWS + DT_RANK, c, :], wx[:, d, h, :],
                                                 xc[:, d, h, c * BANK:(c + 1) * BANK], start=h == 0, stop=h == HALVES - 1)
                        last.then_inc(xdbl_ready, 1)
                    else:
                        h = k - 5
                        take_turn((relu_ready, HALVES * s + h + 1))
                        pe.wait_ge(xdbl_copied, s + 1)
                        for c in range(HALF_BANKS):
                            last = pe.matmul(turn[:, c, :], wdt[BC_ROWS:BC_ROWS + DT_RANK, d, h * P:(h + 1) * P],
                                             x_dbl[BC_ROWS:BC_ROWS + DT_RANK, c * BANK:(c + 1) * BANK], start=True, stop=True)
                        last.then_inc(v_ready, 1)

                def b_rows(s, d, n):
                    if earlier(s, n, 1):
                        pe.wait_ge(drive_ready, UNITS * s + 2 * n)
                    for c in range(HALF_BANKS):
                        last = pe.matmul(b_ps[:, c, :], sel_b[:, n, :], bc[:, d, c * BANK:(c + 1) * BANK], start=True, stop=True)
                    last.then_inc(b_ready, 1)

                def c_rows(s, d, n):
                    take_turn((c_copied, D_STATE * s + n + 1))
                    for c in range(HALF_BANKS):
                        last = pe.matmul(turn[:, c, :], sel_c[:, n, :], bc[:, d, c * BANK:(c + 1) * BANK], start=True, stop=True)
                    last.then_inc(c_ready, 1)

                def add_read(s, n, h):
                    if n == 0 and earlier(s, n, 1):
                        pe.wait_ge(skip_added, HALVES * s - 1 + h)
                    pe.wait_ge(read_ready, UNITS * s + 2 * n + h + 1)
                    for c in range(HALF_BANKS):
                        last = pe.matmul(y_ps[h][:, c, :], ident[:, :], read[:, (2 * n + h) % 4, c * BANK:(c + 1) * BANK],
                                         start=n == 0, stop=n == D_STATE - 1)
                    last.then_inc(summed, 1)

                def output(s, d):
                    take_turn((resid_done, s + 1))
                    for h in range(HALVES):
                        pe.wait_ge(gated_ready, HALVES * s + h + 1)
                        for c in range(HALF_BANKS):
                            last = pe.matmul(turn[:, c, :], wout[:, d, h, :], zs[:, d, h, c * BANK:(c + 1) * BANK],
                                             start=h == 0, stop=h == HALVES - 1)
                    last.then_inc(out_ready, 1)

                def lead(s, d):
                    pe.wait_ge(bc_ready, s + 1)
                    b_rows(s, d, 0)
                    c_rows(s, d, 0)

                def body(s, b, d, first, last):
                    reader[0] = (c_copied, D_STATE * s + 1)
                    for n in range(D_STATE):
                        if n + 1 < D_STATE:
                            b_rows(s, d, n + 1)
                        if n == OUTPUT_AT and not first:
                            output(s - 1, 1 - d)
                        if n:
                            add_read(s, n - 1, 0)
                        if n in PROJECT_AT and not last:
                            project(PROJECT_AT[n], s + 1, b + d, 1 - d)
                        if n:
                            add_read(s, n - 1, 1)
                        if n + 1 < D_STATE:
                            c_rows(s, d, n + 1)
                    if not last:
                        lead(s + 1, 1 - d)
                    for h in range(HALVES):
                        add_read(s, D_STATE - 1, h)

                for k in range(7):
                    project(k, 0, 0, 0)
                lead(0, 0)
                passes(body)(pe)
                output(2 * BATCH - 1, 1)

            @block.scalar
            def _(act):
                for d in range(2):
                    act.activation(neg_a[:, d, :], packed[:, d, A_LOG:A_LOG + 32], ACT.Exp).then_inc(a_exp, 1)
                act.wait_ge(a_ready, 1)
                act.wait_ge(pad_ready, 1)

                def take_projection(k, s, d):
                    if k < HALVES:
                        act.wait_ge(xz_ready, 4 * s + k + 1)
                        act.copy(dt_pad[:, d, k, PAD:], turn).then_inc(xp_ready, 1)
                        act.wait_ge(xp_ready, HALVES * s + k + 1)
                        act.activation(dtx[:, d, k, :], dt_pad[:, d, k, 1:1 + SEQ], ACT.Copy,
                                       scale=packed[:, d, CONV_W + k * D_CONV:CONV_W + k * D_CONV + 1]).then_inc(first_tap, 1)
                    elif k < 2 * HALVES:
                        h = k - HALVES
                        act.wait_ge(xz_ready, 4 * s + k + 1)
                        act.activation(zs[:, d, h, :], turn, ACT.Silu).then_inc(zs_ready, 1)
                        act.wait_ge(conv_ready, HALVES * s + h + 1)
                        act.activation(xc[:, d, h, :], dtx[:, d, h, :], ACT.Silu,
                                       bias=packed[:, d, CONV_B + h:CONV_B + h + 1]).then_inc(xc_ready, 1)
                    elif k == 4:
                        act.wait_ge(xdbl_ready, s + 1)
                        act.copy(x_dbl[:, :], turn[0:BC_ROWS + DT_RANK]).then_inc(xdbl_copied, 1)
                        act.copy(bc[:, d, :], turn[0:BC_ROWS]).then_inc(bc_high, 1)
                    else:
                        h = k - 5
                        bias = packed[:, d, DT_B + h:DT_B + h + 1]
                        act.wait_ge(v_ready, HALVES * s + h + 1)
                        act.activation(dt_pad[:, d, h, PAD:], turn, ACT.Abs, bias=bias).then_inc(abs_ready, 1)
                        act.activation(dtx[:, d, h, :], turn, ACT.Relu, bias=bias).then_inc(relu_ready, 1)

                def softplus(s, d):
                    for h in range(HALVES):
                        act.wait_ge(abs_ready, HALVES * s + h + 1)
                        act.activation(dt_pad[:, d, h, PAD:], dt_pad[:, d, h, PAD:], ACT.Exp, scale=-1.0).then_inc(exp_done, 1)
                    for h in range(HALVES):
                        act.wait_ge(exp_done, HALVES * s + h + 1)
                        act.activation(dt_pad[:, d, h, PAD:], dt_pad[:, d, h, PAD:], ACT.Ln, bias=1.0).then_inc(log_done, 1)

                def decays(s, d, n):
                    for h in range(HALVES):
                        if n == 0:
                            act.wait_ge(dt_ready, HALVES * s + h + 1)
                        if earlier(s, n, AHEAD):
                            act.wait_ge(state_ready, UNITS * s + 2 * (n - AHEAD) + h + 1)
                        act.activation(decay[:, h, n % AHEAD, :], dt_pad[:, d, h, PAD:], ACT.Exp,
                                       scale=neg_a[:, d, h * D_STATE + n:h * D_STATE + n + 1]).then_inc(decay_ready, 1)

                def copy_c(s, n):
                    act.wait_ge(c_ready, D_STATE * s + n + 1)
                    if earlier(s, n, 2):
                        act.wait_ge(read_ready, UNITS * s + 2 * (n - 1))
                    act.copy(c_row[:, n % 2, :], turn).then_inc(c_copied, 1)

                def body(s, b, d, first, last):
                    for n in range(D_STATE):
                        if n + LEAD_DECAYS < D_STATE:
                            decays(s, d, n + LEAD_DECAYS)
                        if n in PROJECT_AT and not last:
                            take_projection(PROJECT_AT[n], s + 1, 1 - d)
                        if n + 1 < D_STATE:
                            copy_c(s, n + 1)
                        if n == SOFTPLUS_AT and not last:
                            softplus(s + 1, 1 - d)
                    if not last:
                        for n in range(LEAD_DECAYS):
                            decays(s + 1, 1 - d, n)
                        copy_c(s + 1, 0)

                for k in range(7):
                    take_projection(k, 0, 0)
                softplus(0, 0)
                for n in range(LEAD_DECAYS):
                    decays(0, 0, n)
                copy_c(0, 0)
                passes(body)(act)

            @block.vector
            def _(dve):
                dve.memset(dt_pad[:, :, :, 0:PAD], 0.0).then_inc(pad_ready, 1)
                dve.wait_ge(a_exp, 2)
                dve.tensor_scalar(neg_a[:, :, :], neg_a[:, :, :], -1.0, None, ALU.mult).then_inc(a_ready, 1)

                def turn_tokens(b):
                    dve.tensor_copy(x_back[:, ::-1], xn[:, bass.ds(b * SEQ, SEQ)]).then_inc(turned, 1)

                def convolve(s, d, h):
                    steps = Steps(conv_step, HALVES * (D_CONV - 2) * s + (D_CONV - 2) * h)
                    dve.wait_ge(first_tap, HALVES * s + h + 1)
                    for k in range(1, D_CONV):
                        ins = dve.scalar_tensor_tensor(
                            out=dtx[:, d, h, :], in0=dt_pad[:, d, h, k + 1:k + 1 + SEQ],
                            scalar=packed[:, d, CONV_W + h * D_CONV + k:CONV_W + h * D_CONV + k + 1],
                            in1=dtx[:, d, h, :], op0=ALU.mult, op1=ALU.add)
                        if k < D_CONV - 1:
                            steps.mark(ins)
                            steps.wait(dve)
                        else:
                            ins.then_inc(conv_ready, 1)

                def split_bc(s, d):
                    steps = Steps(split_step, 4 * s)
                    dve.wait_ge(bc_high, s + 1)
                    steps.mark(dve.tensor_tensor(x_dbl[0:BC_ROWS, :], x_dbl[0:BC_ROWS, :], bc[:, d, :], ALU.subtract))
                    steps.wait(dve)
                    steps.mark(dve.tensor_copy(bc[32:64, d, :], x_dbl[32:64, :]))
                    steps.mark(dve.tensor_copy(bc_mid, x_dbl[64:96, :]))
                    steps.wait(dve)
                    steps.mark(dve.tensor_tensor(x_dbl[64:96, :], x_dbl[64:96, :], bc_mid, ALU.subtract))
                    steps.wait(dve)
                    dve.tensor_copy(bc[64:96, d, :], x_dbl[64:96, :]).then_inc(bc_ready, 1)

                def add_relu(s, d):
                    for h in range(HALVES):
                        dve.wait_ge(log_done, HALVES * s + h + 1)
                        dve.wait_ge(relu_ready, HALVES * s + h + 1)
                        dve.tensor_tensor(dt_pad[:, d, h, PAD:], dt_pad[:, d, h, PAD:], dtx[:, d, h, :],
                                          ALU.add).then_inc(dt_ready, 1)

                def times_xc(s, d):
                    for h in range(HALVES):
                        dve.wait_ge(dt_ready, HALVES * s + h + 1)
                        dve.wait_ge(xc_ready, HALVES * s + h + 1)
                        dve.tensor_tensor(dtx[:, d, h, :], dt_pad[:, d, h, PAD:], xc[:, d, h, :], ALU.mult).then_inc(dtx_ready, 1)

                def gate(s, d):
                    for h in range(HALVES):
                        dve.wait_ge(summed, UNITS * s + UNITS - 1 + h)
                        dve.scalar_tensor_tensor(out=xc[:, d, h, :], in0=xc[:, d, h, :],
                                                 scalar=packed[:, d, D_SKIP + h:D_SKIP + h + 1],
                                                 in1=y_ps[h], op0=ALU.mult, op1=ALU.add).then_inc(skip_added, 1)
                    for h in range(HALVES):
                        dve.wait_ge(skip_added, HALVES * s + h + 1)
                        dve.wait_ge(zs_ready, HALVES * s + h + 1)
                        dve.tensor_tensor(zs[:, d, h, :], xc[:, d, h, :], zs[:, d, h, :], ALU.mult).then_inc(gated_ready, 1)

                def add_output(s, b, d):
                    dve.wait_ge(out_ready, s + 1)
                    if d:
                        dve.wait_ge(resid_done, s)
                    r = resid[:, bass.ds(b * SEQ, SEQ)]
                    y = turn.rearrange("p a b -> p (a b)")
                    if d:
                        y = y[:, ::-1]
                    dve.scalar_tensor_tensor(out=r, in0=y, scalar=0.5, in1=r, op0=ALU.mult, op1=ALU.add).then_inc(resid_done, 1)

                def body(s, b, d, first, last):
                    for n in range(D_STATE):
                        dve.wait_ge(b_ready, D_STATE * s + n + 1)
                        for h in range(HALVES):
                            u = 2 * n + h
                            if n == 0:
                                dve.wait_ge(dtx_ready, HALVES * s + h + 1)
                            if earlier(s, u, 2):
                                dve.wait_ge(state_ready, UNITS * s + u - 1)
                            dve.tensor_tensor(drive[:, h, :], dtx[:, d, h, :], b_ps, ALU.mult).then_inc(drive_ready, 1)
                        if n == GATE_AT and not first:
                            gate(s - 1, 1 - d)
                        for h in range(HALVES):
                            u = 2 * n + h
                            dve.wait_ge(decay_ready, UNITS * s + u + 1)
                            dve.wait_ge(drive_ready, UNITS * s + u + 1)
                            if earlier(s, u, 4):
                                dve.wait_ge(read_ready, UNITS * s + u - 3)
                            dve.tensor_tensor_scan(state[:, u % 4, :], decay[:, h, n % AHEAD, :], drive[:, h, :],
                                                   0.0, ALU.mult, ALU.add).then_inc(state_ready, 1)
                        if n == GATE_AT and not last and not d:
                            turn_tokens(b)
                        if n == OUTPUT_AT and not first:
                            add_output(s - 1, b - 1 + d, 1 - d)
                        if n in CONV_AT and not last:
                            convolve(s + 1, 1 - d, CONV_AT[n])
                        if n == SPLIT_AT and not last:
                            split_bc(s + 1, 1 - d)
                        if n == DT_AT and not last:
                            add_relu(s + 1, 1 - d)
                        if n == DTX_AT and not last:
                            times_xc(s + 1, 1 - d)

                for h in range(HALVES):
                    convolve(0, 0, h)
                split_bc(0, 0)
                add_relu(0, 0)
                times_xc(0, 0)
                passes(body)(dve)
                gate(2 * BATCH - 1, 1)
                add_output(2 * BATCH - 1, BATCH - 1, 1)

            @block.gpsimd
            def _(pool):
                def body(s, b, d, first, last):
                    for u in range(UNITS):
                        pool.wait_ge(state_ready, UNITS * s + u + 1)
                        pool.wait_ge(c_copied, D_STATE * s + u // 2 + 1)
                        if earlier(s, u, 4):
                            pool.wait_ge(summed, UNITS * s + u - 3)
                        pool.tensor_tensor(read[:, u % 4, :], state[:, u % 4, :], c_row[:, (u // 2) % 2, :],
                                           ALU.mult).then_inc(read_ready, 1)
                passes(body)(pool)


DEPTH, HEADS, HEAD_DIM, WINDOW = 6, 16, 64, 32
PAIRS = HEADS // 2
INNER = HEADS * HEAD_DIM
HIDDEN = int(DIM * 4 * 2 / 3)
HIDDEN_PARTS = [(0, P), (P, P), (2 * P, HIDDEN - 2 * P)]
QK_SCALE = 8.0
TILES = TOKENS // P
SEQ_TILES = SEQ // P
CHUNKS = TOKENS // BANK
SEQ_CHUNKS = SEQ // BANK
WINDOWS = P // WINDOW
LEAD = 64
KEYS = P + WINDOW
HIDDEN_ROW = -1e30
NORM_SHIFT = 20
LN_G, LN_B, OUT_B, A_B, GATE_B = 0, 1, 2, 3, 6
LAYER_PACKED = 9


PE_ORDER = [(1, "project2"), (1, "project3"), (3, "head_turn2"), (3, "head_turn3"), (6, "mix1"), (5, "prob_turn1"),
            (5, "prob_turn0"), (3, "score"), (4, "row_turn"), (0, "project0"), (2, "head_turn0"), (5, "mix0"),
            (0, "project1"), (2, "head_turn1"), (6, "output")]
ACT_ORDER = [(6, "copy_mixed0"), (2, "inverse_norm"), (3, "copy_heads2"), (3, "copy_heads3"), (6, "copy_mixed1"),
             (5, "copy_probs1"), (1, "keep2"), (5, "copy_probs0"), (4, "exponent"), (4, "copy_rows"), (1, "keep3"),
             (0, "keep0"), (2, "copy_heads0"), (0, "keep1"), (2, "copy_heads1")]
DVE_ORDER = [(0, "shift_tile"), (4, "subtract_max"), (1, "squares0"), (2, "cosines1"), (1, "sines0"),
             (4, "sum_probs"), (1, "cosines0"), (4, "invert_sum"), (1, "squares1"), (3, "mask_scores"), (1, "guard"),
             (6, "add_output"), (3, "shift_windows"), (3, "find_max"), (1, "sines1")]
POOL_ORDER = [(3, "normed0"), (3, "halo"), (3, "rotated1"), (3, "normed1"), (5, "normalise_probs"), (2, "rotated0"),
              (2, "refine_norm")]
MAX_LAG = 6
TURN_READERS = {"head_turn0": "copy_heads0", "head_turn1": "copy_heads1", "head_turn2": "copy_heads2",
                "head_turn3": "copy_heads3", "row_turn": "copy_rows", "prob_turn0": "copy_probs0",
                "prob_turn1": "copy_probs1", "output": "add_output"}
TURNS = [(lag, name) for lag, name in PE_ORDER if name in TURN_READERS]
TURN_BANK = {name: k % 2 for k, (_, name) in enumerate(TURNS)}


FF_PE_ORDER = [(2, "gate2"), (2, "value1"), (2, "gate1"), (0, "mean"), (2, "value0"), (3, "ff_output"),
               (0, "variance"), (2, "value2"), (1, "gate0")]
FF_ACT_ORDER = [(3, "gelu2"), (1, "log"), (1, "rstd"), (2, "gelu1"), (0, "square"), (2, "gelu0")]
FF_DVE_ORDER = [(0, "shift_chunk"), (3, "product2"), (0, "centre"), (1, "scale"), (1, "affine"), (1, "round"),
                (1, "rest"), (2, "product1"), (2, "product0"), (3, "add_ff")]
FF_LAG = 3
FF_EARLY = {3: 0}


def stepper(order, stages, count):
    def step(i, odd):
        for lag, name in order:
            if not isinstance(i, int) or 0 <= i - lag < count:
                stages[name](i - lag, (odd - lag) % 2)
    return step


def pipeline(eng, tile_step, chunk_step):
    warm = (MAX_LAG + 3) // 2 * 2
    for i in range(warm):
        tile_step(i, i % 2)
    with eng.Fori(warm // 2, TILES // 2) as two:
        tile_step(2 * two, 0)
        tile_step(2 * two + 1, 1)
    for i in range(TILES, TILES + MAX_LAG):
        tile_step(i, i % 2)
        if i - TILES in FF_EARLY and chunk_step:
            chunk_step(FF_EARLY[i - TILES], FF_EARLY[i - TILES] % 2)
    if chunk_step:
        for i in range(len(FF_EARLY), CHUNKS + FF_LAG):
            chunk_step(i, i % 2)


def later(tile, n):
    return not isinstance(tile, int) or tile >= n


def last_turn(name, tile):
    k = [n for _, n in TURNS].index(name)
    lag = TURNS[k][0]
    step = 0
    while True:
        k -= 2
        if k < 0:
            k, step = k + len(TURNS), step - 1
        used = tile + (lag + step - TURNS[k][0])
        if not isinstance(tile, int) or 0 <= used < TILES:
            return TURNS[k][1], used
        if tile + lag + step < 0:
            return None, None


def transformer(nc, ctx, ident, xa, xb, hbm):
    def sb(name, shape, dt=F32):
        return ctx.enter_context(nc.sbuf_tensor(name, shape, dt))

    def sem(name):
        return ctx.enter_context(nc.semaphore(name))

    w_qk = sb("w_qk", [P, 2, 2 * INNER], F32R)
    w_vo = sb("w_vo", [P, HEADS, P])
    w1 = sb("w1", [P, 2 * HIDDEN])
    w1_parts = sb("w1_parts", [P, 2, 2 * HIDDEN], F32R)
    w2 = sb("w2", [P, 3, P])
    lp = sb("lp", [P, LAYER_PACKED])
    head_scale = sb("head_scale", [P, 2, HEAD_DIM])
    rope = sb("rope", [P, 4, SEQ_TILES, HEAD_DIM])
    rope_l = sb("rope_l", [P, 4, SEQ_TILES, HEAD_DIM])
    sight = sb("sight", [P, SEQ_TILES, 2 * WINDOW])
    keep = sb("keep", [P, SEQ_TILES])
    exp_shift = sb("exp_shift", [P, 1])
    ones_mean = sb("ones_mean2", [P, P])
    eps_col = sb("eps_col2", [P, 1])

    xs = sb("xs", [P, 2, P])
    xs_parts = sb("xs_parts", [P, 2, 2, P], F32R)
    xw = sb("xw", [P, 2, WINDOWS, 2 * 2 * WINDOW])
    x_rows = sb("x_rows", [P, 2, WINDOWS, P])
    qk = sb("qk", [P, 2, 2 * INNER])
    sq = sb("sq", [P, 2, 2 * INNER])
    ssq = sb("ssq", [P, 2, 2 * HEADS])
    rnorm = sb("rnorm", [P, 2, 2 * HEADS])
    newton = sb("newton", [P, 2 * HEADS])
    three_halves = sb("three_halves", [P, 1])
    one = sb("one", [P, 1])
    q_t = sb("q_t", [P, PAIRS, P])
    k_t = sb("k_t", [P, 2, PAIRS, 2, KEYS])
    prob = sb("prob", [P, 2, HEADS, 2 * WINDOW])
    stat = sb("stat", [P, 2, 2, HEADS])
    prob_t = sb("prob_t", [P, PAIRS, P])
    mixed = sb("mixed", [P, 2, PAIRS, 2, P])
    ff_parts = sb("ff_parts", [P, 2, 2, BANK], F32R)
    ps = ctx.enter_context(nc.psum_tensor("ps", [P, 8, BANK], F32))
    A, T, S, G = 0, 2, 4, 6

    w_in = mixed[:, 0].rearrange("p a h n -> p (a h n)")
    w_v = mixed[:, 1, 0:4].rearrange("p a h n -> p (a h) n")
    w_o = mixed[:, 1, 4:8].rearrange("p a h n -> p (a h) n")

    done = {name: sem(name) for order in (PE_ORDER, ACT_ORDER, DVE_ORDER, POOL_ORDER, FF_PE_ORDER, FF_ACT_ORDER, FF_DVE_ORDER)
            for _, name in order}
    names = """wqk_loaded wvo_loaded wff_loaded scale_loaded const_loaded const_set vo_ready vo_copied rope_ready
        wqk_high wqk_low xs_low xs_high xs_whole xs_rounded xw_low xw_high rs_log newton_step
        fx_low fx_high w1_high w1_low""".split()
    z = {n: sem(n) for n in names}
    (wqk_loaded, wvo_loaded, wff_loaded, scale_loaded, const_loaded, const_set, vo_ready, vo_copied, rope_ready,
     wqk_high, wqk_low, xs_low, xs_high, xs_whole, xs_rounded, xw_low, xw_high, rs_log, newton_step,
     fx_low, fx_high, w1_high, w1_low) = [z[n] for n in names]

    def ff(odd):
        return (qk[:, odd, 0:BANK], qk[:, odd, BANK:2 * BANK], qk[:, odd, 2 * BANK:3 * BANK],
                [sq[0:m, odd, k * BANK:(k + 1) * BANK] for k, (_, m) in enumerate(HIDDEN_PARTS)])
    STATS, OUT, GATE, VALUE = 0, 1, (4, 5, 2), (3, 6, 7)

    def shift_in(eng, dst, src, first, tokens_before, tile, low, high, ready, n, start):
        width = dst.shape[1]
        eng.tensor_copy(dst[0:64, :], src[0:64, bass.ds(first, width)]).then_inc(low, 1)
        ins = eng.tensor_copy(dst[64:128, :], src[64:128, bass.ds(first - 1, width)])
        if not start:
            ins.then_inc(ready, 1)
            return
        ins.then_inc(high, 1)
        eng.wait_ge(high, n)
        col = dst[64:128, tokens_before:tokens_before + 1]
        eng.tensor_tensor(col, col, keep[64:128, bass.ds(tile % SEQ_TILES, 1)], ALU.mult).then_inc(ready, 1)

    def after(eng, base, *producers):
        for name, tile in producers:
            eng.wait_ge(done[name], base + tile + 1)

    def indexed(name, f, n):
        return {f"{name}{i}": f(i) for i in range(n)}

    with nc.Block() as block:
        @block.sync
        def _(sp):
            consts = [(rope, hbm["rope"]), (sight, hbm["sight"]), (keep, hbm["keep"])]
            for dst, src in consts:
                sp.dma_start(dst[:], src).then_inc(const_loaded, 16)
            for l in range(DEPTH):
                if l:
                    sp.wait_ge(rope_ready, 4 * l)
                sp.dma_start(head_scale[:, :, :], hbm["head_scale"][l].partition_broadcast(P)
                             ).then_inc(scale_loaded, 16)
                if l:
                    sp.wait_ge(done["output"], TILES * l)
                sp.dma_start(w_in, hbm["w_qk"][l]).then_inc(wqk_loaded, 16)
                sp.dma_start(w_v, hbm["w_v"][l]).then_inc(wvo_loaded, 16)
                sp.dma_start(w_o, hbm["w_o"][l]).then_inc(wvo_loaded, 16)
                if l:
                    sp.wait_ge(done["add_ff"], CHUNKS * l)
                sp.dma_start(w1[:, :], hbm["w1"][l]).then_inc(wff_loaded, 16)
                sp.dma_start(w2[:, :, :], hbm["w2"][l]).then_inc(wff_loaded, 16)
                sp.dma_start(lp[:, :], hbm["lp"][l]).then_inc(wff_loaded, 16)

        @block.tensor
        def _(pe):
            pe.wait_ge(const_set, 8)
            with pe.Fori(0, DEPTH) as l:
                base, ff_base = l * TILES, l * CHUNKS
                def fold_values():
                    pe.wait_ge(wvo_loaded, 32 * l + 32)
                    for h in range(HEADS):
                        rows = slice(64 * (h % 2), 64 * (h % 2) + 64)
                        last = pe.matmul(ps[:, S + 2 * (h % 2) + h // 8, (h // 2 % 4) * P:(h // 2 % 4 + 1) * P],
                                         w_v[rows, h // 2, :], w_o[rows, h // 2, :], start=True, stop=True)
                    last.then_inc(vo_ready, 1)

                def turn_bank_free(name, t):
                    user, tile = last_turn(name, t)
                    if user:
                        after(pe, base, (TURN_READERS[user], tile))
                    return T + TURN_BANK[name]

                def project(c):
                    def stage(t, odd):
                        after(pe, base, ("shift_tile", t))
                        if isinstance(t, int) and t == 0:
                            pe.wait_ge(wqk_low, l + 1)
                        if c < 2:
                            if later(t, 1):
                                after(pe, base, (f"keep{c + 2}", t - 1))
                        else:
                            after(pe, base, (f"keep{c - 2}", t))
                        for k, (xpart, wpart) in enumerate([(0, 0), (1, 0), (0, 1)]):
                            last = pe.matmul(ps[:, A + c % 2, :], xs_parts[:, odd, xpart, :],
                                             w_qk[:, wpart, c * BANK:(c + 1) * BANK], start=k == 0, stop=k == 2)
                        last.then_inc(done[f"project{c}"], 1)
                        if isinstance(t, int) and t == 0 and f"project{c}" == [n for _, n in PE_ORDER if "project" in n][-1]:
                            fold_values()
                    return stage

                def head_turn(c):
                    def stage(t, odd):
                        after(pe, base, (f"normed{c // 2}", t))
                        bank = turn_bank_free(f"head_turn{c}", t)
                        for j in range(4):
                            col = c * BANK + j * P
                            last = pe.transpose(ps[:, bank, j * P:(j + 1) * P], qk[:, odd, col:col + P], ident[:, :])
                        last.then_inc(done[f"head_turn{c}"], 1)
                    return stage

                def row_turn(t, odd):
                    after(pe, base, ("shift_windows", t))
                    bank = turn_bank_free("row_turn", t)
                    for w in range(WINDOWS):
                        last = pe.transpose(ps[:, bank, w * P:(w + 1) * P], xw[:, odd, w, :], ident[:, :])
                    last.then_inc(done["row_turn"], 1)

                def score(t, odd):
                    after(pe, base, ("copy_heads0", t), ("copy_heads1", t), ("copy_heads2", t), ("copy_heads3", t), ("halo", t))
                    if later(t, 1):
                        after(pe, base, ("mask_scores", t - 1))
                    elif t == 0:
                        pe.wait_ge(vo_copied, 4 * l + 4)
                    for a in range(PAIRS):
                        for w in range(WINDOWS):
                            last = pe.matmul(ps[w * WINDOW:(w + 1) * WINDOW, S + a // 4, (a % 4) * P:(a % 4 + 1) * P],
                                             q_t[:, a, w * WINDOW:(w + 1) * WINDOW],
                                             k_t[:, odd, a, :, w * WINDOW:(w + 2) * WINDOW], start=True, stop=True,
                                             skip_group_check=True)
                    last.then_inc(done["score"], 1)

                def prob_turn(c):
                    def stage(t, odd):
                        after(pe, base, ("normalise_probs", t))
                        bank = turn_bank_free(f"prob_turn{c}", t)
                        for j in range(4):
                            a = 4 * c + j
                            last = pe.transpose(ps[:, bank, j * P:(j + 1) * P],
                                                prob[:, odd, 2 * a:2 * a + 2, :].rearrange("p h k -> p (h k)"), ident[:, :])
                        last.then_inc(done[f"prob_turn{c}"], 1)
                    return stage

                def mix(r):
                    def stage(t, odd):
                        after(pe, base, ("copy_rows", t), ("copy_probs0", t), ("copy_probs1", t))
                        if r:
                            after(pe, base, ("copy_mixed0", t))
                        elif later(t, 1):
                            after(pe, base, ("copy_mixed1", t - 1))
                        for w in (2 * r, 2 * r + 1):
                            for h in range(2):
                                rows = slice(64 * h, 64 * h + 64)
                                last = pe.matmul(ps[:, G + h, (w % 2) * 256:(w % 2 + 1) * 256],
                                                 x_rows[rows, odd, w, :], prob_t[rows, :, w * WINDOW:(w + 1) * WINDOW],
                                                 start=True, stop=True, skip_group_check=True)
                        last.then_inc(done[f"mix{r}"], 1)
                    return stage

                def output(t, odd):
                    after(pe, base, ("copy_mixed0", t), ("copy_mixed1", t))
                    bank = turn_bank_free("output", t)
                    for a in range(PAIRS):
                        for h in range(2):
                            last = pe.matmul(ps[:, bank, 0:P], w_vo[:, 2 * a + h, :], mixed[:, odd, a, h, :],
                                             start=a + h == 0, stop=a == PAIRS - 1 and h == 1)
                    last.then_inc(done["output"], 1)

                tile_step = stepper(PE_ORDER, {**indexed("project", project, 4), **indexed("head_turn", head_turn, 4),
                                        "row_turn": row_turn, "score": score, **indexed("prob_turn", prob_turn, 2),
                                        **indexed("mix", mix, 2), "output": output}, TILES)

                def mean(c, odd):
                    after(pe, ff_base, ("shift_chunk", c))
                    if c == 0:
                        after(pe, base, ("keep0", TILES - 1), ("keep2", TILES - 1))
                    if later(c, 1):
                        after(pe, ff_base, ("log", c - 1))
                    pe.matmul(ps[:, STATS, :], ones_mean[:, :], ff(odd)[0], start=True, stop=True).then_inc(done["mean"], 1)

                def variance(c, odd):
                    after(pe, ff_base, ("square", c), ("centre", c))
                    pe.matmul(ps[:, STATS, :], ones_mean[:, :], ff(odd)[2], start=True, stop=True).then_inc(done["variance"], 1)

                def hidden(name, reader, bank, first):
                    def part(k):
                        lo, m = HIDDEN_PARTS[k]

                        def stage(c, odd):
                            if c == 0:
                                pe.wait_ge(w1_low, l + 1)
                                after(pe, base, ("mask_scores" if bank[k] == S else "add_output", TILES - 1))
                            after(pe, ff_base, ("rest", c))
                            if later(c, 1):
                                after(pe, ff_base, (f"{reader}{k}", c - 1))
                            for i, (wpart, xpart) in enumerate([(0, 0), (1, 0), (0, 1)]):
                                last = pe.matmul(ps[0:m, bank[k], :], w1_parts[:, wpart, first + lo:first + lo + m],
                                                 ff_parts[:, odd, xpart, :], start=i == 0, stop=i == 2)
                            last.then_inc(done[f"{name}{k}"], 1)
                        return stage
                    return part

                def ff_output(c, odd):
                    if c == 0:
                        pe.wait_ge(wff_loaded, 48 * l + 48)
                    after(pe, ff_base, *[(f"product{k}", c) for k in range(3)])
                    if later(c, 1):
                        after(pe, ff_base, ("add_ff", c - 1))
                    for k, (lo, m) in enumerate(HIDDEN_PARTS):
                        last = pe.matmul(ps[:, OUT, :], w2[0:m, k, :], ff(odd)[3][k], start=k == 0, stop=k == 2)
                    last.then_inc(done["ff_output"], 1)

                chunk_step = stepper(FF_PE_ORDER, {
                    "mean": mean, "variance": variance, **indexed("gate", hidden("gate", "gelu", GATE, HIDDEN), 3),
                    **indexed("value", hidden("value", "product", VALUE, 0), 3), "ff_output": ff_output}, CHUNKS)
                pipeline(pe, tile_step, chunk_step)
                pe.wait_ge(done["add_ff"], CHUNKS * l + CHUNKS)

        @block.scalar
        def _(act):
            act.wait_ge(const_set, 8)
            with act.Fori(0, DEPTH) as l:
                base, ff_base = l * TILES, l * CHUNKS
                act.preload_act_table_set("natural_log_exp_and_others")
                def copy_folded():
                    for k in range(4):
                        act.wait_ge(vo_ready, l + 1)
                        act.copy(w_vo[:, (k % 2) * 8 + k // 2:(k % 2) * 8 + k // 2 + 7:2, :],
                                 ps[:, S + k, :].rearrange("p (j n) -> p j n", j=4)).then_inc(vo_copied, 1)

                def keep_part(c):
                    def stage(t, odd):
                        after(act, base, (f"project{c}", t))
                        if later(t, 2):
                            after(act, base, (f"head_turn{c}", t - 2))
                        cols = slice(c * BANK, (c + 1) * BANK)
                        act.copy(qk[:, odd, cols], ps[:, A + c % 2, :])
                        act.activation(sq[:, odd, cols], ps[:, A + c % 2, :], ACT.Square).then_inc(done[f"keep{c}"], 1)
                        if isinstance(t, int) and t == 0 and f"keep{c}" == [n for _, n in ACT_ORDER if "keep" in n][-1]:
                            copy_folded()
                    return stage

                def inverse_norm(t, odd):
                    after(act, base, ("guard", t))
                    if later(t, 2):
                        after(act, base, ("normed0", t - 2), ("normed1", t - 2))
                    act.activation(rnorm[:, odd, :], ssq[:, odd, :], ACT.Ln, scale=float(2 ** (NORM_SHIFT + 1))).then_inc(rs_log, 1)
                    act.wait_ge(rs_log, base + t + 1)
                    act.activation(rnorm[:, odd, :], rnorm[:, odd, :], ACT.Exp, scale=-0.5,
                                   bias=exp_shift[:, 0:1]).then_inc(done["inverse_norm"], 1)

                def copy_heads(c):
                    def stage(t, odd):
                        name = f"copy_heads{c}"
                        after(act, base, (f"head_turn{c}", t))
                        bank = ps[:, T + TURN_BANK[f"head_turn{c}"], :].rearrange("p (j n) -> p j n", j=4)
                        if c < 2:
                            if later(t, 1):
                                after(act, base, ("score", t - 1))
                            act.copy(q_t[:, 4 * c:4 * c + 4, :], bank).then_inc(done[name], 1)
                            return
                        if later(t, 1):
                            after(act, base, ("halo", t - 1))
                        if later(t, 2):
                            after(act, base, ("score", t - 2))
                        pairs = slice(4 * (c - 2), 4 * (c - 2) + 4)
                        act.copy(k_t[0:64, odd, pairs, 0, WINDOW:], bank[0:64])
                        act.copy(k_t[64:128, odd, pairs, 1, WINDOW:], bank[64:128]).then_inc(done[name], 1)
                    return stage

                def copy_rows(t, odd):
                    after(act, base, ("row_turn", t))
                    if later(t, 2):
                        after(act, base, ("mix0", t - 2), ("mix1", t - 2))
                    act.copy(x_rows[:, odd, :, :], ps[:, T + TURN_BANK["row_turn"], :].rearrange("p (w n) -> p w n", w=4)
                             ).then_inc(done["copy_rows"], 1)

                def exponent(t, odd):
                    after(act, base, ("subtract_max", t))
                    act.activation(prob[:, odd, :, :], prob[:, odd, :, :], ACT.Exp, scale=QK_SCALE).then_inc(done["exponent"], 1)

                def copy_probs(c):
                    def stage(t, odd):
                        after(act, base, (f"prob_turn{c}", t))
                        if later(t, 1):
                            after(act, base, ("mix0", t - 1), ("mix1", t - 1))
                        act.copy(prob_t[:, 4 * c:4 * c + 4, :], ps[:, T + TURN_BANK[f"prob_turn{c}"], :].rearrange(
                            "p (j n) -> p j n", j=4)).then_inc(done[f"copy_probs{c}"], 1)
                    return stage

                def copy_mixed(r):
                    def stage(t, odd):
                        after(act, base, (f"mix{r}", t))
                        if later(t, 2):
                            after(act, base, ("output", t - 2))
                        elif t == 0:
                            act.wait_ge(wqk_low, l + 1)
                        for h in range(2):
                            dst = mixed[:, odd, :, h, :].rearrange("p a (w n) -> p w a n", w=4)[:, 2 * r:2 * r + 2]
                            last = act.copy(dst, ps[:, G + h, :].rearrange("p (w a n) -> p w a n", w=2, a=PAIRS))
                        last.then_inc(done[f"copy_mixed{r}"], 1)
                    return stage

                tile_step = stepper(ACT_ORDER, {**indexed("keep", keep_part, 4), **indexed("copy_heads", copy_heads, 4),
                                          "copy_rows": copy_rows, "inverse_norm": inverse_norm, "exponent": exponent,
                                          **indexed("copy_probs", copy_probs, 2), **indexed("copy_mixed", copy_mixed, 2)}, TILES)

                def square(c, odd):
                    xf, xc, work, hid = ff(odd)
                    after(act, ff_base, ("centre", c))
                    if later(c, 2):
                        after(act, ff_base, ("scale", c - 2))
                    act.activation(work, xc, ACT.Square).then_inc(done["square"], 1)

                def log(c, odd):
                    after(act, ff_base, ("variance", c))
                    act.activation(ff(odd)[2], ps[:, STATS, :], ACT.Ln, bias=eps_col[:, 0:1]).then_inc(done["log"], 1)

                def rstd(c, odd):
                    work = ff(odd)[2]
                    after(act, ff_base, ("log", c))
                    act.activation(work, work, ACT.Exp, scale=-0.5).then_inc(done["rstd"], 1)

                def gelu(k):
                    m = HIDDEN_PARTS[k][1]

                    def stage(c, odd):
                        if c == 0:
                            act.wait_ge(wff_loaded, 48 * l + 48)
                        after(act, ff_base, (f"gate{k}", c))
                        if later(c, 2):
                            after(act, ff_base, ("ff_output", c - 2))
                        act.activation(ff(odd)[3][k], ps[0:m, GATE[k], :], ACT.Gelu,
                                       bias=lp[0:m, GATE_B + k:GATE_B + k + 1]).then_inc(done[f"gelu{k}"], 1)
                    return stage

                chunk_step = stepper(FF_ACT_ORDER, {"square": square, "log": log, "rstd": rstd, **indexed("gelu", gelu, 3)}, CHUNKS)
                pipeline(act, tile_step, chunk_step)

        @block.vector
        def _(dve):
            dve.memset(exp_shift[:, :], float(np.log(2.0) * NORM_SHIFT / 2)).then_inc(const_set, 1)
            dve.memset(ones_mean[:, :], 1.0 / DIM).then_inc(const_set, 1)
            dve.memset(eps_col[:, :], EPS).then_inc(const_set, 1)
            dve.memset(one[:, :], 1.0).then_inc(const_set, 1)
            dve.memset(three_halves[:, :], 1.5).then_inc(const_set, 1)
            dve.memset(xb[:, 0:LEAD], 0.0).then_inc(const_set, 1)
            dve.wait_ge(const_loaded, 48)
            dve.wait_ge(const_set, 8)
            with dve.Fori(0, DEPTH) as l:
                base, ff_base = l * TILES, l * CHUNKS
                def views(part, odd):
                    cols = slice(part * INNER, (part + 1) * INNER)
                    return qk[:, odd, cols], sq[:, odd, cols]

                def table(part, i, t):
                    return rope_l[:, 2 * part + i, bass.ds(t % SEQ_TILES, 1), :].to_broadcast([P, HEADS, HEAD_DIM])

                def squares(part):
                    def stage(t, odd):
                        kept, squared_heads = views(part, odd)
                        after(dve, base, (f"keep{2 * part}", t), (f"keep{2 * part + 1}", t))
                        if later(t, 2):
                                after(dve, base, ("refine_norm", t - 2))
                        dve.tensor_reduce(ssq[:, odd, part * HEADS:(part + 1) * HEADS],
                                          squared_heads.rearrange("p (h d) -> p h d", d=HEAD_DIM),
                                          AX_X, ALU.add).then_inc(done[f"squares{part}"], 1)
                    return stage

                def guard(t, odd):
                    after(dve, base, ("squares0", t), ("squares1", t))
                    dve.tensor_scalar(ssq[:, odd, :], ssq[:, odd, :], 1e-24, 0.5, ALU.max, ALU.mult).then_inc(done["guard"], 1)

                def sines(part):
                    def stage(t, odd):
                        kept, turned = views(part, odd)
                        after(dve, base, (f"squares{part}", t))
                        if isinstance(t, int) and t == 0:
                            dve.wait_ge(rope_ready, 4 * l + 4)
                        swapped = kept.rearrange("p (h s d) -> p h s d", s=2, d=HEAD_DIM // 2)[:, :, ::-1, :]
                        dve.tensor_tensor(turned.rearrange("p (h s d) -> p h s d", s=2, d=HEAD_DIM // 2), swapped,
                                          table(part, 1, t).rearrange("p h (s d) -> p h s d", s=2),
                                          ALU.mult).then_inc(done[f"sines{part}"], 1)
                    return stage

                def cosines(part):
                    def stage(t, odd):
                        heads = views(part, odd)[0].rearrange("p (h d) -> p h d", d=HEAD_DIM)
                        after(dve, base, (f"sines{part}", t))
                        dve.tensor_tensor(heads, heads, table(part, 0, t), ALU.mult).then_inc(done[f"cosines{part}"], 1)
                    return stage

                def mask_scores(t, odd):
                    after(dve, base, ("score", t))
                    if later(t, 2):
                        after(dve, base, ("prob_turn0", t - 2), ("prob_turn1", t - 2))
                    dve.tensor_tensor(prob[:, odd], ps[:, S:S + 2, :].rearrange("p b (h k) -> p (b h) k", k=2 * WINDOW),
                                      sight[:, bass.ds(t % SEQ_TILES, 1), :].to_broadcast([P, HEADS, 2 * WINDOW]),
                                      ALU.add).then_inc(done["mask_scores"], 1)

                def find_max(t, odd):
                    after(dve, base, ("mask_scores", t))
                    dve.tensor_reduce(stat[:, odd, 0, :], prob[:, odd], AX_X, ALU.max).then_inc(done["find_max"], 1)

                def subtract_max(t, odd):
                    after(dve, base, ("find_max", t))
                    dve.tensor_tensor(prob[:, odd], prob[:, odd], stat[:, odd, 0, :].unsqueeze(2).to_broadcast(
                        [P, HEADS, 2 * WINDOW]), ALU.subtract).then_inc(done["subtract_max"], 1)

                def sum_probs(t, odd):
                    after(dve, base, ("exponent", t))
                    if later(t, 2):
                        after(dve, base, ("normalise_probs", t - 2))
                    dve.tensor_reduce(stat[:, odd, 1, :], prob[:, odd], AX_X, ALU.add).then_inc(done["sum_probs"], 1)

                def invert_sum(t, odd):
                    after(dve, base, ("sum_probs", t))
                    dve.reciprocal(stat[:, odd, 1, :], stat[:, odd, 1, :]).then_inc(done["invert_sum"], 1)

                def add_output(t, odd):
                    after(dve, base, ("output", t))
                    cols = bass.ds(LEAD + t * P, P)
                    dve.tensor_tensor(xb[:, cols], ps[:, T + TURN_BANK["output"], 0:P], xa[:, cols],
                                      ALU.add).then_inc(done["add_output"], 1)

                def shift_tile(t, odd):
                    if later(t, 2):
                        after(dve, base, *[(f"project{c}", t - 2) for c in range(4)])
                    shift_in(dve, xs[:, odd, :], xa, LEAD + t * P, 0, t, xs_low, xs_high, xs_whole, base + t + 1, True)
                    dve.wait_ge(xs_low, base + t + 1)
                    dve.wait_ge(xs_whole, base + t + 1)
                    dve.tensor_copy(xs_parts[:, odd, 0, :], xs[:, odd, :]).then_inc(xs_rounded, 1)
                    dve.wait_ge(xs_rounded, base + t + 1)
                    dve.tensor_tensor(xs_parts[:, odd, 1, :], xs[:, odd, :], xs_parts[:, odd, 0, :].bitcast(F32),
                                      ALU.subtract).then_inc(done["shift_tile"], 1)

                def shift_windows(t, odd):
                    if later(t, 2):
                        after(dve, base, ("row_turn", t - 2))

                    def seen(rows, before):
                        first = xa[rows, bass.ds(LEAD + t * P - WINDOW - before, KEYS)]
                        return bass.AP(first.tensor, first.offset, [first.ap[0], (WINDOW, WINDOWS), (0, 2), (1, 2 * WINDOW)])
                    low, high = (xw[r, odd].rearrange("p w (c k) -> p w c k", c=2) for r in (slice(0, 64), slice(64, 128)))
                    dve.tensor_copy(low, seen(slice(0, 64), 0)).then_inc(xw_low, 1)
                    dve.tensor_copy(high, seen(slice(64, 128), 1)).then_inc(xw_high, 1)
                    dve.wait_ge(xw_high, base + t + 1)
                    for w, key in ((0, WINDOW), (1, 0)):
                        col = high[:, w, :, key]
                        last = dve.tensor_tensor(col, col, keep[64:128, bass.ds(t % SEQ_TILES, 1)].to_broadcast([64, 2]), ALU.mult)
                    last.then_inc(done["shift_windows"], 1)

                tile_step = stepper(DVE_ORDER, {
                    "shift_tile": shift_tile, "shift_windows": shift_windows, **indexed("squares", squares, 2), "guard": guard,
                    **indexed("sines", sines, 2), **indexed("cosines", cosines, 2), "mask_scores": mask_scores,
                    "find_max": find_max, "subtract_max": subtract_max, "sum_probs": sum_probs, "invert_sum": invert_sum,
                    "add_output": add_output}, TILES)

                def shift_chunk(c, odd):
                    if c == 0:
                        after(dve, base, *[(f"head_turn{k}", TILES - 1) for k in range(4)])
                    after(dve, base, ("add_output", TILES // CHUNKS * (c + 1) - 1))
                    if later(c, 2):
                        after(dve, ff_base, ("centre", c - 2))
                    start = c % SEQ_CHUNKS == 0
                    n = SEQ_TILES // SEQ_CHUNKS
                    shift_in(dve, ff(odd)[0], xb, LEAD + c * BANK, 0, n * c, fx_low, fx_high, done["shift_chunk"],
                             CHUNKS // SEQ_CHUNKS * l + c // SEQ_CHUNKS + 1, start)

                def centre(c, odd):
                    xf, xc, work, hid = ff(odd)
                    after(dve, ff_base, ("mean", c))
                    dve.tensor_tensor(xc, xf, ps[:, STATS, :], ALU.subtract).then_inc(done["centre"], 1)

                def scale(c, odd):
                    xf, xc, work, hid = ff(odd)
                    after(dve, ff_base, ("rstd", c))
                    dve.tensor_tensor(xc, xc, work, ALU.mult).then_inc(done["scale"], 1)

                def affine(c, odd):
                    xc = ff(odd)[1]
                    if c == 0:
                        dve.wait_ge(wff_loaded, 48 * l + 48)
                    after(dve, ff_base, ("scale", c))
                    dve.tensor_scalar(xc, xc, lp[:, LN_G:LN_G + 1], lp[:, LN_B:LN_B + 1], ALU.mult,
                                      ALU.add).then_inc(done["affine"], 1)

                def round_high(c, odd):
                    after(dve, ff_base, ("affine", c))
                    if later(c, 2):
                        after(dve, ff_base, *[(f"{name}{k}", c - 2) for name in ("gate", "value") for k in range(3)])
                    dve.tensor_copy(ff_parts[:, odd, 0, :], ff(odd)[1]).then_inc(done["round"], 1)

                def rest(c, odd):
                    after(dve, ff_base, ("round", c))
                    dve.tensor_tensor(ff_parts[:, odd, 1, :], ff(odd)[1], ff_parts[:, odd, 0, :].bitcast(F32),
                                      ALU.subtract).then_inc(done["rest"], 1)

                def product(k):
                    m = HIDDEN_PARTS[k][1]

                    def stage(c, odd):
                        hid = ff(odd)[3][k]
                        after(dve, ff_base, (f"value{k}", c), (f"gelu{k}", c))
                        dve.scalar_tensor_tensor(out=hid, in0=ps[0:m, VALUE[k], :], scalar=lp[0:m, A_B + k:A_B + k + 1],
                                                 in1=hid, op0=ALU.add, op1=ALU.mult).then_inc(done[f"product{k}"], 1)
                    return stage

                def add_ff(c, odd):
                    after(dve, ff_base, ("ff_output", c))
                    cols = bass.ds(LEAD + c * BANK, BANK)
                    dve.scalar_tensor_tensor(out=xa[:, cols], in0=ps[:, OUT, :], scalar=lp[:, OUT_B:OUT_B + 1],
                                             in1=xb[:, cols], op0=ALU.add, op1=ALU.add).then_inc(done["add_ff"], 1)

                chunk_step = stepper(FF_DVE_ORDER, {
                    "shift_chunk": shift_chunk, "centre": centre, "scale": scale, "affine": affine,
                    "round": round_high, "rest": rest,
                    **indexed("product", product, 3), "add_ff": add_ff}, CHUNKS)
                pipeline(dve, tile_step, chunk_step)
                dve.wait_ge(done["add_ff"], CHUNKS * l + CHUNKS)

        @block.gpsimd
        def _(pool):
            pool.memset(k_t[:, 0], 0.0).then_inc(const_set, 1)
            pool.memset(k_t[:, 1], 0.0).then_inc(const_set, 1)
            pool.wait_ge(const_loaded, 48)
            pool.wait_ge(const_set, 8)

            with pool.Fori(0, DEPTH) as l:
                base, ff_base = l * TILES, l * CHUNKS
                pool.wait_ge(scale_loaded, 16 * l + 16)
                for part in range(2):
                    scale = head_scale[:, part, :]
                    partner = scale.rearrange("p (s d) -> p s d", s=2)[:, ::-1, :]
                    pool.tensor_tensor(rope_l[:, 2 * part], rope[:, 2 * part],
                                       scale.unsqueeze(1).to_broadcast([P, SEQ_TILES, HEAD_DIM]), ALU.mult).then_inc(rope_ready, 1)
                    pool.tensor_tensor(rope_l[:, 2 * part + 1].rearrange("p t (s d) -> p t s d", s=2),
                                       rope[:, 2 * part + 1].rearrange("p t (s d) -> p t s d", s=2),
                                       partner.unsqueeze(1).to_broadcast([P, SEQ_TILES, 2, HEAD_DIM // 2]),
                                       ALU.mult).then_inc(rope_ready, 1)

                pool.wait_ge(wqk_loaded, 16 * l + 16)
                pool.tensor_tensor(w_qk[:, 0, :], w_in, one[:, 0:1].to_broadcast([P, 2 * INNER]), ALU.mult).then_inc(wqk_high, 1)
                pool.wait_ge(wqk_high, l + 1)
                pool.tensor_tensor(w_qk[:, 1, :], w_in, w_qk[:, 0, :].bitcast(F32), ALU.subtract).then_inc(wqk_low, 1)

                def halo(t, odd):
                    if later(t, 1):
                        after(pool, base, ("copy_heads2", t - 1), ("copy_heads3", t - 1))
                    if later(t, 2):
                        after(pool, base, ("score", t - 2))
                    first = keep[:, bass.ds(t % SEQ_TILES, 1)].unsqueeze(2).to_broadcast([P, 2 * PAIRS, WINDOW])
                    pool.tensor_tensor(k_t[:, odd, :, :, 0:WINDOW].rearrange("p a h k -> p (a h) k"),
                                       k_t[:, 1 - odd, :, :, P:P + WINDOW].rearrange("p a h k -> p (a h) k"), first,
                                       ALU.mult).then_inc(done["halo"], 1)

                def refine_norm(t, odd):
                    after(pool, base, ("inverse_norm", t))
                    r, steps = rnorm[:, odd, :], 3 * (base + t)
                    pool.tensor_tensor(newton[:, :], ssq[:, odd, :], r, ALU.mult).then_inc(newton_step, 1)
                    pool.wait_ge(newton_step, steps + 1)
                    pool.tensor_tensor(newton[:, :], newton[:, :], r, ALU.mult).then_inc(newton_step, 1)
                    pool.wait_ge(newton_step, steps + 2)
                    pool.tensor_tensor(newton[:, :], three_halves[:, 0:1].to_broadcast([P, 2 * HEADS]), newton[:, :],
                                       ALU.subtract).then_inc(newton_step, 1)
                    pool.wait_ge(newton_step, steps + 3)
                    pool.tensor_tensor(r, r, newton[:, :], ALU.mult).then_inc(done["refine_norm"], 1)

                def rotated(part):
                    def stage(t, odd):
                        cols = slice(part * INNER, (part + 1) * INNER)
                        after(pool, base, (f"cosines{part}", t))
                        pool.tensor_tensor(qk[:, odd, cols], qk[:, odd, cols], sq[:, odd, cols],
                                           ALU.add).then_inc(done[f"rotated{part}"], 1)
                    return stage

                def normed(part):
                    def stage(t, odd):
                        heads = qk[:, odd, part * INNER:(part + 1) * INNER].rearrange("p (h d) -> p h d", d=HEAD_DIM)
                        after(pool, base, (f"rotated{part}", t), ("refine_norm", t))
                        norms = rnorm[:, odd, part * HEADS:(part + 1) * HEADS].unsqueeze(2).to_broadcast([P, HEADS, HEAD_DIM])
                        pool.tensor_tensor(heads, heads, norms, ALU.mult).then_inc(done[f"normed{part}"], 1)
                    return stage

                def normalise_probs(t, odd):
                    after(pool, base, ("invert_sum", t))
                    inverse = stat[:, odd, 1, :].unsqueeze(2).to_broadcast([P, HEADS, 2 * WINDOW])
                    pool.tensor_tensor(prob[:, odd], prob[:, odd], inverse, ALU.mult).then_inc(done["normalise_probs"], 1)

                tile_step = stepper(POOL_ORDER, {**indexed("rotated", rotated, 2), **indexed("normed", normed, 2),
                                            "refine_norm": refine_norm, "halo": halo, "normalise_probs": normalise_probs}, TILES)
                pipeline(pool, tile_step, None)
                pool.wait_ge(wff_loaded, 48 * l + 48)
                pool.tensor_tensor(w1_parts[:, 0, :], w1[:, :], one[:, 0:1].to_broadcast([P, 2 * HIDDEN]), ALU.mult).then_inc(w1_high, 1)
                pool.wait_ge(w1_high, l + 1)
                pool.tensor_tensor(w1_parts[:, 1, :], w1[:, :], w1_parts[:, 0, :].bitcast(F32), ALU.subtract).then_inc(w1_low, 1)



def program(nc, hbm, out):
    with ExitStack() as ctx:
        def sb(name, shape, dt=F32):
            return ctx.enter_context(nc.sbuf_tensor(name, shape, dt))

        def sem(name):
            return ctx.enter_context(nc.semaphore(name))

        resid = sb("resid", [P, TOKENS])
        ident = sb("ident", [P, P])
        ones_mean = sb("ones_mean", [P, P])
        eps_col = sb("eps_col", [P, 1])
        norm_sems = [sem(n) for n in ("mean_ready", "centred", "squared", "var_ready", "norm_log_done", "rstd_ready", "norm_done")]
        x_loaded = sem("x_loaded"); loaded = sem("loaded"); consts = sem("consts"); resid_started = sem("resid_started")
        sum_ready = sem("final_sum_ready"); stored = sem("stored")

        with ExitStack() as front:
            def fsb(name, shape, dt=F32):
                return front.enter_context(nc.sbuf_tensor(name, shape, dt))
            xn = fsb("xn", [P, TOKENS])
            win = fsb("win", [P, 2, 2 * D_INNER]); wx = fsb("wx", [P, 2, HALVES, BC_ROWS + DT_RANK])
            wdt = fsb("wdt", [BC_ROWS + DT_RANK, 2, D_INNER]); wout = fsb("wout", [P, 2, HALVES, DIM])
            packed = fsb("packed", [P, 2, PACKED]); ln = fsb("ln", [P, 2])
            sel = fsb("sel", [BC_ROWS, 2 * D_STATE, P], BF16)
            loads = [(win, "win"), (wx, "wx"), (wdt[BC_ROWS:], "wdt"), (wout, "wout"), (packed, "packed"),
                     (ident, "ident"), (sel, "sel")]
            with nc.Block() as block:
                @block.sync
                def _(sp):
                    for q in range(4):
                        part = slice(q * TOKENS // 4, (q + 1) * TOKENS // 4)
                        sp.dma_start(xn[:, part], hbm["x"][:, part]).then_inc(x_loaded, 16)
                    sp.dma_start(ln[:], hbm["ln"]).then_inc(x_loaded, 16)
                    for dst, name in loads:
                        sp.dma_start(dst[:], hbm[name]).then_inc(loaded, 16)
                    sp.wait_ge(x_loaded, 16 * 5)

                @block.vector
                def _(dve):
                    dve.memset(ones_mean[:, :], 1.0 / DIM).then_inc(consts, 1)
                    dve.memset(eps_col[:, :], EPS).then_inc(consts, 1)
                    dve.wait_ge(consts, 2)
            with ExitStack() as norms:
                u = norms.enter_context(nc.sbuf_tensor("u", [P, TOKENS], F32))
                work = norms.enter_context(nc.sbuf_tensor("work", [P, TOKENS], F32))

                def add_input(dve, cols, steps):
                    steps.wait(dve)
                    dve.tensor_tensor(resid[:, cols], xn[:, cols], u[:, cols], ALU.add).then_inc(resid_started, 1)

                def affine(dve, cols, steps):
                    steps.wait(dve)
                    dve.tensor_scalar(xn[:, cols], xn[:, cols], ln[:, 0:1], ln[:, 1:2], ALU.mult, ALU.add).then_inc(resid_started, 1)

                with ExitStack() as a:
                    layer_norm_block(nc, a, norm_sems, 0, ones_mean, eps_col, xn[:, :], u, work, add_input)
                with ExitStack() as a:
                    layer_norm_block(nc, a, norm_sems, 1, ones_mean, eps_col, u, xn[:, :], work, affine)
            with nc.Block() as block:
                @block.sync
                def _(sp):
                    sp.wait_ge(loaded, 16 * len(loads))
            mamba(nc, xn, resid, (win, wx, wdt, wout, packed, ident, sel[:, 0:D_STATE, :], sel[:, D_STATE:, :]))
        with ExitStack() as back:
            xa = back.enter_context(nc.sbuf_tensor("xa", [P, LEAD + TOKENS], F32))
            xb = back.enter_context(nc.sbuf_tensor("xb", [P, LEAD + TOKENS], F32))

            def clear_lead(dve, cols, steps):
                if cols.start == 0:
                    dve.memset(xa[:, 0:LEAD], 0.0).then_inc(resid_started, 1)

            with ExitStack() as a:
                layer_norm_block(nc, a, norm_sems, 2, ones_mean, eps_col, resid, xa[:, LEAD:], xb[:, LEAD:], clear_lead)
            with ExitStack() as a:
                transformer(nc, a, ident, xa, xb, hbm)
            with nc.Block() as block:
                @block.vector
                def _(dve):
                    for c in range(CHUNKS):
                        cols = slice(c * BANK, (c + 1) * BANK)
                        dve.tensor_tensor(resid[:, cols], resid[:, cols], xa[:, LEAD + c * BANK:LEAD + (c + 1) * BANK],
                                          ALU.add).then_inc(sum_ready, 1)

                @block.sync
                def _(sp):
                    for c in range(CHUNKS):
                        sp.wait_ge(sum_ready, c + 1)
                        sp.dma_start(out[:, c * BANK:(c + 1) * BANK], resid[:, c * BANK:(c + 1) * BANK]).then_inc(stored, 16)
                    sp.wait_ge(stored, 16 * CHUNKS)


def rope_tables():
    half = np.arange(0, HEAD_DIM, 2, dtype=np.float64)
    angle = np.arange(SEQ)[:, None] * (10000.0 ** (-half / HEAD_DIM))[None]
    power = (np.arange(SEQ) - SEQ // 2) / (WINDOW // 2)
    scale = ((half + 0.4 * HEAD_DIM) / (1.4 * HEAD_DIM))[None] ** power[:, None]
    cos, sin = np.cos(angle), np.sin(angle)
    tables = [np.concatenate(v, axis=1) for v in ((cos * scale,) * 2, (-sin * scale, sin * scale),
                                                  (cos / scale,) * 2, (-sin / scale, sin / scale))]
    t = np.stack(tables).astype(np.float32).reshape(4, SEQ_TILES, P, HEAD_DIM)
    return np.ascontiguousarray(t.transpose(2, 0, 1, 3))


def sight_table():
    i, j = np.arange(P)[:, None] % WINDOW, np.arange(2 * WINDOW)[None]
    seen = np.where(j < WINDOW, j >= i, j - WINDOW <= i)
    table = np.repeat(np.where(seen, 0.0, HIDDEN_ROW)[:, None, :], SEQ_TILES, axis=1)
    table[:WINDOW, 0, :WINDOW] = HIDDEN_ROW
    return table.astype(np.float32)


def host_layout(inputs):
    a = {k: np.asarray(v) for k, v in inputs.items()}
    both = lambda name, f: np.stack([f(a[f"L0_attn_{d}_{name}"]) for d in "fb"], axis=1)
    halves = lambda v: np.moveaxis(v.reshape(HALVES, P, *v.shape[1:]), 0, 1).reshape(P, -1)
    wx = [a[f"L0_attn_{d}_W_x"].T.reshape(HALVES, P, -1).transpose(1, 0, 2) for d in "fb"]
    bcs = [np.concatenate([w[:, :, DT_RANK:]] * 3 + [w[:, :, :DT_RANK]], axis=2) for w in wx]
    packed = [np.concatenate([halves(a[f"L0_attn_{d}_{n}"]) for n in ("W_conv", "b_conv", "b_dt", "A_log", "D")], axis=1)
              for d in "fb"]
    row, state = np.arange(96)[:, None] % 32, np.arange(32)[None]
    wqkv = a["L0_ffn_Wqkv"]
    w2 = np.zeros((DEPTH, P, 3, DIM), np.float32)
    lp = np.zeros((DEPTH, P, LAYER_PACKED), np.float32)
    lp[:, :, LN_G], lp[:, :, LN_B], lp[:, :, OUT_B] = a["L0_ffn_ln_g"], a["L0_ffn_ln_b"], a["L0_ffn_b2"]
    for k, (lo, m) in enumerate(HIDDEN_PARTS):
        w2[:, :m, k] = a["L0_ffn_W2"][:, lo:lo + m]
        lp[:, :m, A_B + k] = a["L0_ffn_b1"][:, lo:lo + m]
        lp[:, :m, GATE_B + k] = a["L0_ffn_b1"][:, HIDDEN + lo:HIDDEN + lo + m]
    return {
        "x": np.ascontiguousarray(a["L0_attn_x"].reshape(TOKENS, DIM).T),
        "win": np.ascontiguousarray(both("W_in", lambda w: w.T)),
        "wx": np.ascontiguousarray(np.stack(bcs, axis=1)),
        "wdt": np.ascontiguousarray(both("W_dt", lambda w: w.T)),
        "wout": np.ascontiguousarray(both("W_out", lambda w: w.T.reshape(HALVES, P, DIM).transpose(1, 0, 2))),
        "packed": np.ascontiguousarray(np.stack(packed, axis=1)),
        "ln": np.ascontiguousarray(np.stack([a["L0_attn_ln_w"], a["L0_attn_ln_b"]], axis=1)),
        "ident": np.eye(P, dtype=np.float32),
        "sel": np.ascontiguousarray(np.broadcast_to((row == state)[:, :, None], (96, 32, P))).astype(mybir.dt.np(BF16)),
        "rope": rope_tables(),
        "sight": sight_table(),
        "keep": np.ascontiguousarray(np.broadcast_to((np.arange(SEQ_TILES) > 0).astype(np.float32), (P, SEQ_TILES))),
        "w_qk": np.ascontiguousarray(wqkv[:, :, :2 * INNER]),
        "w_v": np.ascontiguousarray(wqkv[:, :, 2 * INNER:].transpose(0, 2, 1).reshape(DEPTH, PAIRS, P, DIM).transpose(0, 2, 1, 3)),
        "w_o": np.ascontiguousarray(a["L0_ffn_Wo"].reshape(DEPTH, PAIRS, P, DIM).transpose(0, 2, 1, 3)),
        "w1": a["L0_ffn_W1"],
        "w2": w2,
        "lp": lp,
        "head_scale": np.stack([a["L0_ffn_q_scale"], a["L0_ffn_k_scale"]], axis=1),
    }


def kernel(**inputs):
    import concourse.bacc as bacc
    from concourse.bass_utils import run_bass_kernel_spmd

    nc = bacc.Bacc("TRN2", target_bir_lowering=False, num_devices=1)
    arrays = {f"{name}_hbm": array for name, array in host_layout(inputs).items()}
    hbm = {name[:-4]: nc.dram_tensor(name, array.shape, mybir.dt.from_np(array.dtype), kind="ExternalInput").ap()
           for name, array in arrays.items()}
    out = nc.dram_tensor("out_hbm", (P, TOKENS), F32, kind="ExternalOutput").ap()
    program(nc, hbm, out)
    result = run_bass_kernel_spmd(nc, [arrays], core_ids=[0]).results[0]["out_hbm"]
    return np.ascontiguousarray(np.asarray(result).T).reshape(BATCH, SEQ, DIM)
```
